# Optimizing a Trainium2 kernel written in Bass

```python
import numpy as np
import jax
import jax.numpy as jnp

def _softmax(x, axis=-1):
    return jax.nn.softmax(x, axis=axis)

def _gelu(x):
    return jax.nn.gelu(x, approximate=True)

def _silu(x):
    return jax.nn.silu(x)

def _sigmoid(x):
    return jax.nn.sigmoid(x)

def _layernorm(x, axis=-1, eps=1e-05):
    m = jnp.mean(x, axis=axis, keepdims=True)
    v = jnp.var(x, axis=axis, keepdims=True)
    return (x - m) / jnp.sqrt(v + eps)

def _scatter_add(tgt, idx, src, axis=0):
    return tgt.at[idx].add(src)

def _segment_sum(src, seg, n):
    return jax.ops.segment_sum(src, seg, n)
kernel_name = 'mk_perceiver_d2_seqx_r2_80a6e5'

def setup_inputs(seed: int=0):
    np.random.seed(seed)
    _w = jnp.asarray

    def _rec_inputs():
        import jax
        import jax.numpy as jnp
        _rk = jax.random.key(seed)
        x = -0.0002928 + 1 * jax.random.normal(jax.random.fold_in(_rk, 1), (8, 64, 512), jnp.float32)
        _lenS = 64 - jax.random.randint(jax.random.fold_in(_rk, 7), (8,), 0, max(1, 64 // 4) + 1, jnp.int32)
        _lenS2 = 1601 - jax.random.randint(jax.random.fold_in(_rk, 8), (8,), 0, max(1, 1601 // 4) + 1, jnp.int32)
        _ctx_1024P = jax.random.normal(jax.random.fold_in(_rk, 11), (8, 16, 512), jnp.float32)
        _ctx_1024c = jax.random.dirichlet(jax.random.fold_in(_rk, 511), 0.3 * jnp.ones((16,), jnp.float32), (8, 1601))
        _ctx_1024t = jnp.einsum('bsk,bkd->bsd', _ctx_1024c, _ctx_1024P)
        _ctx_1024t = _ctx_1024t * jax.lax.rsqrt(jnp.mean(jnp.square(_ctx_1024t)) + 1e-12) * 0.953939
        ctx_1024 = -1.39393e-06 + 0.999914 * (_ctx_1024t + 0.3 * jax.random.normal(jax.random.fold_in(_rk, 611), (8, 1601, 512), jnp.float32))
        return (x, ctx_1024)
    x, ctx_1024 = _rec_inputs()

    def _L0_xattn_setup():
        import jax, jax.numpy as jnp
        import numpy as np
        DIM = 512
        NUM_HEADS = 16
        HEAD_DIM = DIM // NUM_HEADS
        key = jax.random.key(seed)
        ks = jax.random.split(key, 11)
        B, N, C = (2, 1024, DIM)
        s = 1.0 / np.sqrt(C)
        inp = {'q': jax.random.normal(ks[0], (B, N, C), jnp.float32), 'k': jax.random.normal(ks[1], (B, N, C), jnp.float32), 'v': jax.random.normal(ks[2], (B, N, C), jnp.float32), 'Wq': jax.random.normal(ks[3], (C, C), jnp.float32) * s, 'bq': jnp.zeros((C,), jnp.float32), 'Wk': jax.random.normal(ks[4], (C, C), jnp.float32) * s, 'bk': jnp.zeros((C,), jnp.float32), 'Wv': jax.random.normal(ks[5], (C, C), jnp.float32) * s, 'bv': jnp.zeros((C,), jnp.float32), 'Wo': jax.random.normal(ks[6], (C, C), jnp.float32) * s, 'bo': jnp.zeros((C,), jnp.float32)}
        return inp
    _L0_xattn_all = _L0_xattn_setup()
    _L0_xattn_in = {k: v for k, v in _L0_xattn_all.items() if k in ('Wq', 'bq', 'Wk', 'bk', 'Wv', 'bv', 'Wo', 'bo')}
    del _L0_xattn_all

    def _L0_attn_setup():
        import jax, jax.numpy as jnp
        import numpy as np
        EPS = 1e-12
        key = jax.random.key(seed)
        k1, k2 = jax.random.split(key)
        b, n, d = (4, 2048, 512)
        x = jax.random.normal(k1, (b, n, d), dtype=jnp.float32)
        W_qkva = jax.random.normal(k2, (3 * d, d), dtype=jnp.float32) * 0.02
        gamma = jnp.ones((d,), dtype=jnp.float32)
        return {'x': x, 'W_qkva': W_qkva, 'gamma': gamma}
    _L0_attn_all = _L0_attn_setup()
    _L0_attn_in = {k: v for k, v in _L0_attn_all.items() if k in ('W_qkva', 'gamma')}
    del _L0_attn_all

    def _L0_ffn_setup():
        import jax, jax.numpy as jnp
        import numpy as np
        B, S, H, E = (4, 1024, 512, 8)
        key = jax.random.key(seed)
        k1, k2, k3 = jax.random.split(key, 3)
        scale_w = 1.0 / np.sqrt(H)
        return {'x': jax.random.normal(k1, (B, S, H), dtype=jnp.float32), 'router_w': jax.random.normal(k2, (H, E), dtype=jnp.float32) * scale_w, 'router_b': jnp.zeros((E,), dtype=jnp.float32), 'expert_w': jax.random.normal(k3, (E, H, H), dtype=jnp.float32) * scale_w, 'expert_b': jnp.zeros((E, H), dtype=jnp.float32)}
    _L0_ffn_all = _L0_ffn_setup()
    _L0_ffn_in = {k: v for k, v in _L0_ffn_all.items() if k in ('router_w', 'router_b', 'expert_w', 'expert_b')}
    del _L0_ffn_all

    def _L1_xattn_setup():
        import jax, jax.numpy as jnp
        import numpy as np
        D_MODEL = 512
        B, S = (4, 1024)
        key = jax.random.key(seed)
        ks = jax.random.split(key, 10)
        s = 1.0 / np.sqrt(D_MODEL)
        return {'k': jax.random.normal(ks[0], (B, S, D_MODEL), jnp.float32), 'v': jax.random.normal(ks[1], (B, S, D_MODEL), jnp.float32), 'q': jax.random.normal(ks[2], (B, S, D_MODEL), jnp.float32), 'Wk': jax.random.normal(ks[3], (D_MODEL, D_MODEL), jnp.float32) * s, 'Wv': jax.random.normal(ks[4], (D_MODEL, D_MODEL), jnp.float32) * s, 'bv': jnp.zeros((D_MODEL,), jnp.float32), 'Wq': jax.random.normal(ks[5], (D_MODEL, D_MODEL), jnp.float32) * s, 'bq': jnp.zeros((D_MODEL,), jnp.float32), 'Wo': jax.random.normal(ks[6], (D_MODEL, D_MODEL), jnp.float32) * s, 'bo': jnp.zeros((D_MODEL,), jnp.float32)}
    _L1_xattn_all = _L1_xattn_setup()
    _L1_xattn_in = {k: v for k, v in _L1_xattn_all.items() if k in ('Wk', 'Wv', 'bv', 'Wq', 'bq', 'Wo', 'bo')}
    del _L1_xattn_all

    def _L1_attn_setup():
        import jax, jax.numpy as jnp
        import numpy as np
        DIM = 512
        HEADS = 16
        DIM_HEAD = DIM // HEADS
        LATENT = DIM // 4
        SCALE = DIM_HEAD ** (-0.5)
        key = jax.random.key(seed)
        ks = jax.random.split(key, 8)
        B, S = (2, 1024)
        init = lambda k, shape, fan_in: jax.random.normal(k, shape, jnp.float32) * fan_in ** (-0.5)
        return {'x': jax.random.normal(ks[0], (B, S, DIM), jnp.float32), 'Wq': init(ks[1], (DIM, DIM), DIM), 'bq': jnp.zeros((DIM,), jnp.float32), 'Wl': init(ks[2], (DIM, LATENT), DIM), 'bl': jnp.zeros((LATENT,), jnp.float32), 'Wk': init(ks[3], (LATENT, DIM), LATENT), 'bk': jnp.zeros((DIM,), jnp.float32), 'Wv': init(ks[4], (LATENT, DIM), LATENT), 'bv': jnp.zeros((DIM,), jnp.float32), 'Wo': init(ks[5], (DIM, DIM), DIM), 'bo': jnp.zeros((DIM,), jnp.float32)}
    _L1_attn_all = _L1_attn_setup()
    _L1_attn_in = {k: v for k, v in _L1_attn_all.items() if k in ('Wq', 'bq', 'Wl', 'bl', 'Wk', 'bk', 'Wv', 'bv', 'Wo', 'bo')}
    del _L1_attn_all

    def _L1_ffn_setup():
        import jax, jax.numpy as jnp
        import numpy as np
        D = 512
        H = 4
        HD = D // H
        E = 8
        FF = 2048
        CAP_FACTOR = 1.0

        def _ln(x, g, b, eps=1e-05):
            mu = jnp.mean(x, -1, keepdims=True)
            v = jnp.mean((x - mu) ** 2, -1, keepdims=True)
            return (x - mu) * jax.lax.rsqrt(v + eps) * g + b

        def _mha(x, w, b, ow, ob):
            L, N, _ = x.shape
            qkv = x @ w.T + b
            q, k, v = jnp.split(qkv, 3, axis=-1)
            rh = lambda t: t.reshape(L, N, H, HD).transpose(1, 2, 0, 3)
            q, k, v = (rh(q), rh(k), rh(v))
            scores = jnp.einsum('nhld,nhmd->nhlm', q, k) / np.float32(np.sqrt(HD))
            attn = jax.nn.softmax(scores, axis=-1)
            o = jnp.einsum('nhlm,nhmd->nhld', attn, v).transpose(2, 0, 1, 3).reshape(L, N, D)
            return o @ ow.T + ob

        def _moe(x, wg, w1, b1, w2, b2):
            L, N, _ = x.shape
            S = L * N
            cap = int(CAP_FACTOR * S) // E
            xf = x.reshape(S, D)
            gates = jax.nn.softmax(xf @ wg, axis=-1)
            idx = jnp.argmax(gates, axis=-1)
            mask1 = jax.nn.one_hot(idx, E, dtype=x.dtype)
            loc = jnp.sum((jnp.cumsum(mask1, 0) - 1.0) * mask1, -1).astype(jnp.int32)
            keep = loc < cap
            gate_val = jnp.take_along_axis(gates, idx[:, None], -1)[:, 0]
            slot = jnp.where(keep, idx.astype(jnp.int32) * cap + loc, E * cap)
            disp = jnp.zeros((E * cap, D), x.dtype).at[slot].set(xf, mode='drop')
            disp = disp.reshape(E, cap, D)
            h = jnp.einsum('ecd,edf->ecf', disp, w1) + b1[:, None, :]
            y = (jnp.einsum('ecf,efd->ecd', h, w2) + b2[:, None, :]).reshape(E * cap, D)
            out = jnp.where(keep[:, None], gate_val[:, None] * y[jnp.minimum(slot, E * cap - 1)], 0.0)
            return out.reshape(L, N, D)
        key = jax.random.key(seed)
        ks = jax.random.split(key, 8)
        L, N = (512, 16)
        s = 0.02
        return {'x': jax.random.normal(ks[0], (L, N, D), jnp.float32), 'in_proj_w': jax.random.normal(ks[1], (3 * D, D), jnp.float32) * s, 'in_proj_b': jnp.zeros((3 * D,), jnp.float32), 'out_proj_w': jax.random.normal(ks[2], (D, D), jnp.float32) * s, 'out_proj_b': jnp.zeros((D,), jnp.float32), 'ln1_g': jnp.ones((D,), jnp.float32), 'ln1_b': jnp.zeros((D,), jnp.float32), 'ln2_g': jnp.ones((D,), jnp.float32), 'ln2_b': jnp.zeros((D,), jnp.float32), 'wg': jax.random.normal(ks[3], (D, E), jnp.float32) * s, 'w1': jax.random.normal(ks[4], (E, D, FF), jnp.float32) * s, 'b1': jnp.zeros((E, FF), jnp.float32), 'w2': jax.random.normal(ks[5], (E, FF, D), jnp.float32) * s, 'b2': jnp.zeros((E, D), jnp.float32)}
    _L1_ffn_all = _L1_ffn_setup()
    _L1_ffn_in = {k: v for k, v in _L1_ffn_all.items() if k in ('in_proj_w', 'in_proj_b', 'out_proj_w', 'out_proj_b', 'ln1_g', 'ln1_b', 'ln2_g', 'ln2_b', 'wg', 'w1', 'b1', 'w2', 'b2')}
    del _L1_ffn_all
    return {'x': x, 'ctx_1024': ctx_1024, 'L0_xattn_Wq': _L0_xattn_in['Wq'], 'L0_xattn_bq': _L0_xattn_in['bq'], 'L0_xattn_Wk': _L0_xattn_in['Wk'], 'L0_xattn_bk': _L0_xattn_in['bk'], 'L0_xattn_Wv': _L0_xattn_in['Wv'], 'L0_xattn_bv': _L0_xattn_in['bv'], 'L0_xattn_Wo': _L0_xattn_in['Wo'], 'L0_xattn_bo': _L0_xattn_in['bo'], 'L0_attn_W_qkva': _L0_attn_in['W_qkva'], 'L0_attn_gamma': _L0_attn_in['gamma'], 'L0_ffn_router_w': _L0_ffn_in['router_w'], 'L0_ffn_router_b': _L0_ffn_in['router_b'], 'L0_ffn_expert_w': _L0_ffn_in['expert_w'], 'L0_ffn_expert_b': _L0_ffn_in['expert_b'], 'L1_xattn_Wk': _L1_xattn_in['Wk'], 'L1_xattn_Wv': _L1_xattn_in['Wv'], 'L1_xattn_bv': _L1_xattn_in['bv'], 'L1_xattn_Wq': _L1_xattn_in['Wq'], 'L1_xattn_bq': _L1_xattn_in['bq'], 'L1_xattn_Wo': _L1_xattn_in['Wo'], 'L1_xattn_bo': _L1_xattn_in['bo'], 'L1_attn_Wq': _L1_attn_in['Wq'], 'L1_attn_bq': _L1_attn_in['bq'], 'L1_attn_Wl': _L1_attn_in['Wl'], 'L1_attn_bl': _L1_attn_in['bl'], 'L1_attn_Wk': _L1_attn_in['Wk'], 'L1_attn_bk': _L1_attn_in['bk'], 'L1_attn_Wv': _L1_attn_in['Wv'], 'L1_attn_bv': _L1_attn_in['bv'], 'L1_attn_Wo': _L1_attn_in['Wo'], 'L1_attn_bo': _L1_attn_in['bo'], 'L1_ffn_in_proj_w': _L1_ffn_in['in_proj_w'], 'L1_ffn_in_proj_b': _L1_ffn_in['in_proj_b'], 'L1_ffn_out_proj_w': _L1_ffn_in['out_proj_w'], 'L1_ffn_out_proj_b': _L1_ffn_in['out_proj_b'], 'L1_ffn_ln1_g': _L1_ffn_in['ln1_g'], 'L1_ffn_ln1_b': _L1_ffn_in['ln1_b'], 'L1_ffn_ln2_g': _L1_ffn_in['ln2_g'], 'L1_ffn_ln2_b': _L1_ffn_in['ln2_b'], 'L1_ffn_wg': _L1_ffn_in['wg'], 'L1_ffn_w1': _L1_ffn_in['w1'], 'L1_ffn_b1': _L1_ffn_in['b1'], 'L1_ffn_w2': _L1_ffn_in['w2'], 'L1_ffn_b2': _L1_ffn_in['b2']}

def reference(x, ctx_1024, L0_xattn_Wq, L0_xattn_bq, L0_xattn_Wk, L0_xattn_bk, L0_xattn_Wv, L0_xattn_bv, L0_xattn_Wo, L0_xattn_bo, L0_attn_W_qkva, L0_attn_gamma, L0_ffn_router_w, L0_ffn_router_b, L0_ffn_expert_w, L0_ffn_expert_b, L1_xattn_Wk, L1_xattn_Wv, L1_xattn_bv, L1_xattn_Wq, L1_xattn_bq, L1_xattn_Wo, L1_xattn_bo, L1_attn_Wq, L1_attn_bq, L1_attn_Wl, L1_attn_bl, L1_attn_Wk, L1_attn_bk, L1_attn_Wv, L1_attn_bv, L1_attn_Wo, L1_attn_bo, L1_ffn_in_proj_w, L1_ffn_in_proj_b, L1_ffn_out_proj_w, L1_ffn_out_proj_b, L1_ffn_ln1_g, L1_ffn_ln1_b, L1_ffn_ln2_g, L1_ffn_ln2_b, L1_ffn_wg, L1_ffn_w1, L1_ffn_b1, L1_ffn_w2, L1_ffn_b2):
    import jax
    import jax.numpy as jnp

    def _L0_xattn_ref(q, k, v, Wq, bq, Wk, bk, Wv, bv, Wo, bo):
        import jax, jax.numpy as jnp
        import numpy as np
        DIM = 512
        NUM_HEADS = 16
        HEAD_DIM = DIM // NUM_HEADS
        B, Nq, C = q.shape
        Nkv = k.shape[1]
        H, D = (NUM_HEADS, HEAD_DIM)
        qh = (q @ Wq.T + bq).reshape(B, Nq, H, D).transpose(0, 2, 1, 3)
        kh = (k @ Wk.T + bk).reshape(B, Nkv, H, D).transpose(0, 2, 1, 3)
        vh = (v @ Wv.T + bv).reshape(B, Nkv, H, D).transpose(0, 2, 1, 3)
        scale = D ** (-0.5)
        attn = jax.nn.softmax(jnp.einsum('bhqd,bhkd->bhqk', qh, kh) * scale, axis=-1)
        out = jnp.einsum('bhqk,bhkd->bhqd', attn, vh)
        out = out.transpose(0, 2, 1, 3).reshape(B, Nq, C)
        return out @ Wo.T + bo

    def _L0_attn_ref(x, W_qkva, gamma):
        import jax, jax.numpy as jnp
        import numpy as np
        EPS = 1e-12
        d = gamma.shape[0]
        scale = d ** 0.5
        norm = jnp.maximum(jnp.linalg.norm(x, axis=-1, keepdims=True), EPS)
        xn = x / norm * scale * gamma
        h = jnp.einsum('bnd,ed->bne', xn, W_qkva)
        q, kv, a = jnp.split(h, 3, axis=-1)
        a = jax.nn.sigmoid(a)

        def binop(e_i, e_j):
            a_i, kv_i = e_i
            a_j, kv_j = e_j
            return (a_j * a_i, a_j * kv_i + kv_j)
        _, y = jax.lax.associative_scan(binop, (a, kv), axis=1)
        return q * y

    def _L0_ffn_ref(x, router_w, router_b, expert_w, expert_b):
        import jax, jax.numpy as jnp
        import numpy as np
        B, S, H, E = (4, 1024, 512, 8)
        b, s, h = x.shape
        xt = x.reshape(b * s, h)
        logits = xt @ router_w + router_b
        probs = jax.nn.softmax(logits, axis=-1)
        gate = jnp.max(probs, axis=-1)
        idx = jnp.argmax(probs, axis=-1)
        out_all = jnp.einsum('th,ehd->ted', xt, expert_w) + expert_b[None, :, :]
        e_out = jnp.take_along_axis(out_all, idx[:, None, None], axis=1)[:, 0, :]
        y = gate[:, None] * e_out
        return y.reshape(b, s, h)

    def _L1_xattn_ref(k, v, q, Wk, Wv, bv, Wq, bq, Wo, bo):
        import jax, jax.numpy as jnp
        import numpy as np
        D_MODEL = 512
        B, S = (4, 1024)
        kp = jnp.einsum('bsd,ed->bse', k, Wk)
        vp = jnp.einsum('bsd,ed->bse', v, Wv) + bv
        qp = jnp.einsum('bsd,ed->bse', q, Wq) + bq
        scale = 1.0 / jnp.sqrt(jnp.float32(kp.shape[-1]))
        scores = jnp.einsum('bqd,bkd->bqk', qp, kp) * scale
        probs = jax.nn.softmax(scores, axis=-1)
        ctx = jnp.einsum('bqk,bkd->bqd', probs, vp)
        return jnp.einsum('bqd,ed->bqe', ctx, Wo) + bo

    def _L1_attn_ref(x, Wq, bq, Wl, bl, Wk, bk, Wv, bv, Wo, bo):
        import jax, jax.numpy as jnp
        import numpy as np
        DIM = 512
        HEADS = 16
        DIM_HEAD = DIM // HEADS
        LATENT = DIM // 4
        SCALE = DIM_HEAD ** (-0.5)
        B, S, D = x.shape
        H, Dh = (HEADS, DIM_HEAD)
        q = (x @ Wq + bq).reshape(B, S, H, Dh)
        latent = x @ Wl + bl
        k = (latent @ Wk + bk).reshape(B, S, H, Dh)
        v = (latent @ Wv + bv).reshape(B, S, H, Dh)
        scores = jnp.einsum('bihd,bjhd->bhij', q, k) * SCALE
        attn = jax.nn.softmax(scores, axis=-1)
        out = jnp.einsum('bhij,bjhd->bihd', attn, v).reshape(B, S, D)
        out = out @ Wo + bo
        return out

    def _L1_ffn_ref(x, in_proj_w, in_proj_b, out_proj_w, out_proj_b, ln1_g, ln1_b, ln2_g, ln2_b, wg, w1, b1, w2, b2):
        import jax, jax.numpy as jnp
        import numpy as np
        D = 512
        H = 4
        HD = D // H
        E = 8
        FF = 2048
        CAP_FACTOR = 1.0

        def _ln(x, g, b, eps=1e-05):
            mu = jnp.mean(x, -1, keepdims=True)
            v = jnp.mean((x - mu) ** 2, -1, keepdims=True)
            return (x - mu) * jax.lax.rsqrt(v + eps) * g + b

        def _mha(x, w, b, ow, ob):
            L, N, _ = x.shape
            qkv = x @ w.T + b
            q, k, v = jnp.split(qkv, 3, axis=-1)
            rh = lambda t: t.reshape(L, N, H, HD).transpose(1, 2, 0, 3)
            q, k, v = (rh(q), rh(k), rh(v))
            scores = jnp.einsum('nhld,nhmd->nhlm', q, k) / np.float32(np.sqrt(HD))
            attn = jax.nn.softmax(scores, axis=-1)
            o = jnp.einsum('nhlm,nhmd->nhld', attn, v).transpose(2, 0, 1, 3).reshape(L, N, D)
            return o @ ow.T + ob

        def _moe(x, wg, w1, b1, w2, b2):
            L, N, _ = x.shape
            S = L * N
            cap = int(CAP_FACTOR * S) // E
            xf = x.reshape(S, D)
            gates = jax.nn.softmax(xf @ wg, axis=-1)
            idx = jnp.argmax(gates, axis=-1)
            mask1 = jax.nn.one_hot(idx, E, dtype=x.dtype)
            loc = jnp.sum((jnp.cumsum(mask1, 0) - 1.0) * mask1, -1).astype(jnp.int32)
            keep = loc < cap
            gate_val = jnp.take_along_axis(gates, idx[:, None], -1)[:, 0]
            slot = jnp.where(keep, idx.astype(jnp.int32) * cap + loc, E * cap)
            disp = jnp.zeros((E * cap, D), x.dtype).at[slot].set(xf, mode='drop')
            disp = disp.reshape(E, cap, D)
            h = jnp.einsum('ecd,edf->ecf', disp, w1) + b1[:, None, :]
            y = (jnp.einsum('ecf,efd->ecd', h, w2) + b2[:, None, :]).reshape(E * cap, D)
            out = jnp.where(keep[:, None], gate_val[:, None] * y[jnp.minimum(slot, E * cap - 1)], 0.0)
            return out.reshape(L, N, D)
        y1 = _ln(x + _mha(x, in_proj_w, in_proj_b, out_proj_w, out_proj_b), ln1_g, ln1_b)
        y2 = _ln(y1 + _moe(y1, wg, w1, b1, w2, b2), ln2_g, ln2_b)
        return y2
    x = x + _L0_xattn_ref(_layernorm(x, axis=-1), ctx_1024, ctx_1024, L0_xattn_Wq, L0_xattn_bq, L0_xattn_Wk, L0_xattn_bk, L0_xattn_Wv, L0_xattn_bv, L0_xattn_Wo, L0_xattn_bo)
    x = x + _L0_attn_ref(_layernorm(x, axis=-1), L0_attn_W_qkva, L0_attn_gamma)
    x = x + _L0_ffn_ref(_layernorm(x, axis=-1), L0_ffn_router_w, L0_ffn_router_b, L0_ffn_expert_w, L0_ffn_expert_b)
    x = x + _L1_xattn_ref(ctx_1024, ctx_1024, _layernorm(x, axis=-1), L1_xattn_Wk, L1_xattn_Wv, L1_xattn_bv, L1_xattn_Wq, L1_xattn_bq, L1_xattn_Wo, L1_xattn_bo)
    x = x + _L1_attn_ref(_layernorm(x, axis=-1), L1_attn_Wq, L1_attn_bq, L1_attn_Wl, L1_attn_bl, L1_attn_Wk, L1_attn_bk, L1_attn_Wv, L1_attn_bv, L1_attn_Wo, L1_attn_bo)
    x = x + _L1_ffn_ref(_layernorm(x, axis=-1), L1_ffn_in_proj_w, L1_ffn_in_proj_b, L1_ffn_out_proj_w, L1_ffn_out_proj_b, L1_ffn_ln1_g, L1_ffn_ln1_b, L1_ffn_ln2_g, L1_ffn_ln2_b, L1_ffn_wg, L1_ffn_w1, L1_ffn_b1, L1_ffn_w2, L1_ffn_b2)
    return x

_drawn_inputs = setup_inputs


def setup_inputs(seed=0):
    import zlib

    import numpy as np

    out = dict(_drawn_inputs(seed))
    spreads = {'L0_xattn_bq': (0.0, 0.1),
     'L0_xattn_bk': (0.0, 0.8),
     'L0_xattn_bv': (0.0, 0.1),
     'L0_xattn_bo': (0.0, 0.1),
     'L0_attn_gamma': (1.0, 0.2),
     'L0_ffn_router_b': (0.0, 0.1),
     'L0_ffn_expert_b': (0.0, 0.285),
     'L1_xattn_bv': (0.0, 0.1),
     'L1_xattn_bq': (0.0, 0.421),
     'L1_xattn_bo': (0.0, 0.1),
     'L1_attn_bq': (0.0, 0.71),
     'L1_attn_bl': (0.0, 0.1),
     'L1_attn_bk': (0.0, 0.8),
     'L1_attn_bv': (0.0, 0.1),
     'L1_attn_bo': (0.0, 0.1),
     'L1_ffn_in_proj_b': (0.0, 0.377),
     'L1_ffn_out_proj_b': (0.0, 0.1),
     'L1_ffn_ln1_g': (1.0, 0.2),
     'L1_ffn_ln1_b': (0.0, 0.1),
     'L1_ffn_ln2_g': (1.0, 0.2),
     'L1_ffn_ln2_b': (0.0, 0.1),
     'L1_ffn_b1': (0.0, 0.8),
     'L1_ffn_b2': (0.0, 0.8)}
    factors = {}
    for name, (base, spread) in spreads.items():
        noise = np.random.default_rng([zlib.crc32(name.encode()), seed]).standard_normal(out[name].shape)
        drawn = base * np.exp(spread * noise) if base else spread * noise
        out[name] = jnp.asarray(drawn.astype(out[name].dtype))
    for name, factor in factors.items():
        out[name] = (out[name] * factor).astype(out[name].dtype)
    return out
```

```python
from contextlib import ExitStack

import concourse.bass as bass
from concourse import mybir

F32 = mybir.dt.float32
F32R = mybir.dt.float32r
I32 = mybir.dt.int32
ALU = mybir.AluOpType
ACT = mybir.ActivationFunctionType
AX = mybir.AxisListType

P = 128
D = 512
KC = D // P
B = 8
LAT = 64
T = B * LAT
TC = T // P
KEYS = 1601
KPAD = KEYS + 1
GW = 512
GROUPS = [(s, min(GW, KPAD - s)) for s in range(0, KPAD, GW)]
CHUNKS = [(s, min(P, KEYS - s)) for s in range(0, KEYS, P)]
NCH = len(CHUNKS)
HEADS = 16
HD = D // HEADS
HPC = P // HD
PAIRS = HEADS // 2
E0 = 8
CAP = T // E0
FF = 2048
FC = FF // P
EPS = 1e-5


class Scope:

    def __init__(self, nc, ctx, name):
        self.nc, self.ctx, self.name = nc, ctx, name
        self.sems = []
        ctx.callback(self.close)

    def close(self):
        if self.sems:
            self.nc.clear_and_free_semaphores(self.sems)
            self.nc.all_engine_barrier()

    def sb(self, name, shape, dt=F32):
        return self.ctx.enter_context(self.nc.sbuf_tensor(f"{self.name}_{name}", shape, dt))

    def ps(self, name, shape, dt=F32):
        return self.ctx.enter_context(self.nc.psum_tensor(f"{self.name}_{name}", shape, dt))

    def sem(self, name):
        self.sems.append(self.nc.alloc_semaphore(name=f"{self.name}_{name}"))
        return self.sems[-1]


class Norm:

    def __init__(self, sc, tag):
        self.stats = sc.sb(f"{tag}_stats", [P, TC, 6])
        self.mv = sc.sb(f"{tag}_mv", [P, TC, 2])
        self.std = sc.sb(f"{tag}_std", [P, TC])
        self.rstd = sc.sb(f"{tag}_rstd", [P, TC])
        self.stats_ready = sc.sem(f"{tag}_stats_ready")
        self.var_ready = sc.sem(f"{tag}_var_ready")
        self.std_ready = sc.sem(f"{tag}_std_ready")
        self.rstd_ready = sc.sem(f"{tag}_rstd_ready")
        self.done = sc.sem(f"{tag}_done")

    def vector(self, nc, dve, x, xn):
        for t in range(TC):
            nc.vector.bn_stats(self.stats[:, t, :], x[:, t, :]).then_inc(self.stats_ready, 1)
        dve.wait_ge(self.stats_ready, TC)
        for t in range(TC):
            nc.vector.bn_aggr(self.mv[:, t, :], self.stats[:, t, :]).then_inc(self.stats_ready, 1)
        dve.wait_ge(self.stats_ready, 2 * TC)
        nc.vector.tensor_scalar(self.std[:], self.mv[:, :, 1], EPS, None, ALU.add).then_inc(self.var_ready, 1)
        dve.wait_ge(self.std_ready, 1)
        nc.vector.reciprocal(self.rstd[:], self.std[:]).then_inc(self.rstd_ready, 1)
        dve.wait_ge(self.rstd_ready, 1)
        for t in range(TC):
            nc.vector.tensor_scalar(xn[:, t, :], x[:, t, :], self.mv[:, t, 0:1], self.rstd[:, t:t + 1],
                                    ALU.subtract, ALU.mult).then_inc(self.done, 1)

    def scalar(self, nc, act):
        act.wait_ge(self.var_ready, 1)
        nc.scalar.activation(self.std[:], self.std[:], ACT.Sqrt).then_inc(self.std_ready, 1)


def transpose_rows(nc, out_bank, rows, c, ident):
    for t in range(TC):
        last = nc.tensor.transpose(out_bank[:, t * P:(t + 1) * P], rows[:, t, c * P:(c + 1) * P], ident[:])
    return last


def product(nc, out, pairs):
    for n, (lhsT, rhs) in enumerate(pairs):
        last = nc.tensor.matmul(out, lhsT, rhs, start=(n == 0), stop=(n == len(pairs) - 1))
    return last


def product3(nc, out, parts):
    n, N = 0, 3 * len(parts)
    for (ah, al), (bh, bl) in parts:
        for a, b in ((ah, bh), (ah, bl), (al, bh)):
            last = nc.tensor.matmul(out, a, b, start=(n == 0), stop=(n == N - 1))
            n += 1
    return last


def phase_queries(nc, dram, res):
    with ExitStack() as ctx:
        sc = Scope(nc, ctx, "qry")
        x = sc.sb("x", [P, TC, D])
        xn = sc.sb("xn", [P, TC, D])
        xnT = sc.sb("xnT", [P, KC, T])
        wq = sc.sb("wq", [P, KC, D])
        wkv = sc.sb("wkv", [P, 2, KC, D])
        bq = sc.sb("bq", [P, KC])
        norm = Norm(sc, "ln")
        banks = [sc.ps(f"bank{i}", [P, T]) for i in range(2 * KC)]
        x_in, wq_in, bq_in, wkv_in = sc.sem("x_in"), sc.sem("wq_in"), sc.sem("bq_in"), sc.sem("wkv_in")
        bk_in = sc.sem("bk_in")
        ident0, ident_ready = sc.sem("ident0"), sc.sem("ident_ready")
        turned, turned_out, q_mm, q_out = sc.sem("turned"), sc.sem("turned_out"), sc.sem("q_mm"), sc.sem("q_out")
        w_hi, w_lo = sc.sem("w_hi"), sc.sem("w_lo")
        block = ctx.enter_context(nc.Block())

        @block.sync
        def _(sp):
            sp.dma_start(x[:], dram["x"].rearrange("(t p) d -> p t d", p=P)).then_inc(x_in, 16)
            sp.dma_start(wq[:], dram["L0_xattn_Wq"]).then_inc(wq_in, 16)
            sp.dma_start(bq[:], dram["L0_xattn_bq"]).then_inc(bq_in, 16)
            sp.dma_start(res["bk"][:], dram["L0_xattn_bk"]).then_inc(bk_in, 16)
            sp.dma_start(wkv[:, 0], dram["L0_xattn_Wk"]).then_inc(wkv_in, 16)
            sp.dma_start(wkv[:, 1], dram["L0_xattn_Wv"]).then_inc(wkv_in, 16)
            sp.wait_ge(bk_in, 16)

        @block.gpsimd
        def _(pool):
            nc.gpsimd.memset(res["ident"][:], 0.0).then_inc(ident0, 1)
            pool.wait_ge(ident0, 1)
            nc.gpsimd.affine_select(out=res["ident"][:], in_=res["ident"][:], compare_op=ALU.not_equal, fill=1.0,
                                    base=0, pattern=[[-1, P]], channel_multiplier=1).then_inc(ident_ready, 1)
            nc.gpsimd.memset(res["q_blk_hi"][:].bitcast(F32), 0.0)
            nc.gpsimd.memset(res["q_blk_lo"][:].bitcast(F32), 0.0)
            for i in range(2):
                pool.wait_ge(w_hi, i + 1)
                nc.gpsimd.tensor_tensor(res["w_lo"][:, i], wkv[:, i], res["w_hi"][:, i].bitcast(F32),
                                        ALU.subtract).then_inc(w_lo, 1)

        @block.scalar
        def _(act):
            norm.scalar(nc, act)
            act.wait_ge(wkv_in, 32)
            for i in range(2):
                nc.scalar.activation(res["w_hi"][:, i], wkv[:, i], ACT.Copy).then_inc(w_hi, 1)
            for c in range(KC):
                act.wait_ge(turned, c + 1)
                nc.scalar.activation(xnT[:, c, :], banks[c][:], ACT.Copy).then_inc(turned_out, 1)

        @block.vector
        def _(dve):
            dve.wait_ge(x_in, 16)
            norm.vector(nc, dve, x, xn)
            dve.wait_ge(bq_in, 16)
            for o in range(KC):
                dve.wait_ge(q_mm, o + 1)
                nc.vector.tensor_scalar(res["qT"][:, o, :], banks[KC + o][:], bq[:, o:o + 1], HD ** -0.5,
                                        ALU.add, ALU.mult).then_inc(q_out, 1)

        @block.tensor
        def _(pe):
            pe.wait_ge(ident_ready, 1)
            pe.wait_ge(norm.done, TC)
            for c in range(KC):
                transpose_rows(nc, banks[c], xn, c, res["ident"]).then_inc(turned, 1)
            pe.wait_ge(wq_in, 16)
            pe.wait_ge(turned_out, KC)
            for o in range(KC):
                product(nc, banks[KC + o][:], [(wq[:, k, o * P:(o + 1) * P], xnT[:, k, :]) for k in range(KC)]
                        ).then_inc(q_mm, 1)


def v_uses(half):
    sizes = [2] * 6 + [1] if half == 0 else [2] * 5 + [1] * 3
    at = 0
    for n in sizes:
        yield ("v", half, at, n)
        at += n


SLOTS = []
for _p in range(PAIRS):
    _fill = []
    if _p < PAIRS - 2:
        _g = _p // 2 + 1
        _fill += [("k", _g, 2 * (_p % 2)), ("k", _g, 2 * (_p % 2) + 1)]
    if _p == 5:
        _fill += list(v_uses(1))
    if _p:
        _fill += [("t", _p - 1, i) for i in range(4)]
    SLOTS.append(_fill)
HEAD = list(v_uses(0)) + [("k", 0, i) for i in range(4)]
TAIL = [("t", PAIRS - 1, i) for i in range(4)]
ORDER = HEAD + [u for s in SLOTS for u in s] + TAIL
USE = {u: n for n, u in enumerate(ORDER)}
NUSE = len(ORDER)
RING = 3
assert NUSE % RING == 0


START = 1


def phase_cross(nc, dram, res):
    with ExitStack() as ctx:
        sc = Scope(nc, ctx, "crs")
        stage = [sc.sb(f"stage{i}", [P, KC, GW]) for i in range(2)]
        ct_hi = sc.sb("ct_hi", [P, KC, KPAD], F32R)
        ct_lo = sc.sb("ct_lo", [P, KC, KPAD], F32R)
        kt_hi = sc.sb("kt_hi", [P, 2, KPAD], F32R)
        kt_lo = sc.sb("kt_lo", [P, 2, KPAD], F32R)
        v_hi = sc.sb("v_hi", [P, NCH, 2 * P], F32R)
        v_lo = sc.sb("v_lo", [P, NCH, 2 * P], F32R)
        pt_hi = sc.sb("pt_hi", [P, NCH, P], F32R)
        pt_lo = sc.sb("pt_lo", [P, NCH, P], F32R)
        prob = sc.sb("prob", [P, 2, KEYS])
        mx = sc.sb("mx", [P, 2])
        nmx = sc.sb("nmx", [P, 2])
        rsum = sc.sb("rsum", [P, 2])
        rinv = sc.sb("rinv", [P, 2])
        w_hi, w_lo, q_hi, q_lo = res["w_hi"], res["w_lo"], res["q_blk_hi"], res["q_blk_lo"]
        qT, oT, bk, ident = res["qT"], res["oT"], res["bk"], res["ident"]

        score = sc.ps("score", [P, 4 * GW])
        ring = [sc.ps(f"ring{i}", [P, GW]) for i in range(RING)]
        out_bank = sc.ps("out_bank", [P, GW])

        ct_in = [sc.sem(f"ct_in{i}") for i in range(2)]
        ct_hi_ready, ct_lo_ready = sc.sem("ct_hi_ready"), sc.sem("ct_lo_ready")
        q_hi_ready, q_lo_ready = sc.sem("q_hi_ready"), sc.sem("q_lo_ready")
        filled = sc.sem("filled")
        hi_out = sc.sem("hi_out")
        freed = sc.sem("freed")
        scored = sc.sem("scored")
        max_ready, nmax_ready, exp_done = sc.sem("max_ready"), sc.sem("nmax_ready"), sc.sem("exp_done")
        rinv_ready, prob_ready = sc.sem("rinv_ready"), sc.sem("prob_ready")
        pv_done, o_out = sc.sem("pv_done"), sc.sem("o_out")
        block = ctx.enter_context(nc.Block())
        NG = len(GROUPS)
        ctxT = dram["ctxT"]

        @block.sync
        def _(sp):
            def load(b, g):
                s, w = GROUPS[g]
                sp.dma_start(stage[g % 2][:, :, 0:w], ctxT[b, :, :, s:s + w]).then_inc(ct_in[g % 2], 16)

            load(0, 0)
            load(0, 1)

            def turn(b, last):
                for g in range(NG):
                    if last and g >= 2:
                        break
                    sp.wait_ge(ct_lo_ready, NG * b + g + 1)
                    if g < 2:
                        load(b, g + 2)
                    else:
                        load(b + 1, g - 2)

            with sp.Fori(0, B - 1) as b:
                turn(b, False)
            turn(B - 1, True)

        @block.gpsimd
        def _(pool):
            with pool.Fori(0, B) as b:
                for g, (s, w) in enumerate(GROUPS):
                    pool.wait_ge(ct_hi_ready, NG * b + g + 1)
                    nc.gpsimd.tensor_tensor(ct_lo[:, :, s:s + w], stage[g % 2][:, :, 0:w],
                                            ct_hi[:, :, s:s + w].bitcast(F32), ALU.subtract).then_inc(ct_lo_ready, 1)

        def out_tiles(use):
            bank = ring[USE[use] % RING]
            if use[0] == "v":
                _, half, c0, n = use
                kk = CHUNKS[c0][1]
                view = bank[0:kk, 0:n * 2 * P].rearrange("p (c f) -> p c f", c=n)
                return view, v_hi[0:kk, c0:c0 + n, :], v_lo[0:kk, c0:c0 + n, :]
            if use[0] == "k":
                _, fc, g = use
                s, w = GROUPS[g]
                return bank[:, 0:w], kt_hi[:, fc % 2, s:s + w], kt_lo[:, fc % 2, s:s + w]
            _, p, i = use
            if i < 3:
                view = bank[:].rearrange("p (c f) -> p c f", c=4)
                return view, pt_hi[:, 4 * i:4 * i + 4, :], pt_lo[:, 4 * i:4 * i + 4, :]
            kk = CHUNKS[NCH - 1][1]
            return bank[0:kk, 0:P], pt_hi[0:kk, NCH - 1, :], pt_lo[0:kk, NCH - 1, :]

        def reusable(eng, use, b):
            if use[0] == "v":
                eng.wait_ge(pv_done, START + PAIRS * b + 4 * use[1])
            elif use[0] == "k":
                eng.wait_ge(scored, START + PAIRS * b + max(0, 2 * use[1] - 2))
            else:
                eng.wait_ge(pv_done, START + PAIRS * b + use[1])

        @block.scalar
        def _(act):
            act.sem_inc(exp_done, START)

            def empty_high(use, b):
                view, hi, _ = out_tiles(use)
                reusable(act, use, b)
                act.wait_ge(filled, START + NUSE * b + USE[use] + 1)
                if use[0] == "k":
                    nc.scalar.activation(hi, view, ACT.Identity, bias=bk[:, use[1]:use[1] + 1]).then_inc(hi_out, 1)
                else:
                    nc.scalar.activation(hi, view, ACT.Copy).then_inc(hi_out, 1)

            with act.Fori(0, B) as b:
                act.wait_ge(filled, START + NUSE * b)
                for g, (s, w) in enumerate(GROUPS):
                    act.wait_ge(ct_in[g % 2], 32 * b + 16 * (g // 2 + 1))
                    nc.scalar.activation(ct_hi[:, :, s:s + w], stage[g % 2][:, :, 0:w], ACT.Copy
                                         ).then_inc(ct_hi_ready, 1)
                act.wait_ge(scored, START + PAIRS * b)
                for h in range(HPC):
                    r = slice(h * HD, (h + 1) * HD)
                    last = nc.scalar.activation(q_hi[r, :, h // 2, (h % 2) * LAT:(h % 2 + 1) * LAT],
                                                qT[r, :, bass.ts(b, LAT)], ACT.Copy)
                last.then_inc(q_hi_ready, 1)
                for use in HEAD:
                    empty_high(use, b)
                for p in range(PAIRS):
                    act.wait_ge(nmax_ready, PAIRS * b + p + 1)
                    nc.scalar.activation(prob[:, p % 2, :], score[:, 0:KEYS], ACT.Exp, bias=nmx[:, p % 2:p % 2 + 1],
                                         accum_out=rsum[:, p % 2:p % 2 + 1]).then_inc(exp_done, 1)
                    for use in SLOTS[p]:
                        empty_high(use, b)
                for use in TAIL:
                    empty_high(use, b)

        @block.vector
        def _(dve):
            dve.sem_inc(freed, RING)
            dve.sem_inc(o_out, START)

            def empty_low(use, b):
                view, hi, lo = out_tiles(use)
                dve.wait_ge(hi_out, NUSE * b + USE[use] + 1)
                if use[0] == "k":
                    nc.vector.scalar_tensor_tensor(lo, view, bk[:, use[1]:use[1] + 1], hi.bitcast(F32),
                                                   ALU.add, ALU.subtract).then_inc(freed, 1)
                else:
                    nc.vector.tensor_tensor(lo, view, hi.bitcast(F32), ALU.subtract).then_inc(freed, 1)

            def normalise(p, b):
                i = p % 2
                dve.wait_ge(exp_done, START + PAIRS * b + p + 1)
                nc.vector.reciprocal(rinv[:, i:i + 1], rsum[:, i:i + 1]).then_inc(rinv_ready, 1)
                dve.wait_ge(rinv_ready, PAIRS * b + p + 1)
                nc.vector.tensor_scalar(prob[:, i, :], prob[:, i, :], rinv[:, i:i + 1], None, ALU.mult
                                        ).then_inc(prob_ready, 1)

            def take_out(p, b):
                fc, i = p // 2, p % 2
                dve.wait_ge(pv_done, START + PAIRS * b + p + 1)
                for j in range(2):
                    h = 2 * i + j
                    last = nc.vector.tensor_copy(oT[h * HD:(h + 1) * HD, fc, bass.ts(b, LAT)],
                                                 out_bank[h * HD:(h + 1) * HD, j * LAT:(j + 1) * LAT])
                last.then_inc(o_out, 1)

            with dve.Fori(0, B) as b:
                dve.wait_ge(q_hi_ready, b + 1)
                for h in range(HPC):
                    r = slice(h * HD, (h + 1) * HD)
                    at = (r, slice(None), h // 2, slice((h % 2) * LAT, (h % 2 + 1) * LAT))
                    last = nc.vector.tensor_tensor(q_lo[at], qT[r, :, bass.ts(b, LAT)], q_hi[at].bitcast(F32),
                                                   ALU.subtract)
                last.then_inc(q_lo_ready, 1)
                for use in HEAD:
                    empty_low(use, b)
                for p in range(PAIRS):
                    i = p % 2
                    dve.wait_ge(scored, START + PAIRS * b + p + 1)
                    nc.vector.reduce_max(mx[:, i:i + 1], score[:, 0:KEYS], AX.X).then_inc(max_ready, 1)
                    dve.wait_ge(max_ready, PAIRS * b + p + 1)
                    nc.vector.tensor_scalar(nmx[:, i:i + 1], mx[:, i:i + 1], -1.0, None, ALU.mult
                                            ).then_inc(nmax_ready, 1)
                    for use in SLOTS[p]:
                        empty_low(use, b)
                    normalise(p, b)
                    if p:
                        take_out(p - 1, b)
                for use in TAIL:
                    empty_low(use, b)
                take_out(PAIRS - 1, b)

        @block.tensor
        def _(pe):
            for counter in (filled, scored, pv_done):
                pe.sem_inc(counter, START)

            def bank_for(use, b):
                pe.wait_ge(freed, NUSE * b + USE[use] + 1)
                return ring[USE[use] % RING]

            def written(use, b):
                pe.wait_ge(freed, NUSE * b + USE[use] + 1 + RING)

            def fill(use, b):
                bank = bank_for(use, b)
                if use[0] == "v":
                    _, half, c0, n = use
                    for c in range(c0, c0 + n):
                        s, kk = CHUNKS[c]
                        if half == 0:
                            pe.wait_ge(ct_lo_ready, NG * b + s // GW + 1)
                        f = slice(half * 2 * P, (half + 1) * 2 * P)
                        last = product3(nc, bank[0:kk, (c - c0) * 2 * P:(c - c0 + 1) * 2 * P],
                                        [((ct_hi[:, k, s:s + kk], ct_lo[:, k, s:s + kk]),
                                          (w_hi[:, 1, k, f], w_lo[:, 1, k, f])) for k in range(KC)])
                elif use[0] == "k":
                    _, fc, g = use
                    s, w = GROUPS[g]
                    f = slice(fc * P, (fc + 1) * P)
                    last = product3(nc, bank[:, 0:w],
                                    [((w_hi[:, 0, k, f], w_lo[:, 0, k, f]),
                                      (ct_hi[:, k, s:s + w], ct_lo[:, k, s:s + w])) for k in range(KC)])
                else:
                    _, p, i = use
                    if i == 0:
                        pe.wait_ge(prob_ready, PAIRS * b + p + 1)
                    for c in range(4 * i, min(4 * i + 4, NCH)):
                        s, kk = CHUNKS[c]
                        last = nc.tensor.transpose(bank[0:kk, (c - 4 * i) * P:(c - 4 * i + 1) * P],
                                                   prob[:, p % 2, s:s + kk], ident[:])
                last.then_inc(filled, 1)

            def scores(p, b):
                fc, i = p // 2, p % 2
                pe.wait_ge(exp_done, START + PAIRS * b + p)
                for g, (s, w) in enumerate(GROUPS):
                    if i == 0:
                        written(("k", fc, g), b)
                    last = product3(nc, score[:, s:s + w],
                                    [((q_hi[:, fc, i, :], q_lo[:, fc, i, :]),
                                      (kt_hi[:, fc % 2, s:s + w], kt_lo[:, fc % 2, s:s + w]))])
                last.then_inc(scored, 1)

            def weigh(p, b):
                fc = p // 2
                f = slice((fc % 2) * P, (fc % 2 + 1) * P)
                pe.wait_ge(o_out, START + PAIRS * b + p)
                parts = []
                for c, (s, kk) in enumerate(CHUNKS):
                    parts.append(((v_hi[0:kk, c, f], v_lo[0:kk, c, f]), (pt_hi[0:kk, c, :], pt_lo[0:kk, c, :])))
                n = 0
                for c, ((vh, vl), (ph, pl)) in enumerate(parts):
                    if c % 4 == 0:
                        written(("t", p, c // 4), b)
                    for a, m in ((vh, ph), (vh, pl), (vl, ph)):
                        last = nc.tensor.matmul(out_bank[:, 0:P], a, m, start=(n == 0), stop=(n == 3 * NCH - 1))
                        n += 1
                last.then_inc(pv_done, 1)

            with pe.Fori(0, B) as b:
                for use in HEAD:
                    fill(use, b)
                pe.wait_ge(q_lo_ready, b + 1)
                for p in range(PAIRS):
                    scores(p, b)
                    for use in SLOTS[p]:
                        fill(use, b)
                    if p:
                        weigh(p - 1, b)
                for use in TAIL:
                    fill(use, b)
                weigh(PAIRS - 1, b)


def phase_cross_out(nc, dram, res):
    with ExitStack() as ctx:
        sc = Scope(nc, ctx, "cro")
        wo = sc.sb("wo", [P, KC, D])
        bo = sc.sb("bo", [P, D])
        bv = sc.sb("bv", [P, KC])
        xb = sc.sb("xb", [P, TC, D])
        x, oT = res["x"], res["oT"]
        banks = [sc.ps(f"bank{i}", [P, D]) for i in range(TC)]
        x_in, w_in, bo_in, bv_in = sc.sem("x_in"), sc.sem("w_in"), sc.sem("bo_in"), sc.sem("bv_in")
        biased, o_biased, mm, out = sc.sem("biased"), sc.sem("o_biased"), sc.sem("mm"), sc.sem("out")
        block = ctx.enter_context(nc.Block())

        @block.sync
        def _(sp):
            sp.dma_start(bv[:], dram["L0_xattn_bv"]).then_inc(bv_in, 16)
            sp.dma_start(wo[:], dram["L0_xattn_Wo"]).then_inc(w_in, 16)
            sp.dma_start(x[:], dram["x"].rearrange("(t p) d -> p t d", p=P)).then_inc(x_in, 16)
            sp.dma_start(bo[:], dram["L0_xattn_bo"].partition_broadcast(P)).then_inc(bo_in, 16)

        @block.vector
        def _(dve):
            dve.wait_ge(bv_in, 16)
            for c in range(KC):
                nc.vector.tensor_scalar(oT[:, c, :], oT[:, c, :], bv[:, c:c + 1], None, ALU.add
                                        ).then_inc(o_biased, 1)
            dve.wait_ge(x_in, 16)
            dve.wait_ge(bo_in, 16)
            for t in range(TC):
                nc.vector.tensor_tensor(xb[:, t, :], x[:, t, :], bo[:], ALU.add).then_inc(biased, 1)
            for t in range(TC):
                dve.wait_ge(mm, t + 1)
                dve.wait_ge(biased, t + 1)
                nc.vector.tensor_tensor(x[:, t, :], xb[:, t, :], banks[t][:], ALU.add).then_inc(out, 1)

        @block.tensor
        def _(pe):
            pe.wait_ge(w_in, 16)
            pe.wait_ge(o_biased, KC)
            for t in range(TC):
                product(nc, banks[t][:], [(oT[:, c, t * P:(t + 1) * P], wo[:, c, :]) for c in range(KC)]
                        ).then_inc(mm, 1)


def phase_scan(nc, dram, ident, x):
    with ExitStack() as ctx:
        sc = Scope(nc, ctx, "scn")
        xn = sc.sb("xn", [P, TC, D])
        sq = sc.sb("sq", [P, D])
        ss = sc.sb("ss", [P, TC])
        nrm = sc.sb("nrm", [P, TC])
        rn = sc.sb("rn", [P, TC])
        xs = sc.sb("xs", [P, TC, D])
        xnT = sc.sb("xnT", [P, KC, T])
        w = sc.sb("w", [P, KC, 3 * D])
        gamma = sc.sb("gamma", [P, KC])
        decay = sc.sb("decay", [P, KC, T])
        y = sc.sb("y", [P, KC, T])
        yq = sc.sb("yq", [P, KC, T])
        norm = Norm(sc, "ln")
        banks = [sc.ps(f"bank{i}", [P, T]) for i in range(8)]
        g_in, w_in = sc.sem("g_in"), sc.sem("w_in")
        squared, nrm_ready, nrm_done = sc.sem("squared"), sc.sem("nrm_ready"), sc.sem("nrm_done")
        scaled, turned, turned_out, mm = sc.sem("scaled"), sc.sem("turned"), sc.sem("turned_out"), sc.sem("mm")
        decay_ready, decay_cut, scanned = sc.sem("decay_ready"), sc.sem("decay_cut"), sc.sem("scanned")
        gated, back, out = sc.sem("gated"), sc.sem("back"), sc.sem("out")
        KV, A, Q = range(3)
        column = {KV: 1, A: 2, Q: 0}

        def bank(f, part):
            return banks[(KC + 3 * f + part) % 8]

        block = ctx.enter_context(nc.Block())

        @block.sync
        def _(sp):
            sp.dma_start(gamma[:], dram["L0_attn_gamma"]).then_inc(g_in, 16)
            sp.dma_start(w[:], dram["L0_attn_W_qkva"]).then_inc(w_in, 16)

        @block.scalar
        def _(act):
            norm.scalar(nc, act)
            for t in range(TC):
                act.wait_ge(norm.done, t + 1)
                if t:
                    act.wait_ge(squared, t)
                nc.scalar.activation(sq[:], xn[:, t, :], ACT.Square, accum_out=ss[:, t:t + 1]).then_inc(squared, 1)
            act.wait_ge(squared, TC)
            nc.scalar.activation(nrm[:], ss[:], ACT.Sqrt).then_inc(nrm_ready, 1)
            act.wait_ge(g_in, 16)
            for c in range(KC):
                act.wait_ge(turned, c + 1)
                nc.scalar.activation(xnT[:, c, :], banks[c][:], ACT.Copy, scale=gamma[:, c:c + 1]
                                     ).then_inc(turned_out, 1)
            for f in range(KC):
                act.wait_ge(mm, 3 * f + A + 1)
                nc.scalar.activation(decay[:, f, :], bank(f, A)[:], ACT.Sigmoid).then_inc(decay_ready, 1)

        @block.vector
        def _(dve):
            norm.vector(nc, dve, x, xn)
            dve.wait_ge(nrm_ready, 1)
            nc.vector.tensor_scalar(nrm[:], nrm[:], 1e-12, D ** -0.5, ALU.max, ALU.mult).then_inc(nrm_done, 1)
            dve.wait_ge(nrm_done, 1)
            nc.vector.reciprocal(rn[:], nrm[:]).then_inc(nrm_done, 1)
            dve.wait_ge(nrm_done, 2)
            for t in range(TC):
                nc.vector.tensor_scalar(xs[:, t, :], xn[:, t, :], rn[:, t:t + 1], None, ALU.mult
                                        ).then_inc(scaled, 1)
            for f in range(KC):
                dve.wait_ge(decay_ready, f + 1)
                nc.vector.memset(decay[:, f, :].rearrange("p (b n) -> p b n", b=B)[:, :, 0:1], 0.0
                                 ).then_inc(decay_cut, 1)
                dve.wait_ge(decay_cut, f + 1)
                nc.vector.tensor_tensor_scan(y[:, f, :], decay[:, f, :], bank(f, KV)[:], 0.0, ALU.mult, ALU.add
                                             ).then_inc(scanned, 1)
                dve.wait_ge(scanned, f + 1)
                dve.wait_ge(mm, 3 * f + Q + 1)
                nc.vector.tensor_tensor(yq[:, f, :], y[:, f, :], bank(f, Q)[:], ALU.mult).then_inc(gated, 1)
            for t in range(TC):
                dve.wait_ge(back, t + 1)
                nc.vector.tensor_tensor(x[:, t, :], x[:, t, :], banks[t][:], ALU.add).then_inc(out, 1)

        @block.tensor
        def _(pe):
            pe.wait_ge(scaled, TC)
            for c in range(KC):
                transpose_rows(nc, banks[c], xs, c, ident).then_inc(turned, 1)
            pe.wait_ge(turned_out, KC)
            pe.wait_ge(w_in, 16)
            for f in range(KC):
                for part in (KV, A, Q):
                    n = 3 * f + part
                    if n >= 8:
                        pe.wait_ge(gated, (n - 8) // 3 + 1)
                    o = column[part] * D + f * P
                    product(nc, bank(f, part)[:], [(w[:, k, o:o + P], xnT[:, k, :]) for k in range(KC)]
                            ).then_inc(mm, 1)
            pe.wait_ge(gated, KC)
            for t in range(TC):
                for f in range(KC):
                    last = nc.tensor.transpose(banks[t][:, f * P:(f + 1) * P], yq[:, f, t * P:(t + 1) * P], ident[:])
                last.then_inc(back, 1)


class Route:

    def __init__(self, sc, dram, bias=None):
        self.dram, self.bias = dram, bias
        shape = [P, TC, E0]
        self.rank = sc.sb("rt_rank", shape)
        self.rb = sc.sb("rt_bias", [P, E0]) if bias is not None else None
        self.lg, self.dl, self.ex = (sc.sb(f"rt_{n}", shape) for n in ("lg", "dl", "ex"))
        self.eq, self.cand, self.mask, self.coef = (sc.sb(f"rt_{n}", shape) for n in ("eq", "cand", "mask", "coef"))
        self.mx, self.sum, self.gate, self.best = (sc.sb(f"rt_{n}", [P, TC]) for n in ("mx", "sum", "gate", "best"))
        self.const_in = sc.sem("rt_const_in")
        self.step = sc.sem("rt_step")
        self.dl_ready, self.ex_ready, self.done = (sc.sem(f"rt_{n}") for n in ("dl_ready", "ex_ready", "done"))

    def sync(self, sp):
        sp.dma_start(self.rank[:], self.dram["rank"].partition_broadcast(P)).then_inc(self.const_in, 16)
        if self.bias is not None:
            sp.dma_start(self.rb[:], self.bias.partition_broadcast(P)).then_inc(self.const_in, 16)

    def scalar(self, nc, act):
        act.wait_ge(self.dl_ready, 1)
        nc.scalar.activation(self.ex[:], self.dl[:], ACT.Exp).then_inc(self.ex_ready, 1)

    def vector(self, nc, dve, logits):
        n = [0]

        def step(ins):
            n[0] += 1
            ins.then_inc(self.step, 1)
            dve.wait_ge(self.step, n[0])

        wide = lambda a: a[:].unsqueeze(2).broadcast_to([P, TC, E0])
        dve.wait_ge(self.const_in, 32 if self.bias is not None else 16)
        if self.bias is not None:
            step(nc.vector.tensor_tensor(self.lg[:], logits, self.rb[:].unsqueeze(1).broadcast_to([P, TC, E0]),
                                         ALU.add))
        else:
            step(nc.vector.tensor_copy(self.lg[:], logits))
        step(nc.vector.reduce_max(self.mx[:], self.lg[:], AX.X))
        nc.vector.tensor_tensor(self.dl[:], self.lg[:], wide(self.mx), ALU.subtract).then_inc(self.dl_ready, 1)
        step(nc.vector.tensor_tensor(self.eq[:], self.lg[:], wide(self.mx), ALU.is_equal))
        step(nc.vector.tensor_tensor(self.cand[:], self.eq[:], self.rank[:], ALU.mult))
        step(nc.vector.reduce_max(self.best[:], self.cand[:], AX.X))
        step(nc.vector.tensor_tensor(self.mask[:], self.cand[:], wide(self.best), ALU.is_equal))
        dve.wait_ge(self.ex_ready, 1)
        step(nc.vector.reduce_sum(self.sum[:], self.ex[:], AX.X))
        step(nc.vector.reciprocal(self.gate[:], self.sum[:]))
        nc.vector.tensor_tensor(self.coef[:], self.mask[:], wide(self.gate), ALU.mult).then_inc(self.done, 1)


def phase_experts(nc, dram, ident, x):
    with ExitStack() as ctx:
        sc = Scope(nc, ctx, "moe")
        RINGW = 3
        xn = sc.sb("xn", [P, TC, D])
        xnT = sc.sb("xnT", [P, KC, T])
        wr = sc.sb("wr", [P, KC, E0])
        eb = sc.sb("eb", [E0, D])
        ew = [sc.sb(f"ew{i}", [P, KC, D]) for i in range(RINGW)]
        coefT = sc.sb("coefT", [E0, T])
        norm = Norm(sc, "ln")
        rt = Route(sc, dram, dram["L0_ffn_router_b"])
        banks = [sc.ps(f"bank{i}", [P, T]) for i in range(8)]
        wr_in, eb_in = sc.sem("wr_in"), sc.sem("eb_in")
        ew_in = [sc.sem(f"ew_in{i}") for i in range(RINGW)]
        turned, turned_out, routed = sc.sem("turned"), sc.sem("turned_out"), sc.sem("routed")
        coef_turned, coef_out = sc.sem("coef_turned"), sc.sem("coef_out")
        bias_mm, biased, mm, added = sc.sem("bias_mm"), sc.sem("biased"), sc.sem("mm"), sc.sem("added")
        block = ctx.enter_context(nc.Block())

        @block.sync
        def _(sp):
            sp.dma_start(wr[:], dram["L0_ffn_router_w"]).then_inc(wr_in, 16)
            rt.sync(sp)
            sp.dma_start(eb[:], dram["L0_ffn_expert_b"]).then_inc(eb_in, 16)
            for e in range(E0):
                if e >= RINGW:
                    sp.wait_ge(mm, TC * (e - RINGW + 1))
                sp.dma_start(ew[e % RINGW][:], dram["L0_ffn_expert_w"][e]).then_inc(ew_in[e % RINGW], 16)

        @block.scalar
        def _(act):
            norm.scalar(nc, act)
            for c in range(KC):
                act.wait_ge(turned, c + 1)
                nc.scalar.activation(xnT[:, c, :], banks[c][:], ACT.Copy).then_inc(turned_out, 1)
            rt.scalar(nc, act)
            act.wait_ge(coef_turned, 1)
            nc.scalar.activation(coefT[:], banks[5][0:E0, :], ACT.Copy).then_inc(coef_out, 1)

        @block.vector
        def _(dve):
            norm.vector(nc, dve, x, xn)
            dve.wait_ge(routed, 1)
            rt.vector(nc, dve, banks[4][:, 0:TC * E0].rearrange("p (t e) -> p t e", t=TC))
            dve.wait_ge(rt.done, 1)
            for t in range(TC):
                dve.wait_ge(bias_mm, t + 1)
                nc.vector.tensor_tensor(x[:, t, :], x[:, t, :], banks[t][:], ALU.add).then_inc(added, 1)
            for e in range(E0):
                for t in range(TC):
                    n = e * TC + t
                    dve.wait_ge(mm, n + 1)
                    dve.wait_ge(added, n + 1)
                    nc.vector.scalar_tensor_tensor(x[:, t, :], banks[4 + t][:] if e % 2 == 0 else banks[t][:],
                                                   rt.coef[:, t, e:e + 1], x[:, t, :], ALU.mult, ALU.add
                                                   ).then_inc(added, 1)

        @block.tensor
        def _(pe):
            pe.wait_ge(norm.done, TC)
            for c in range(KC):
                transpose_rows(nc, banks[c], xn, c, ident).then_inc(turned, 1)
            pe.wait_ge(turned_out, KC)
            pe.wait_ge(wr_in, 16)
            for t in range(TC):
                last = product(nc, banks[4][:, t * E0:(t + 1) * E0],
                               [(xnT[:, k, t * P:(t + 1) * P], wr[:, k, :]) for k in range(KC)])
            last.then_inc(routed, 1)
            pe.wait_ge(rt.done, 1)
            for t in range(TC):
                last = nc.tensor.transpose(banks[5][0:E0, t * P:(t + 1) * P], rt.coef[:, t, :], ident[:])
            last.then_inc(coef_turned, 1)
            pe.wait_ge(coef_out, 1)
            pe.wait_ge(eb_in, 16)
            for t in range(TC):
                product(nc, banks[t][:], [(coefT[:, t * P:(t + 1) * P], eb[:])]).then_inc(bias_mm, 1)
            for e in range(E0):
                pe.wait_ge(ew_in[e % RINGW], 16 * (e // RINGW + 1))
                for t in range(TC):
                    n = e * TC + t
                    pe.wait_ge(added, max(1, n - TC + 1))
                    product(nc, banks[4 + t][:] if e % 2 == 0 else banks[t][:],
                            [(xnT[:, k, t * P:(t + 1) * P], ew[e % RINGW][:, k, :]) for k in range(KC)]
                            ).then_inc(mm, 1)


def phase_context(nc, dram, ident, x):
    with ExitStack() as ctx:
        sc = Scope(nc, ctx, "ctx")
        qk = sc.sb("qk", [P, KC, T])
        u = sc.sb("u", [P, TC, D])
        with ExitStack() as c2:
            s2 = Scope(nc, c2, "ctq")
            xn = s2.sb("xn", [P, TC, D])
            xnT = s2.sb("xnT", [P, KC, T])
            qT = s2.sb("qT", [P, KC, T])
            wq, wk = s2.sb("wq", [P, KC, D]), s2.sb("wk", [P, KC, D])
            bq = s2.sb("bq", [P, KC])
            norm = Norm(s2, "ln")
            banks = [s2.ps(f"bank{i}", [P, T]) for i in range(8)]
            wq_in, wk_in, bq_in = s2.sem("wq_in"), s2.sem("wk_in"), s2.sem("bq_in")
            turned, turned_out = s2.sem("turned"), s2.sem("turned_out")
            q_mm, q_out, qk_mm, qk_out = s2.sem("q_mm"), s2.sem("q_out"), s2.sem("qk_mm"), s2.sem("qk_out")
            block = c2.enter_context(nc.Block())

            @block.sync
            def _(sp):
                sp.dma_start(wq[:], dram["L1_xattn_Wq"]).then_inc(wq_in, 16)
                sp.dma_start(bq[:], dram["L1_xattn_bq"]).then_inc(bq_in, 16)
                sp.dma_start(wk[:], dram["L1_xattn_Wk"]).then_inc(wk_in, 16)

            @block.scalar
            def _(act):
                norm.scalar(nc, act)
                for c in range(KC):
                    act.wait_ge(turned, c + 1)
                    nc.scalar.activation(xnT[:, c, :], banks[c][:], ACT.Copy).then_inc(turned_out, 1)
                for c in range(KC):
                    act.wait_ge(qk_mm, c + 1)
                    nc.scalar.activation(qk[:, c, :], banks[c][:], ACT.Copy, scale=D ** -0.5).then_inc(qk_out, 1)

            @block.vector
            def _(dve):
                norm.vector(nc, dve, x, xn)
                dve.wait_ge(bq_in, 16)
                for o in range(KC):
                    dve.wait_ge(q_mm, o + 1)
                    nc.vector.tensor_scalar(qT[:, o, :], banks[KC + o][:], bq[:, o:o + 1], None, ALU.add
                                            ).then_inc(q_out, 1)

            @block.tensor
            def _(pe):
                pe.wait_ge(norm.done, TC)
                for c in range(KC):
                    transpose_rows(nc, banks[c], xn, c, ident).then_inc(turned, 1)
                pe.wait_ge(turned_out, KC)
                pe.wait_ge(wq_in, 16)
                for o in range(KC):
                    product(nc, banks[KC + o][:], [(wq[:, k, o * P:(o + 1) * P], xnT[:, k, :]) for k in range(KC)]
                            ).then_inc(q_mm, 1)
                pe.wait_ge(q_out, KC)
                pe.wait_ge(wk_in, 16)
                for c in range(KC):
                    product(nc, banks[c][:], [(wk[:, k, c * P:(c + 1) * P], qT[:, k, :]) for k in range(KC)]
                            ).then_inc(qk_mm, 1)

        with ExitStack() as c3:
            s3 = Scope(nc, c3, "cta")
            ct = [s3.sb(f"ct{i}", [P, KC, KPAD]) for i in range(2)]
            cr = [s3.sb(f"cr{i}", [P, NCH, D]) for i in range(2)]
            qs = s3.sb("qs", [P, KC, P])
            prob = s3.sb("prob", [P, KEYS])
            pt = s3.sb("pt", [P, NCH, P])
            nmx, rsum, rinv = s3.sb("nmx", [P, 1]), s3.sb("rsum", [P, 1]), s3.sb("rinv", [P, 1])
            score = s3.ps("score", [P, 4 * GW])
            tb = [s3.ps(f"tb{i}", [P, GW]) for i in range(2)]
            ub = s3.ps("ub", [P, D])
            ct_in = [s3.sem(f"ct_in{i}") for i in range(2)]
            cr_in = [s3.sem(f"cr_in{i}") for i in range(2)]
            qs_ready, scored, max_ready, exp_done = (s3.sem(n) for n in ("qs_ready", "scored", "max_ready", "exp_done"))
            rinv_ready, turned, turned_out = s3.sem("rinv_ready"), s3.sem("turned"), s3.sem("turned_out")
            weighed, u_out = s3.sem("weighed"), s3.sem("u_out")
            NT = 4
            block = c3.enter_context(nc.Block())
            ctxT, ctxR, ctxL = dram["ctxT"], dram["ctxR"], dram["ctxL"]
            KL = CHUNKS[-1][1]

            @block.sync
            def _(sp):
                def load(t):
                    for i in range(2):
                        sp.dma_start(ct[i][:], ctxT[2 * t + i]).then_inc(ct_in[i], 16)
                    for i in range(2):
                        sp.dma_start(cr[i][:, 0:NCH - 1, :], ctxR[2 * t + i]).then_inc(cr_in[i], 16)
                        sp.dma_start(cr[i][0:KL, NCH - 1, :], ctxL[2 * t + i]).then_inc(cr_in[i], 16)

                load(0)
                with sp.Fori(0, TC - 1) as t:
                    for i in range(2):
                        sp.wait_ge(scored, 2 * t + i + 1)
                        sp.dma_start(ct[i][:], ctxT[2 * t + 2 + i]).then_inc(ct_in[i], 16)
                    for i in range(2):
                        sp.wait_ge(weighed, 2 * t + i + 1)
                        sp.dma_start(cr[i][:, 0:NCH - 1, :], ctxR[2 * t + 2 + i]).then_inc(cr_in[i], 16)
                        sp.dma_start(cr[i][0:KL, NCH - 1, :], ctxL[2 * t + 2 + i]).then_inc(cr_in[i], 16)

            @block.scalar
            def _(act):
                act.sem_inc(turned_out, 2)
                with act.Fori(0, TC) as t:
                    nc.scalar.activation(qs[:], qk[:, :, bass.ts(t, P)], ACT.Copy).then_inc(qs_ready, 1)
                    act.wait_ge(max_ready, t + 1)
                    nc.scalar.activation(prob[:], score[:, 0:KEYS], ACT.Exp, bias=nmx[:], accum_out=rsum[:]
                                         ).then_inc(exp_done, 1)
                    for i in range(NT):
                        act.wait_ge(turned, NT * t + i + 1)
                        if i < 3:
                            nc.scalar.activation(pt[:, 4 * i:4 * i + 4, :],
                                                 tb[i % 2][:].rearrange("p (c f) -> p c f", c=4), ACT.Copy
                                                 ).then_inc(turned_out, 1)
                        else:
                            nc.scalar.activation(pt[0:KL, NCH - 1, :], tb[i % 2][0:KL, 0:P], ACT.Copy
                                                 ).then_inc(turned_out, 1)
                    act.wait_ge(weighed, 2 * t + 2)

            @block.vector
            def _(dve):
                with dve.Fori(0, TC) as t:
                    dve.wait_ge(scored, 2 * t + 2)
                    nc.vector.reduce_max(nmx[:], score[:, 0:KEYS], AX.X, negate=True).then_inc(max_ready, 1)
                    dve.wait_ge(exp_done, t + 1)
                    nc.vector.reciprocal(rinv[:], rsum[:]).then_inc(rinv_ready, 1)
                    dve.wait_ge(rinv_ready, t + 1)
                    dve.wait_ge(weighed, 2 * t + 2)
                    nc.vector.tensor_scalar(u[:, bass.ds(t, 1), :], ub[:].unsqueeze(1), rinv[:], None, ALU.mult
                                            ).then_inc(u_out, 1)

            @block.tensor
            def _(pe):
                pe.sem_inc(u_out, 1)
                with pe.Fori(0, TC) as t:
                    pe.wait_ge(qs_ready, t + 1)
                    for i in range(2):
                        pe.wait_ge(ct_in[i], 16 * t + 16)
                        r = slice(i * LAT, (i + 1) * LAT)
                        for s, w in GROUPS:
                            last = product(nc, score[r, s:s + w], [(qs[:, k, r], ct[i][:, k, s:s + w])
                                                                   for k in range(KC)])
                        last.then_inc(scored, 1)
                    pe.wait_ge(exp_done, t + 1)
                    for i in range(NT):
                        pe.wait_ge(turned_out, NT * t + i + 1)
                        for c in range(4 * i, min(4 * i + 4, NCH)):
                            s, kk = CHUNKS[c]
                            last = nc.tensor.transpose(tb[i % 2][0:kk, (c - 4 * i) * P:(c - 4 * i + 1) * P],
                                                       prob[:, s:s + kk], ident[:])
                        last.then_inc(turned, 1)
                    pe.wait_ge(turned_out, NT * t + NT + 2)
                    pe.wait_ge(u_out, t + 1)
                    for i in range(2):
                        pe.wait_ge(cr_in[i], 32 * t + 32)
                        r = slice(i * LAT, (i + 1) * LAT)
                        product(nc, ub[r, :], [(pt[0:kk, c, r], cr[i][0:kk, c, :])
                                               for c, (s, kk) in enumerate(CHUNKS)]).then_inc(weighed, 1)

        with ExitStack() as c4:
            s4 = Scope(nc, c4, "cto")
            uT, vT = s4.sb("uT", [P, KC, T]), s4.sb("vT", [P, KC, T])
            wv, wo = s4.sb("wv", [P, KC, D]), s4.sb("wo", [P, KC, D])
            bv, bo = s4.sb("bv", [P, KC]), s4.sb("bo", [P, D])
            banks = [s4.ps(f"bank{i}", [P, T]) for i in range(8)]
            wv_in, wo_in, bv_in, bo_in = s4.sem("wv_in"), s4.sem("wo_in"), s4.sem("bv_in"), s4.sem("bo_in")
            turned, turned_out, v_mm, v_out = s4.sem("turned"), s4.sem("turned_out"), s4.sem("v_mm"), s4.sem("v_out")
            o_mm, biased, out = s4.sem("o_mm"), s4.sem("biased"), s4.sem("out")
            block = c4.enter_context(nc.Block())

            @block.sync
            def _(sp):
                sp.dma_start(wv[:], dram["L1_xattn_Wv"]).then_inc(wv_in, 16)
                sp.dma_start(bv[:], dram["L1_xattn_bv"]).then_inc(bv_in, 16)
                sp.dma_start(wo[:], dram["L1_xattn_Wo"]).then_inc(wo_in, 16)
                sp.dma_start(bo[:], dram["L1_xattn_bo"].partition_broadcast(P)).then_inc(bo_in, 16)

            @block.scalar
            def _(act):
                for c in range(KC):
                    act.wait_ge(turned, c + 1)
                    nc.scalar.activation(uT[:, c, :], banks[c][:], ACT.Copy).then_inc(turned_out, 1)
                act.wait_ge(bv_in, 16)
                for c in range(KC):
                    act.wait_ge(v_mm, c + 1)
                    nc.scalar.activation(vT[:, c, :], banks[KC + c][:], ACT.Identity, bias=bv[:, c:c + 1]
                                         ).then_inc(v_out, 1)

            @block.vector
            def _(dve):
                dve.wait_ge(bo_in, 16)
                for t in range(TC):
                    nc.vector.tensor_tensor(x[:, t, :], x[:, t, :], bo[:], ALU.add).then_inc(biased, 1)
                for t in range(TC):
                    dve.wait_ge(o_mm, t + 1)
                    dve.wait_ge(biased, t + 1)
                    nc.vector.tensor_tensor(x[:, t, :], x[:, t, :], banks[t][:], ALU.add).then_inc(out, 1)

            @block.tensor
            def _(pe):
                for c in range(KC):
                    transpose_rows(nc, banks[c], u, c, ident).then_inc(turned, 1)
                pe.wait_ge(turned_out, KC)
                pe.wait_ge(wv_in, 16)
                for o in range(KC):
                    product(nc, banks[KC + o][:], [(wv[:, k, o * P:(o + 1) * P], uT[:, k, :]) for k in range(KC)]
                            ).then_inc(v_mm, 1)
                pe.wait_ge(v_out, KC)
                pe.wait_ge(wo_in, 16)
                for t in range(TC):
                    product(nc, banks[t][:], [(vT[:, k, t * P:(t + 1) * P], wo[:, k, :]) for k in range(KC)]
                            ).then_inc(o_mm, 1)


def phase_latent(nc, dram, ident, x):
    with ExitStack() as ctx:
        sc = Scope(nc, ctx, "lat")
        xn = sc.sb("xn", [P, TC, D])
        xnT = sc.sb("xnT", [P, KC, T])
        wq, wl = sc.sb("wq", [P, KC, D]), sc.sb("wl", [P, KC, P])
        wk, wv, wo = sc.sb("wk", [P, D]), sc.sb("wv", [P, D]), sc.sb("wo", [P, KC, D])
        bq, bl, bk, bv = sc.sb("bq", [P, KC]), sc.sb("bl", [P, 1]), sc.sb("bk", [P, KC]), sc.sb("bv", [P, KC])
        bo = sc.sb("bo", [P, D])
        qT, kT, lT = sc.sb("qT", [P, KC, T]), sc.sb("kT", [P, KC, T]), sc.sb("lT", [P, T])
        v = sc.sb("v", [P, TC, D])
        q_blk = sc.sb("q_blk", [P, KC, 2, B, P])
        dif = sc.sb("dif", [P, PAIRS, B, LAT])
        prob = sc.sb("prob", [P, PAIRS, B, LAT])
        nmx, rs, ri = (sc.sb(n, [P, PAIRS, B]) for n in ("nmx", "rs", "ri"))
        pt = sc.sb("pt", [P, PAIRS, TC, P])
        oT = sc.sb("oT", [P, KC, T])
        norm = Norm(sc, "ln")
        banks = [sc.ps(f"bank{i}", [P, T]) for i in range(8)]
        w_in = {n: sc.sem(f"{n}_in") for n in ("wq", "wl", "wk", "wv", "wo", "bq", "bl", "bk", "bv", "bo")}
        zeroed, turned, turned_out = sc.sem("zeroed"), sc.sem("turned"), sc.sem("turned_out")
        q_mm, q_out, l_mm, l_out = sc.sem("q_mm"), sc.sem("q_out"), sc.sem("l_mm"), sc.sem("l_out")
        k_mm, k_out, v_mm, v_out = sc.sem("k_mm"), sc.sem("k_out"), sc.sem("v_mm"), sc.sem("v_out")
        blk_ready, scored, max_ready, dif_ready = (sc.sem(n) for n in ("blk_ready", "scored", "max_ready", "dif_ready"))
        exp_done, sum_ready, inv_ready, prob_ready = (sc.sem(n) for n in ("exp_done", "sum_ready", "inv_ready",
                                                                          "prob_ready"))
        p_turned, pt_out, weighed, o_out = (sc.sem(n) for n in ("p_turned", "pt_out", "weighed", "o_out"))
        biased, o_mm, out = sc.sem("biased"), sc.sem("o_mm"), sc.sem("out")
        block = ctx.enter_context(nc.Block())

        @block.sync
        def _(sp):
            tiles = dict(wq=wq, bq=bq, wl=wl, bl=bl, wk=wk, bk=bk, wv=wv, bv=bv, wo=wo)
            for n, tile in tiles.items():
                sp.dma_start(tile[:], dram[f"L1_attn_{n[0].upper() + n[1] if n[0] == 'w' else n}"]
                             ).then_inc(w_in[n], 16)
            sp.dma_start(bo[:], dram["L1_attn_bo"].partition_broadcast(P)).then_inc(w_in["bo"], 16)

        @block.gpsimd
        def _(pool):
            nc.gpsimd.memset(q_blk[:], 0.0).then_inc(zeroed, 1)

        @block.scalar
        def _(act):
            norm.scalar(nc, act)
            for c in range(KC):
                act.wait_ge(turned, c + 1)
                nc.scalar.activation(xnT[:, c, :], banks[c][:], ACT.Copy).then_inc(turned_out, 1)
            act.wait_ge(w_in["bl"], 16)
            act.wait_ge(l_mm, 1)
            nc.scalar.activation(lT[:], banks[4][:], ACT.Identity, bias=bl[:]).then_inc(l_out, 1)
            act.wait_ge(w_in["bk"], 16)
            for c in range(KC):
                act.wait_ge(k_mm, c + 1)
                nc.scalar.activation(kT[:, c, :], banks[c][:], ACT.Identity, bias=bk[:, c:c + 1]).then_inc(k_out, 1)
            for t in range(TC):
                act.wait_ge(v_mm, t + 1)
                nc.scalar.activation(v[:, t, :], banks[4 + t][:], ACT.Copy).then_inc(v_out, 1)
            for u in range(PAIRS):
                act.wait_ge(dif_ready, u + 1)
                nc.scalar.activation(prob[:, u], dif[:, u], ACT.Exp).then_inc(exp_done, 1)
            for u in range(PAIRS):
                act.wait_ge(p_turned, u + 1)
                nc.scalar.activation(pt[:, u], banks[u][:].rearrange("p (t f) -> p t f", t=TC), ACT.Copy
                                     ).then_inc(pt_out, 1)

        @block.vector
        def _(dve):
            norm.vector(nc, dve, x, xn)
            dve.wait_ge(w_in["bq"], 16)
            for c in range(KC):
                dve.wait_ge(q_mm, c + 1)
                nc.vector.tensor_scalar(qT[:, c, :], banks[(5 + c) % 8][:], bq[:, c:c + 1], HD ** -0.5, ALU.add,
                                        ALU.mult).then_inc(q_out, 1)
            dve.wait_ge(zeroed, 1)
            dve.wait_ge(q_out, KC)
            for h in range(HPC):
                r = slice(h * HD, (h + 1) * HD)
                for c in range(KC):
                    last = nc.vector.tensor_copy(q_blk[r, c, h // 2, :, (h % 2) * LAT:(h % 2 + 1) * LAT],
                                                 qT[r, c, :].rearrange("p (b n) -> p b n", b=B))
            last.then_inc(blk_ready, 1)
            for u in range(PAIRS):
                dve.wait_ge(scored, u + 1)
                s = banks[u][:].rearrange("p (b n) -> p b n", b=B)
                nc.vector.reduce_max(nmx[:, u], s, AX.X, negate=True).then_inc(max_ready, 1)
                dve.wait_ge(max_ready, u + 1)
                nc.vector.tensor_tensor(dif[:, u], s, nmx[:, u].unsqueeze(2).broadcast_to([P, B, LAT]), ALU.add
                                        ).then_inc(dif_ready, 1)
            for u in range(PAIRS):
                dve.wait_ge(exp_done, u + 1)
                nc.vector.reduce_sum(rs[:, u], prob[:, u], AX.X).then_inc(sum_ready, 1)
                dve.wait_ge(sum_ready, u + 1)
                nc.vector.reciprocal(ri[:, u], rs[:, u]).then_inc(inv_ready, 1)
                dve.wait_ge(inv_ready, u + 1)
                nc.vector.tensor_tensor(prob[:, u], prob[:, u], ri[:, u].unsqueeze(2).broadcast_to([P, B, LAT]),
                                        ALU.mult).then_inc(prob_ready, 1)
            dve.wait_ge(w_in["bv"], 16)
            for n in range(4 * KC):
                c, half, par = n // 4, (n // 2) % 2, n % 2
                dve.wait_ge(weighed, n + 1)
                s = banks[n % 8][:].rearrange("p (t h n) -> p t h n", t=2, h=HPC)
                o = oT[:, c, :].rearrange("p (t r n) -> p t r n", t=TC, r=2)
                for h in range(HPC):
                    r = slice(h * HD, (h + 1) * HD)
                    last = nc.vector.tensor_scalar(o[r, 2 * half:2 * half + 2, par, :], s[r, :, h, :],
                                                   bv[r, c:c + 1], None, ALU.add)
                last.then_inc(o_out, 1)
            dve.wait_ge(w_in["bo"], 16)
            for t in range(TC):
                nc.vector.tensor_tensor(x[:, t, :], x[:, t, :], bo[:], ALU.add).then_inc(biased, 1)
            for t in range(TC):
                dve.wait_ge(o_mm, t + 1)
                dve.wait_ge(biased, t + 1)
                nc.vector.tensor_tensor(x[:, t, :], x[:, t, :], banks[t][:], ALU.add).then_inc(out, 1)

        @block.tensor
        def _(pe):
            pe.wait_ge(norm.done, TC)
            for c in range(KC):
                transpose_rows(nc, banks[c], xn, c, ident).then_inc(turned, 1)
            pe.wait_ge(turned_out, KC)
            pe.wait_ge(w_in["wl"], 16)
            product(nc, banks[4][:], [(wl[:, k, :], xnT[:, k, :]) for k in range(KC)]).then_inc(l_mm, 1)
            pe.wait_ge(w_in["wq"], 16)
            for c in range(KC):
                product(nc, banks[(5 + c) % 8][:], [(wq[:, k, c * P:(c + 1) * P], xnT[:, k, :]) for k in range(KC)]
                        ).then_inc(q_mm, 1)
            pe.wait_ge(l_out, 1)
            pe.wait_ge(q_out, KC)
            pe.wait_ge(w_in["wk"], 16)
            for c in range(KC):
                product(nc, banks[c][:], [(wk[:, c * P:(c + 1) * P], lT[:])]).then_inc(k_mm, 1)
            pe.wait_ge(w_in["wv"], 16)
            for t in range(TC):
                product(nc, banks[4 + t][:], [(lT[:, t * P:(t + 1) * P], wv[:])]).then_inc(v_mm, 1)
            pe.wait_ge(blk_ready, 1)
            pe.wait_ge(k_out, KC)
            for u in range(PAIRS):
                if u == 4:
                    pe.wait_ge(v_out, TC)
                for b in range(B):
                    last = product(nc, banks[u][:, b * LAT:(b + 1) * LAT],
                                   [(q_blk[:, u // 2, u % 2, b, :], kT[:, u // 2, b * LAT:(b + 1) * LAT])])
                last.then_inc(scored, 1)
            for u in range(PAIRS):
                pe.wait_ge(exp_done, u + 1)
                pe.wait_ge(prob_ready, u + 1)
                for t in range(TC):
                    last = nc.tensor.transpose(banks[u][:, t * P:(t + 1) * P],
                                               prob[:, u, 2 * t:2 * t + 2, :].rearrange("p b n -> p (b n)"), ident[:])
                last.then_inc(p_turned, 1)
            pe.wait_ge(pt_out, PAIRS)
            for n in range(4 * KC):
                c, half, par = n // 4, (n // 2) % 2, n % 2
                if n >= 8:
                    pe.wait_ge(o_out, n - 7)
                r = slice(par * LAT, (par + 1) * LAT)
                for j in range(2):
                    t = 2 * half + j
                    last = product(nc, banks[n % 8][:, j * 2 * P:(j + 1) * 2 * P],
                                   [(v[r, t, c * P:(c + 1) * P], pt[r, 2 * c:2 * c + 2, t, :])])
                last.then_inc(weighed, 1)
            pe.wait_ge(o_out, 4 * KC)
            pe.wait_ge(w_in["wo"], 16)
            for t in range(TC):
                product(nc, banks[t][:], [(oT[:, c, t * P:(t + 1) * P], wo[:, c, :]) for c in range(KC)]
                        ).then_inc(o_mm, 1)


def phase_rows(nc, dram, ident, x, y1):
    NH, SC = KC, P ** -0.5
    with ExitStack() as ctx:
        sc = Scope(nc, ctx, "row")
        xn = sc.sb("xn", [P, TC, D])
        xnT = sc.sb("xnT", [P, KC, T])
        w, wo = sc.sb("w", [P, KC, 3 * D]), sc.sb("wo", [P, KC, D])
        bc = sc.sb("bc", [P, 3 * KC])
        bqs = sc.sb("bqs", [P, KC])
        bo, g, bb = sc.sb("bo", [P, D]), sc.sb("g", [P, D]), sc.sb("bb", [P, D])
        same = sc.sb("same", [P, LAT])
        qT, kT, v = sc.sb("qT", [P, NH, T]), sc.sb("kT", [P, NH, T]), sc.sb("v", [P, TC, D])
        cut = sc.sb("cut", [P, 2, T])
        N = NH * TC
        s8, d8, e8, p8 = (sc.sb(n, [P, N, B]) for n in ("s8", "d8", "e8", "p8"))
        nm8, sm8, iv8 = (sc.sb(n, [P, N]) for n in ("nm8", "sm8", "iv8"))
        full = sc.sb("full", [P, 2, TC, T])
        pt = sc.sb("pt", [P, 2, TC, T])
        oT = sc.sb("oT", [P, NH, T])
        r = sc.sb("r", [P, TC, D])
        rn = sc.sb("rn", [P, TC, D])
        norm, norm1 = Norm(sc, "ln"), Norm(sc, "ln1")
        banks = [sc.ps(f"bank{i}", [P, T]) for i in range(8)]
        w_in, bc_in, wo_in, same_in = sc.sem("w_in"), sc.sem("bc_in"), sc.sem("wo_in"), sc.sem("same_in")
        bo_in, g_in, bb_in = sc.sem("bo_in"), sc.sem("g_in"), sc.sem("bb_in")
        turned, turned_out = sc.sem("turned"), sc.sem("turned_out")
        bqs_ready, mm, q_out, k_out, v_out = (sc.sem(n) for n in ("bqs_ready", "mm", "q_out", "k_out", "v_out"))
        scored, cut_ready, picked, step = (sc.sem(n) for n in ("scored", "cut_ready", "picked", "step"))
        d_ready, e_ready, spread, p_turned, pt_out = (sc.sem(n) for n in ("d_ready", "e_ready", "spread", "p_turned",
                                                                          "pt_out"))
        weighed, o_out, biased, o_mm, r_ready = (sc.sem(n) for n in ("weighed", "o_out", "biased", "o_mm", "r_ready"))
        geared = sc.sem("geared")
        block = ctx.enter_context(nc.Block())
        by_batch = lambda a: a.rearrange("p (b n) -> p b n", b=B)
        same_all = same[:].unsqueeze(1).broadcast_to([P, B, LAT])

        @block.sync
        def _(sp):
            sp.dma_start(bc[:], dram["L1_ffn_in_proj_b"]).then_inc(bc_in, 16)
            sp.dma_start(same[:], dram["same_latent"]).then_inc(same_in, 16)
            sp.dma_start(w[:], dram["L1_ffn_in_proj_w"]).then_inc(w_in, 16)
            sp.dma_start(wo[:], dram["L1_ffn_out_proj_w"]).then_inc(wo_in, 16)
            sp.dma_start(bo[:], dram["L1_ffn_out_proj_b"].partition_broadcast(P)).then_inc(bo_in, 16)
            sp.dma_start(g[:], dram["L1_ffn_ln1_g"].partition_broadcast(P)).then_inc(g_in, 16)
            sp.dma_start(bb[:], dram["L1_ffn_ln1_b"].partition_broadcast(P)).then_inc(bb_in, 16)

        @block.scalar
        def _(act):
            norm.scalar(nc, act)
            for c in range(KC):
                act.wait_ge(turned, c + 1)
                nc.scalar.activation(xnT[:, c, :], banks[c][:], ACT.Copy).then_inc(turned_out, 1)
            act.wait_ge(bc_in, 16)
            for h in range(NH):
                act.wait_ge(mm, h + 1)
                nc.scalar.activation(kT[:, h, :], banks[4 + h][:], ACT.Identity, bias=bc[:, KC + h:KC + h + 1]
                                     ).then_inc(k_out, 1)
            for t in range(TC):
                act.wait_ge(mm, 2 * NH + t + 1)
                nc.scalar.activation(v[:, t, :], banks[4 + t][:], ACT.Copy).then_inc(v_out, 1)
            act.wait_ge(d_ready, 1)
            nc.scalar.activation(e8[:], d8[:], ACT.Exp).then_inc(e_ready, 1)
            for h in range(NH):
                if h >= 2:
                    act.wait_ge(weighed, h - 1)
                for k in range(TC):
                    act.wait_ge(p_turned, TC * h + k + 1)
                    nc.scalar.activation(pt[:, h % 2, k, :], banks[k][:], ACT.Copy).then_inc(pt_out, 1)
                act.wait_ge(weighed, h + 1)
                nc.scalar.activation(oT[:, h, :], banks[4 + h % 2][:], ACT.Identity,
                                     bias=bc[:, 2 * KC + h:2 * KC + h + 1]).then_inc(o_out, 1)
            norm1.scalar(nc, act)

        @block.vector
        def _(dve):
            norm.vector(nc, dve, x, xn)
            dve.wait_ge(bc_in, 16)
            for h in range(NH):
                dve.wait_ge(mm, NH + h + 1)
                nc.vector.tensor_scalar(qT[:, h, :], banks[h][:], bc[:, h:h + 1], SC, ALU.add, ALU.mult
                                        ).then_inc(q_out, 1)
            dve.wait_ge(same_in, 16)
            for n in range(N):
                dve.wait_ge(scored, n + 1)
                nc.vector.tensor_tensor(by_batch(cut[:, n % 2, :]), by_batch(banks[n % 4][:]), same_all, ALU.mult
                                        ).then_inc(cut_ready, 1)
                dve.wait_ge(cut_ready, n + 1)
                nc.vector.reduce_sum(s8[:, n, :], by_batch(cut[:, n % 2, :]), AX.X).then_inc(picked, 1)
            dve.wait_ge(picked, N)
            wide = lambda a: a[:].unsqueeze(2).broadcast_to([P, N, B])
            nc.vector.reduce_max(nm8[:], s8[:], AX.X, negate=True).then_inc(step, 1)
            dve.wait_ge(step, 1)
            nc.vector.tensor_tensor(d8[:], s8[:], wide(nm8), ALU.add).then_inc(d_ready, 1)
            dve.wait_ge(e_ready, 1)
            nc.vector.reduce_sum(sm8[:], e8[:], AX.X).then_inc(step, 1)
            dve.wait_ge(step, 2)
            nc.vector.reciprocal(iv8[:], sm8[:]).then_inc(step, 1)
            dve.wait_ge(step, 3)
            nc.vector.tensor_tensor(p8[:], e8[:], wide(iv8), ALU.mult).then_inc(step, 1)
            dve.wait_ge(step, 4)
            for h in range(NH):
                if h >= 2:
                    dve.wait_ge(p_turned, TC * (h - 1))
                for t in range(TC):
                    nc.vector.tensor_tensor(by_batch(full[:, h % 2, t, :]),
                                            p8[:, h * TC + t, :].unsqueeze(2).broadcast_to([P, B, LAT]), same_all,
                                            ALU.mult).then_inc(spread, 1)
            dve.wait_ge(bo_in, 16)
            for t in range(TC):
                nc.vector.tensor_tensor(xn[:, t, :], xn[:, t, :], bo[:], ALU.add).then_inc(biased, 1)
            for t in range(TC):
                dve.wait_ge(o_mm, t + 1)
                dve.wait_ge(biased, t + 1)
                nc.vector.tensor_tensor(r[:, t, :], xn[:, t, :], banks[t][:], ALU.add).then_inc(r_ready, 1)
            dve.wait_ge(r_ready, TC)
            norm1.vector(nc, dve, r, rn)
            dve.wait_ge(norm1.done, TC)
            dve.wait_ge(g_in, 16)
            dve.wait_ge(bb_in, 16)
            for t in range(TC):
                nc.vector.tensor_tensor(rn[:, t, :], rn[:, t, :], g[:], ALU.mult).then_inc(geared, 1)
            for t in range(TC):
                dve.wait_ge(geared, t + 1)
                nc.vector.tensor_tensor(y1[:, t, :], rn[:, t, :], bb[:], ALU.add)

        @block.tensor
        def _(pe):
            pe.wait_ge(norm.done, TC)
            for c in range(KC):
                transpose_rows(nc, banks[c], xn, c, ident).then_inc(turned, 1)
            pe.wait_ge(turned_out, KC)
            pe.wait_ge(w_in, 16)
            for h in range(NH):
                o = D + h * P
                product(nc, banks[4 + h][:], [(w[:, k, o:o + P], xnT[:, k, :]) for k in range(KC)]).then_inc(mm, 1)
            for h in range(NH):
                o = h * P
                product(nc, banks[h][:], [(w[:, k, o:o + P], xnT[:, k, :]) for k in range(KC)]).then_inc(mm, 1)
            pe.wait_ge(k_out, NH)
            for t in range(TC):
                product(nc, banks[4 + t][:], [(xnT[:, k, t * P:(t + 1) * P], w[:, k, 2 * D:3 * D]) for k in range(KC)]
                        ).then_inc(mm, 1)
            pe.wait_ge(q_out, NH)
            for n in range(N):
                h, t = n // TC, n % TC
                if n >= 4:
                    pe.wait_ge(cut_ready, n - 3)
                product(nc, banks[n % 4][:], [(qT[:, h, t * P:(t + 1) * P], kT[:, h, :])]).then_inc(scored, 1)
            pe.wait_ge(v_out, TC)
            pe.wait_ge(cut_ready, N)
            for h in range(NH):
                pe.wait_ge(spread, TC * (h + 1))
                for k in range(TC):
                    if h:
                        pe.wait_ge(pt_out, TC * (h - 1) + k + 1)
                    for t in range(TC):
                        last = nc.tensor.transpose(banks[k][:, t * P:(t + 1) * P],
                                                   full[:, h % 2, t, k * P:(k + 1) * P], ident[:])
                    last.then_inc(p_turned, 1)
                pe.wait_ge(pt_out, TC * (h + 1))
                if h >= 2:
                    pe.wait_ge(o_out, h - 1)
                product(nc, banks[4 + h % 2][:], [(v[:, k, h * P:(h + 1) * P], pt[:, h % 2, k, :])
                                                  for k in range(TC)]).then_inc(weighed, 1)
            pe.wait_ge(o_out, NH)
            pe.wait_ge(wo_in, 16)
            for t in range(TC):
                product(nc, banks[t][:], [(oT[:, h, t * P:(t + 1) * P], wo[:, h, :]) for h in range(NH)]
                        ).then_inc(o_mm, 1)


def phase_dispatch(nc, dram, ident, x, y1):
    with ExitStack() as ctx:
        sc = Scope(nc, ctx, "dsp")
        w1 = [sc.sb(f"w1_{i}", [P, KC, FF]) for i in range(2)]
        w2 = [sc.sb(f"w2_{i}", [P, FC, D]) for i in range(2)]
        b1 = sc.sb("b1", [P, E0, FC])
        b2 = sc.sb("b2", [P, E0 // 2, D])
        dT = sc.sb("dT", [P, KC, T])
        hot = sc.sb("hot", [P, TC, T])
        hotT = sc.sb("hotT", [P, TC, T])
        gate = sc.sb("gate", [P, TC])
        w1_in = [sc.sem(f"w1_in{i}") for i in range(2)]
        w2_in = [sc.sem(f"w2_in{i}") for i in range(2)]
        b1_in, b2_in = sc.sem("b1_in"), sc.sem("b2_in")
        W1, W2 = dram["L1_ffn_w1"], dram["L1_ffn_w2"]
        with ExitStack() as c1:
            s1 = Scope(nc, c1, "dsr")
            wg = s1.sb("wg", [P, KC, E0])
            before, ones = s1.sb("before", [P, P]), s1.sb("ones", [P, P])
            slots = s1.sb("slots", [P, T])
            first = s1.sb("first", [P, TC, E0])
            cnt, cm, at = (s1.sb(n, [P, TC, E0]) for n in ("cnt", "cm", "at"))
            loc, pos, over, slot = (s1.sb(n, [P, TC]) for n in ("loc", "pos", "over", "slot"))
            rt = Route(s1, dram)
            banks = [s1.ps(f"bank{i}", [P, T]) for i in range(8)]
            c_in, ones_ready = s1.sem("c_in"), s1.sem("ones_ready")
            turned, turned_out, routed, counted = (s1.sem(n) for n in ("turned", "turned_out", "routed", "counted"))
            step, hot_ready, moved, moved_out = (s1.sem(n) for n in ("step", "hot_ready", "moved", "moved_out"))
            hot_turned, hot_out = s1.sem("hot_turned"), s1.sem("hot_out")
            block = c1.enter_context(nc.Block())

            @block.sync
            def _(sp):
                sp.dma_start(wg[:], dram["L1_ffn_wg"]).then_inc(c_in, 16)
                rt.sync(sp)
                sp.dma_start(before[:], dram["before"]).then_inc(c_in, 16)
                sp.dma_start(slots[:], dram["slots"].partition_broadcast(P)).then_inc(c_in, 16)
                sp.dma_start(first[:], dram["first_slot"].partition_broadcast(P)).then_inc(c_in, 16)
                for i in range(2):
                    sp.dma_start(w1[i][:], W1[i]).then_inc(w1_in[i], 16)
                    sp.dma_start(w2[i][:], W2[i]).then_inc(w2_in[i], 16)
                sp.dma_start(b1[:], dram["L1_ffn_b1"]).then_inc(b1_in, 16)
                for i in range(2):
                    sp.dma_start(b2[i * CAP:(i + 1) * CAP],
                                 dram["L1_ffn_b2"].rearrange("(j r) d -> r j d", r=2)[i].partition_broadcast(CAP)
                                 ).then_inc(b2_in, 16)

            @block.gpsimd
            def _(pool):
                nc.gpsimd.memset(ones[:], 1.0).then_inc(ones_ready, 1)

            @block.scalar
            def _(act):
                for c in range(KC):
                    act.wait_ge(turned, c + 1)
                    nc.scalar.activation(dT[:, c, :], banks[c][:], ACT.Copy).then_inc(turned_out, 1)
                rt.scalar(nc, act)
                for c in range(TC):
                    act.wait_ge(hot_turned, c + 1)
                    nc.scalar.activation(hotT[:, c, :], banks[c][:], ACT.Copy).then_inc(hot_out, 1)

            @block.vector
            def _(dve):
                dve.wait_ge(routed, 1)
                rt.vector(nc, dve, banks[4][:, 0:TC * E0].rearrange("p (t e) -> p t e", t=TC))
                n = [0]

                def step_(ins):
                    n[0] += 1
                    ins.then_inc(step, 1)
                    dve.wait_ge(step, n[0])

                dve.wait_ge(c_in, 64)
                dve.wait_ge(counted, 1)
                step_(nc.vector.tensor_copy(cnt[:], banks[5][:, 0:TC * E0].rearrange("p (t e) -> p t e", t=TC)))
                step_(nc.vector.tensor_tensor(cm[:], cnt[:], rt.mask[:], ALU.mult))
                step_(nc.vector.reduce_sum(loc[:], cm[:], AX.X))
                step_(nc.vector.tensor_tensor(at[:], first[:], rt.mask[:], ALU.mult))
                step_(nc.vector.reduce_sum(pos[:], at[:], AX.X))
                step_(nc.vector.tensor_scalar(over[:], loc[:], float(CAP), float(4 * T), ALU.is_ge, ALU.mult))
                step_(nc.vector.tensor_tensor(pos[:], pos[:], loc[:], ALU.add))
                step_(nc.vector.tensor_tensor(slot[:], pos[:], over[:], ALU.add))
                step_(nc.vector.tensor_copy(gate[:], rt.gate[:]))
                for t in range(TC):
                    nc.vector.tensor_scalar(hot[:, t, :], slots[:], slot[:, t:t + 1], None, ALU.is_equal
                                            ).then_inc(hot_ready, 1)
                for c in range(KC):
                    dve.wait_ge(moved, c + 1)
                    nc.vector.tensor_copy(dT[:, c, :], banks[4 + c][:]).then_inc(moved_out, 1)

            @block.tensor
            def _(pe):
                for c in range(KC):
                    transpose_rows(nc, banks[c], y1, c, ident).then_inc(turned, 1)
                pe.wait_ge(turned_out, KC)
                pe.wait_ge(c_in, 64)
                for t in range(TC):
                    last = product(nc, banks[4][:, t * E0:(t + 1) * E0],
                                   [(dT[:, k, t * P:(t + 1) * P], wg[:, k, :]) for k in range(KC)])
                last.then_inc(routed, 1)
                pe.wait_ge(rt.done, 1)
                pe.wait_ge(ones_ready, 1)
                for t in range(TC):
                    last = product(nc, banks[5][:, t * E0:(t + 1) * E0],
                                   [(ones[:], rt.mask[:, s, :]) for s in range(t)] + [(before[:], rt.mask[:, t, :])])
                last.then_inc(counted, 1)
                pe.wait_ge(hot_ready, TC)
                for c in range(KC):
                    product(nc, banks[4 + c][:], [(y1[:, t, c * P:(c + 1) * P], hot[:, t, :]) for t in range(TC)]
                            ).then_inc(moved, 1)
                for c in range(TC):
                    transpose_rows(nc, banks[c], hot, c, ident).then_inc(hot_turned, 1)

        with ExitStack() as c2:
            s2 = Scope(nc, c2, "dse")
            hT = [s2.sb(f"hT{i}", [P, FC, CAP]) for i in range(2)]
            ys = s2.sb("ys", [P, E0 // 2, D])
            mixed, rn = w1[0][:, 0, :].rearrange("p (t d) -> p t d", t=TC), w1[0][:, 1, :].rearrange("p (t d) -> p t d", t=TC)
            g, bb = s2.sb("g", [P, D]), s2.sb("bb", [P, D])
            norm2 = Norm(s2, "ln2")
            g_in, bb_in, back, r_ready, geared, out = (s2.sem(n) for n in ("g_in", "bb_in", "back", "r_ready",
                                                                           "geared", "out"))
            hb = [s2.ps(f"hb{i}", [P, 512]) for i in range(4)]
            yb = [s2.ps(f"yb{i}", [P, D]) for i in range(2)]
            h_mm, h_out, y_mm, y_out = s2.sem("h_mm"), s2.sem("h_out"), s2.sem("y_mm"), s2.sem("y_out")
            FB = 8
            block = c2.enter_context(nc.Block())

            @block.sync
            def _(sp):
                sp.dma_start(g[:], dram["L1_ffn_ln2_g"].partition_broadcast(P)).then_inc(g_in, 16)
                sp.dma_start(bb[:], dram["L1_ffn_ln2_b"].partition_broadcast(P)).then_inc(bb_in, 16)
                with sp.Fori(0, E0 // 2 - 1) as j:
                    for i in range(2):
                        sp.wait_ge(h_mm, 4 * j + 2 * i + 2)
                        sp.dma_start(w1[i][:], W1[2 * j + 2 + i]).then_inc(w1_in[i], 16)
                        sp.wait_ge(y_mm, 2 * j + i + 1)
                        sp.dma_start(w2[i][:], W2[2 * j + 2 + i]).then_inc(w2_in[i], 16)

            @block.vector
            def _(dve):
                dve.sem_inc(h_out, 4)
                dve.sem_inc(y_out, 2)
                dve.wait_ge(b1_in, 16)
                dve.wait_ge(b2_in, 32)
                with dve.Fori(0, E0 // 2) as j:
                    for i in range(2):
                        for f in range(2):
                            dve.wait_ge(h_mm, 4 * j + 2 * i + f + 1)
                            fs = slice(f * FB, (f + 1) * FB)
                            nc.vector.tensor_tensor(
                                hT[i][:, fs, :], hb[2 * i + f][:].rearrange("p (f c) -> p f c", f=FB),
                                b1[:, bass.ds(2 * j + i, 1), fs].rearrange("p o f -> p (o f)").unsqueeze(2)
                                .broadcast_to([P, FB, CAP]), ALU.add).then_inc(h_out, 1)
                        dve.wait_ge(y_mm, 2 * j + i + 1)
                        r = slice(i * CAP, (i + 1) * CAP)
                        nc.vector.tensor_tensor(ys[r, bass.ds(j, 1), :], yb[i][r, :].unsqueeze(1),
                                                b2[r, bass.ds(j, 1), :], ALU.add).then_inc(y_out, 1)
                for t in range(TC):
                    dve.wait_ge(back, t + 1)
                    nc.vector.scalar_tensor_tensor(mixed[:, t, :], hb[t][:], gate[:, t:t + 1], y1[:, t, :],
                                                   ALU.mult, ALU.add).then_inc(r_ready, 1)
                dve.wait_ge(r_ready, TC)
                norm2.vector(nc, dve, mixed, rn)
                dve.wait_ge(norm2.done, TC)
                dve.wait_ge(g_in, 16)
                dve.wait_ge(bb_in, 16)
                for t in range(TC):
                    nc.vector.tensor_tensor(rn[:, t, :], rn[:, t, :], g[:], ALU.mult).then_inc(geared, 1)
                for t in range(TC):
                    dve.wait_ge(geared, t + 1)
                    nc.vector.tensor_tensor(rn[:, t, :], rn[:, t, :], bb[:], ALU.add).then_inc(geared, 1)
                for t in range(TC):
                    dve.wait_ge(geared, TC + t + 1)
                    nc.vector.tensor_tensor(x[:, t, :], x[:, t, :], rn[:, t, :], ALU.add).then_inc(out, 1)

            @block.scalar
            def _(act):
                norm2.scalar(nc, act)

            @block.tensor
            def _(pe):
                with pe.Fori(0, E0 // 2) as j:
                    for i in range(2):
                        pe.wait_ge(w1_in[i], 16 * j + 16)
                        for f in range(2):
                            pe.wait_ge(h_out, 4 * j + 2 * i + f + 1)
                            for q in range(FB):
                                o = (f * FB + q) * P
                                last = product(nc, hb[2 * i + f][:, q * CAP:(q + 1) * CAP],
                                               [(w1[i][:, k, o:o + P],
                                                 dT[:, k, bass.ds((2 * j + i) * CAP, CAP)]) for k in range(KC)])
                            last.then_inc(h_mm, 1)
                        pe.wait_ge(w2_in[i], 16 * j + 16)
                        pe.wait_ge(h_out, 4 * j + 2 * i + 6)
                        pe.wait_ge(y_out, 2 * j + i + 1)
                        product(nc, yb[i][i * CAP:(i + 1) * CAP, :],
                                [(hT[i][:, f, :], w2[i][:, f, :]) for f in range(FC)]).then_inc(y_mm, 1)
                pe.wait_ge(y_out, E0 + 2)
                for t in range(TC):
                    product(nc, hb[t][:], [(hotT[:, c, t * P:(t + 1) * P], ys[:, c, :]) for c in range(TC)]
                            ).then_inc(back, 1)


def phase_block(nc, dram, ident, x):
    with ExitStack() as ctx:
        y1 = ctx.enter_context(nc.sbuf_tensor("y1", [P, TC, D], F32))
        phase_rows(nc, dram, ident, x, y1)
        phase_dispatch(nc, dram, ident, x, y1)


def rest(nc, dram, ident, x):
    for phase in (phase_scan, phase_experts, phase_context, phase_latent, phase_block):
        phase(nc, dram, ident, x)


def lay_rest(n, put, rows, cols):
    import numpy as np
    ctx = n["ctx_1024"]
    put["ctxR"] = ctx[:, :P * (NCH - 1)].reshape(B, NCH - 1, P, D).transpose(0, 2, 1, 3)
    put["ctxL"] = ctx[:, P * (NCH - 1):]
    put["rank"] = np.tile(np.arange(E0, 0, -1, dtype=np.float32), (TC, 1))
    put["L0_attn_W_qkva"] = rows(n["L0_attn_W_qkva"].T)
    put["L0_attn_gamma"] = cols(n["L0_attn_gamma"])
    put["L0_ffn_router_w"] = rows(n["L0_ffn_router_w"])
    put["L0_ffn_router_b"] = n["L0_ffn_router_b"]
    put["L0_ffn_expert_b"] = n["L0_ffn_expert_b"]
    put["L0_ffn_expert_w"] = n["L0_ffn_expert_w"].reshape(E0, KC, P, D).transpose(0, 2, 1, 3)
    put["L1_xattn_Wq"] = rows(n["L1_xattn_Wq"].T)
    put["L1_xattn_Wk"] = rows(n["L1_xattn_Wk"])
    put["L1_xattn_Wv"] = rows(n["L1_xattn_Wv"].T)
    put["L1_xattn_Wo"] = rows(n["L1_xattn_Wo"].T)
    put["L1_xattn_bq"] = cols(n["L1_xattn_bq"])
    put["L1_xattn_bv"] = cols(n["L1_xattn_bv"])
    put["L1_xattn_bo"] = n["L1_xattn_bo"]
    put["L1_attn_Wq"] = rows(n["L1_attn_Wq"])
    put["L1_attn_Wl"] = rows(n["L1_attn_Wl"])
    put["L1_attn_Wk"] = n["L1_attn_Wk"]
    put["L1_attn_Wv"] = n["L1_attn_Wv"]
    put["L1_attn_Wo"] = rows(n["L1_attn_Wo"])
    for k in ("bq", "bl", "bk", "bv"):
        put[f"L1_attn_{k}"] = cols(n[f"L1_attn_{k}"])
    put["L1_attn_bo"] = n["L1_attn_bo"]
    put["L1_ffn_in_proj_w"] = rows(n["L1_ffn_in_proj_w"].T)
    put["L1_ffn_in_proj_b"] = cols(n["L1_ffn_in_proj_b"])
    put["L1_ffn_in_proj_bv"] = n["L1_ffn_in_proj_b"][2 * D:]
    put["L1_ffn_out_proj_w"] = rows(n["L1_ffn_out_proj_w"].T)
    for k in ("out_proj_b", "ln1_g", "ln1_b", "ln2_g", "ln2_b"):
        put[f"L1_ffn_{k}"] = n[f"L1_ffn_{k}"]
    put["L1_ffn_wg"] = rows(n["L1_ffn_wg"])
    put["L1_ffn_w1"] = n["L1_ffn_w1"].reshape(E0, KC, P, FF).transpose(0, 2, 1, 3)
    put["L1_ffn_w2"] = n["L1_ffn_w2"].reshape(E0, FC, P, D).transpose(0, 2, 1, 3)
    put["L1_ffn_b1"] = n["L1_ffn_b1"].reshape(E0, FC, P).transpose(2, 0, 1)
    put["L1_ffn_b2"] = n["L1_ffn_b2"]
    at = np.arange(T)
    put["same_latent"] = (np.arange(LAT)[None, :] == (np.arange(P) % LAT)[:, None]).astype(np.float32)
    put["before"] = (np.arange(P)[:, None] < np.arange(P)[None, :]).astype(np.float32)
    put["slots"] = at.astype(np.float32)
    put["first_slot"] = np.tile(np.arange(0, T, CAP, dtype=np.float32), (TC, 1))


def store_rows(nc, dst, rows):
    with ExitStack() as ctx:
        sc = Scope(nc, ctx, "sto")
        stored = sc.sem("stored")
        block = ctx.enter_context(nc.Block())

        @block.sync
        def _(sp):
            sp.dma_start(dst.rearrange("(t p) d -> p t d", p=P), rows[:]).then_inc(stored, 16)
            sp.wait_ge(stored, 16)


def build(nc, dram, out):
    with ExitStack() as whole:
        keep = Scope(nc, whole, "all")
        ident = keep.sb("ident", [P, P])
        x = keep.sb("x", [P, TC, D])
        with ExitStack() as ctx:
            sc = Scope(nc, ctx, "a")
            res = {"ident": ident, "oT": sc.sb("oT", [P, KC, T])}
            with ExitStack() as attn:
                at = Scope(nc, attn, "x")
                res["qT"] = at.sb("qT", [P, KC, T])
                res["w_hi"] = at.sb("w_hi", [P, 2, KC, D], F32R)
                res["w_lo"] = at.sb("w_lo", [P, 2, KC, D], F32R)
                res["q_blk_hi"] = at.sb("q_blk_hi", [P, KC, 2, P], F32R)
                res["q_blk_lo"] = at.sb("q_blk_lo", [P, KC, 2, P], F32R)
                res["bk"] = at.sb("bk", [P, KC])
                phase_queries(nc, dram, res)
                phase_cross(nc, dram, res)
            res["x"] = x
            phase_cross_out(nc, dram, res)
        rest(nc, dram, ident, x)
        store_rows(nc, out, x)


def kernel(**inputs):
    import numpy as np
    import concourse.bacc as bacc
    from concourse.bass_utils import run_bass_kernel_spmd

    arrays = {}

    def rows(w):
        k, n = w.shape
        return w.reshape(k // P, P, n).transpose(1, 0, 2)

    def cols(v):
        return v.reshape(-1, P).T

    n = {k: np.asarray(v) for k, v in inputs.items()}
    put = dict(x=n["x"].reshape(T, D))
    ctxT = np.zeros((B, P, KC, KPAD), n["ctx_1024"].dtype)
    ctxT[..., :KEYS] = n["ctx_1024"].transpose(0, 2, 1).reshape(B, KC, P, KEYS).transpose(0, 2, 1, 3)
    put["ctxT"] = ctxT
    for k in ("L0_xattn_Wq", "L0_xattn_Wk", "L0_xattn_Wv", "L0_xattn_Wo"):
        put[k] = rows(n[k].T)
    for k in ("L0_xattn_bq", "L0_xattn_bk", "L0_xattn_bv"):
        put[k] = cols(n[k])
    put["L0_xattn_bo"] = n["L0_xattn_bo"]
    lay_rest(n, put, rows, cols)

    nc = bacc.Bacc("TRN2", target_bir_lowering=False, num_devices=1)
    dram = {}
    for name, a in put.items():
        a = np.ascontiguousarray(a)
        arrays[f"in_{name}"] = a
        dram[name] = nc.dram_tensor(f"in_{name}", a.shape, mybir.dt.from_np(a.dtype), kind="ExternalInput").ap()
    out = nc.dram_tensor("out_0", (T, D), F32, kind="ExternalOutput").ap()
    build(nc, dram, out)
    r = run_bass_kernel_spmd(nc, [arrays], core_ids=[0])
    return r.results[0]["out_0"].reshape(B, LAT, D)
```

```python
from contextlib import ExitStack

import concourse.bass as bass
from concourse import mybir

F32 = mybir.dt.float32
F32R = mybir.dt.float32r
I32 = mybir.dt.int32
ALU = mybir.AluOpType
ACT = mybir.ActivationFunctionType
AX = mybir.AxisListType

P = 128
D = 512
KC = D // P
B = 8
LAT = 64
T = B * LAT
TC = T // P
KEYS = 1601
KPAD = KEYS + 1
BANK = 512
GROUPS_N = -(-KPAD // BANK)
GW = KPAD // GROUPS_N // 2 * 2
GROUPS = [(g * GW, GW if g + 1 < GROUPS_N else KPAD - g * GW) for g in range(GROUPS_N)]
SW = GROUPS[-1][1]
CHUNKS = [(s, min(P, KEYS - s)) for s in range(0, KEYS, P)]
NCH = len(CHUNKS)
HEADS = 16
HD = D // HEADS
HPC = P // HD
PAIRS = HEADS // 2
E0 = 8
CAP = T // E0
FF = 2048
FC = FF // P
EPS = 1e-5


class Scope:

    def __init__(self, nc, ctx, name):
        self.nc, self.ctx, self.name = nc, ctx, name
        self.sems = []
        ctx.callback(self.close)

    def close(self):
        if self.sems:
            self.nc.clear_and_free_semaphores(self.sems)
            self.nc.all_engine_barrier()

    def sb(self, name, shape, dt=F32):
        return self.ctx.enter_context(self.nc.sbuf_tensor(f"{self.name}_{name}", shape, dt))

    def ps(self, name, shape, dt=F32):
        return self.ctx.enter_context(self.nc.psum_tensor(f"{self.name}_{name}", shape, dt))

    def sem(self, name):
        self.sems.append(self.nc.alloc_semaphore(name=f"{self.name}_{name}"))
        return self.sems[-1]


class Norm:

    def __init__(self, sc, tag):
        self.stats = sc.sb(f"{tag}_stats", [P, TC, 6])
        self.mv = sc.sb(f"{tag}_mv", [P, TC, 2])
        self.std = sc.sb(f"{tag}_std", [P, TC])
        self.rstd = sc.sb(f"{tag}_rstd", [P, TC])
        self.stats_ready = sc.sem(f"{tag}_stats_ready")
        self.var_ready = sc.sem(f"{tag}_var_ready")
        self.std_ready = sc.sem(f"{tag}_std_ready")
        self.rstd_ready = sc.sem(f"{tag}_rstd_ready")
        self.done = sc.sem(f"{tag}_done")

    def vector(self, nc, dve, x, xn):
        for t in range(TC):
            nc.vector.bn_stats(self.stats[:, t, :], x[:, t, :]).then_inc(self.stats_ready, 1)
        dve.wait_ge(self.stats_ready, TC)
        for t in range(TC):
            nc.vector.bn_aggr(self.mv[:, t, :], self.stats[:, t, :]).then_inc(self.stats_ready, 1)
        dve.wait_ge(self.stats_ready, 2 * TC)
        nc.vector.tensor_scalar(self.std[:], self.mv[:, :, 1], EPS, None, ALU.add).then_inc(self.var_ready, 1)
        dve.wait_ge(self.std_ready, 1)
        nc.vector.reciprocal(self.rstd[:], self.std[:]).then_inc(self.rstd_ready, 1)
        dve.wait_ge(self.rstd_ready, 1)
        for t in range(TC):
            nc.vector.tensor_scalar(xn[:, t, :], x[:, t, :], self.mv[:, t, 0:1], self.rstd[:, t:t + 1],
                                    ALU.subtract, ALU.mult).then_inc(self.done, 1)

    def scalar(self, nc, act):
        act.wait_ge(self.var_ready, 1)
        nc.scalar.activation(self.std[:], self.std[:], ACT.Sqrt).then_inc(self.std_ready, 1)


def transpose_rows(nc, out_bank, rows, c, ident):
    for t in range(TC):
        last = nc.tensor.transpose(out_bank[:, t * P:(t + 1) * P], rows[:, t, c * P:(c + 1) * P], ident[:])
    return last


def product(nc, out, pairs):
    for n, (lhsT, rhs) in enumerate(pairs):
        last = nc.tensor.matmul(out, lhsT, rhs, start=(n == 0), stop=(n == len(pairs) - 1))
    return last


def product3(nc, out, parts):
    n, N = 0, 3 * len(parts)
    for (ah, al), (bh, bl) in parts:
        for a, b in ((ah, bh), (ah, bl), (al, bh)):
            last = nc.tensor.matmul(out, a, b, start=(n == 0), stop=(n == N - 1))
            n += 1
    return last


def phase_queries(nc, dram, res):
    with ExitStack() as ctx:
        sc = Scope(nc, ctx, "qry")
        x = sc.sb("x", [P, TC, D])
        xn = sc.sb("xn", [P, TC, D])
        xnT = sc.sb("xnT", [P, KC, T])
        wq = sc.sb("wq", [P, KC, D])
        wkv = sc.sb("wkv", [P, 2, KC, D])
        bq = sc.sb("bq", [P, KC])
        ct = sc.sb("ct", [P, KC, KPAD])
        norm = Norm(sc, "ln")
        banks = [sc.ps(f"bank{i}", [P, T]) for i in range(2 * KC)]
        ct_in = [sc.sem(f"ct_in{g}") for g in range(len(GROUPS))]
        x_in, wq_in, bq_in, wkv_in = sc.sem("x_in"), sc.sem("wq_in"), sc.sem("bq_in"), sc.sem("wkv_in")
        bk_in = sc.sem("bk_in")
        ident0, ident_ready = sc.sem("ident0"), sc.sem("ident_ready")
        turned, turned_out, q_mm, q_out = sc.sem("turned"), sc.sem("turned_out"), sc.sem("q_mm"), sc.sem("q_out")
        w_hi, w_lo, ct_hi, ct_lo = (sc.sem(n) for n in ("w_hi", "w_lo", "ct_hi", "ct_lo"))
        block = ctx.enter_context(nc.Block())

        @block.sync
        def _(sp):
            sp.dma_start(x[:], dram["x"].rearrange("(t p) d -> p t d", p=P)).then_inc(x_in, 16)
            sp.dma_start(wq[:], dram["L0_xattn_Wq"]).then_inc(wq_in, 16)
            sp.dma_start(bq[:], dram["L0_xattn_bq"]).then_inc(bq_in, 16)
            sp.dma_start(res["bk"][:], dram["L0_xattn_bk"]).then_inc(bk_in, 16)
            sp.dma_start(wkv[:, 0], dram["L0_xattn_Wk"]).then_inc(wkv_in, 16)
            sp.dma_start(wkv[:, 1], dram["L0_xattn_Wv"]).then_inc(wkv_in, 16)
            for g, (s, w) in enumerate(GROUPS):
                sp.dma_start(ct[:, :, s:s + w], dram["ctxT"][0, :, :, s:s + w]).then_inc(ct_in[g], 16)
            sp.wait_ge(bk_in, 16)

        @block.gpsimd
        def _(pool):
            nc.gpsimd.memset(res["ident"][:], 0.0).then_inc(ident0, 1)
            pool.wait_ge(ident0, 1)
            nc.gpsimd.affine_select(out=res["ident"][:], in_=res["ident"][:], compare_op=ALU.not_equal, fill=1.0,
                                    base=0, pattern=[[-1, P]], channel_multiplier=1).then_inc(ident_ready, 1)
            nc.gpsimd.memset(res["q_blk_hi"][:].bitcast(F32), 0.0)
            nc.gpsimd.memset(res["q_blk_lo"][:].bitcast(F32), 0.0)
            for i in range(2):
                pool.wait_ge(w_hi, i + 1)
                nc.gpsimd.tensor_tensor(res["w_lo"][:, i], wkv[:, i], res["w_hi"][:, i].bitcast(F32),
                                        ALU.subtract).then_inc(w_lo, 1)

        @block.scalar
        def _(act):
            norm.scalar(nc, act)
            for c in range(KC):
                act.wait_ge(turned, c + 1)
                nc.scalar.activation(xnT[:, c, :], banks[c][:], ACT.Copy).then_inc(turned_out, 1)
            act.wait_ge(wkv_in, 32)
            for i in range(2):
                nc.scalar.activation(res["w_hi"][:, i], wkv[:, i], ACT.Copy).then_inc(w_hi, 1)
            for g, (s, w) in enumerate(GROUPS):
                act.wait_ge(ct_in[g], 16)
                nc.scalar.activation(res["ct_hi"][:, :, s:s + w], ct[:, :, s:s + w], ACT.Copy).then_inc(ct_hi, 1)

        @block.vector
        def _(dve):
            dve.wait_ge(x_in, 16)
            norm.vector(nc, dve, x, xn)
            dve.wait_ge(bq_in, 16)
            for o in range(KC):
                dve.wait_ge(q_mm, o + 1)
                nc.vector.tensor_scalar(res["qT"][:, o, :], banks[KC + o][:], bq[:, o:o + 1], HD ** -0.5,
                                        ALU.add, ALU.mult).then_inc(q_out, 1)
            for g, (s, w) in enumerate(GROUPS):
                dve.wait_ge(ct_hi, g + 1)
                nc.vector.tensor_tensor(res["ct_lo"][:, :, s:s + w], ct[:, :, s:s + w],
                                        res["ct_hi"][:, :, s:s + w].bitcast(F32), ALU.subtract).then_inc(ct_lo, 1)

        @block.tensor
        def _(pe):
            pe.wait_ge(ident_ready, 1)
            pe.wait_ge(norm.done, TC)
            for c in range(KC):
                transpose_rows(nc, banks[c], xn, c, res["ident"]).then_inc(turned, 1)
            pe.wait_ge(wq_in, 16)
            pe.wait_ge(turned_out, KC)
            for o in range(KC):
                product(nc, banks[KC + o][:], [(wq[:, k, o * P:(o + 1) * P], xnT[:, k, :]) for k in range(KC)]
                        ).then_inc(q_mm, 1)


V_SIZES = [2] * 6 + [1]


def order(text):
    uses = []
    for word in text.split():
        kind = word[0]
        at = [int(word[1:])] if kind == "c" else [int(a) for a in word[1:]]
        if kind == "v":
            half, n = at
            at = [half, sum(V_SIZES[:n]), V_SIZES[n]]
        uses.append((kind, *at))
    return uses


BODY = order("""
    s0 v00 e0 n0 v01 s1 v02 e1 u0 t00 v03 n1 t01 v04 t02 v05 v06 u1 k10 t10 k11 t11 k12 t12 k13
    s2 o0 e2 n2 k20 s3 k21 e3 u2 t20 k22 n3 t21 k23 t22 k30 u3 t30 k31 t31 k32 t32 k33
    s4 o1 e4 n4 v10 s5 v11 e5 u4 t40 c0 c1 v12 n5 t41 c2 c3 v13 t42 c4 c5 s6 v14 e6 u5 t50 c6 c7 v15 n6 t51 c8 c9
    v16 t52 c10 c11 s7 o2 e7 n7 c12 c13 k40 u6 t60 c14 c15 k41 t61 k42 t62 u7 t70 k43 t71 t72 q o3""")
BEFORE = order("k00 k01 k02 k03")
BANKED = [u for u in BEFORE + BODY if u[0] in "vkt"]
USE = {u: n - len(BEFORE) for n, u in enumerate(BANKED)}
NUSE = len(BANKED) - len(BEFORE)
LAST = [u for u in BODY if u[0] not in "cq" and u[:2] != ("k", KC)]
LAST_USE = {u: n for n, u in enumerate(u for u in LAST if u[0] in "vkt")}
RING = 3
assert NUSE % RING == 0
OGROUPS = D // P


NPIECE = KC * GROUPS_N
NSTAGE = 4


def piece(n):
    s, w = GROUPS[n // KC]
    return (slice(None), n % KC, slice(s, s + w)), w


START = 1


def phase_cross(nc, dram, res):
    with ExitStack() as ctx:
        sc = Scope(nc, ctx, "crs")
        ct_hi, ct_lo = res["ct_hi"], res["ct_lo"]
        stage = [sc.sb(f"stage{i}", [P, SW]) for i in range(NSTAGE)]
        kt_hi = sc.sb("kt_hi", [P, 2, KPAD], F32R)
        kt_lo = sc.sb("kt_lo", [P, 2, KPAD], F32R)
        v_hi = sc.sb("v_hi", [P, NCH, 2 * P], F32R)
        v_lo = sc.sb("v_lo", [P, NCH, 2 * P], F32R)
        pt_hi = sc.sb("pt_hi", [P, NCH, 2 * P], F32R)
        pt_lo = sc.sb("pt_lo", [P, NCH, 2 * P], F32R)
        prob = sc.sb("prob", [P, 2, KEYS])
        nmx = sc.sb("nmx", [P, 2])
        rsum, rtot = sc.sb("rsum", [P, 2]), sc.sb("rtot", [P, 2])
        rinv = sc.sb("rinv", [P, 2])
        w_hi, w_lo, q_hi, q_lo = res["w_hi"], res["w_lo"], res["q_blk_hi"], res["q_blk_lo"]
        qT, oT, bk, ident = res["qT"], res["oT"], res["bk"], res["ident"]

        score = sc.ps("score", [P, GROUPS_N, BANK])
        ring = [sc.ps(f"ring{i}", [P, BANK]) for i in range(RING)]
        out_bank = sc.ps("out_bank", [P, BANK])

        ct_hi_ready = sc.sem("ct_hi_ready")
        ct_lo_ready = [sc.sem(f"ct_lo_ready{i}") for i in range(2)]
        ct_in = [sc.sem(f"ct_in{i}") for i in range(NSTAGE)]
        q_hi_ready, q_lo_ready = sc.sem("q_hi_ready"), sc.sem("q_lo_ready")
        filled = sc.sem("filled")
        hi_out = sc.sem("hi_out")
        freed = sc.sem("freed")
        tail_filled, tail_hi, tail_freed = sc.sem("tail_filled"), sc.sem("tail_hi"), sc.sem("tail_freed")
        rtot_ready = sc.sem("rtot_ready")
        scored = sc.sem("scored")
        nmax_ready, exp_done = sc.sem("nmax_ready"), sc.sem("exp_done")
        rinv_ready, prob_ready = sc.sem("rinv_ready"), sc.sem("prob_ready")
        pv_done, o_out = sc.sem("pv_done"), sc.sem("o_out")
        block = ctx.enter_context(nc.Block())
        LEAD = len(BEFORE)

        def split_low(eng, engine, n, b):
            at, w = piece(n)
            eng.wait_ge(ct_hi_ready, NPIECE * b + n + 1)
            engine.tensor_tensor(ct_lo[at], stage[n % NSTAGE][:, 0:w], ct_hi[at].bitcast(F32), ALU.subtract
                                 ).then_inc(ct_lo_ready[n % 2], 1)

        @block.sync
        def _(sp):
            with sp.Fori(0, B - 1) as b:
                for n in range(NPIECE):
                    sp.wait_ge(ct_lo_ready[n % 2], START + NPIECE // 2 * b + max(0, (n - NSTAGE) // 2 + 1))
                    at, w = piece(n)
                    sp.dma_start(stage[n % NSTAGE][:, 0:w], dram["ctxT"][(b + 1, *at)]).then_inc(ct_in[n % NSTAGE], 16)

        @block.gpsimd
        def _(pool):
            pool.sem_inc(ct_lo_ready[0], START)
            with pool.Fori(0, B - 1) as b:
                for n in range(0, NPIECE, 2):
                    split_low(pool, nc.gpsimd, n, b)

        def out_tiles(use, at):
            bank = ring[at[use] % RING]
            if use[0] == "v":
                _, half, c0, n = use
                kk = CHUNKS[c0][1]
                view = bank[0:kk, 0:n * 2 * P].rearrange("p (c f) -> p c f", c=n)
                return view, v_hi[0:kk, c0:c0 + n, :], v_lo[0:kk, c0:c0 + n, :]
            if use[0] == "k":
                _, fc, g = use
                s, w = GROUPS[g]
                return bank[:, 0:w], kt_hi[:, fc % 2, s:s + w], kt_lo[:, fc % 2, s:s + w]
            _, p, i = use
            f = slice((p % 2) * P, (p % 2 + 1) * P)
            view = bank[:].rearrange("p (c f) -> p c f", c=4)
            return view, pt_hi[:, 4 * i:4 * i + 4, f], pt_lo[:, 4 * i:4 * i + 4, f]

        def tail_tiles(p):
            kk, i = CHUNKS[NCH - 1][1], p % 2
            f = slice(i * P, (i + 1) * P)
            return out_bank[0:kk, (2 + i) * P:(3 + i) * P], pt_hi[0:kk, NCH - 1, f], pt_lo[0:kk, NCH - 1, f]

        def reusable(eng, use, b):
            if use[0] == "v":
                eng.wait_ge(pv_done, START + OGROUPS * b + 2 * use[1])
            elif use[0] == "k":
                eng.wait_ge(scored, START + PAIRS * b + max(0, 2 * use[1] - 2))
            else:
                eng.wait_ge(pv_done, START + OGROUPS * b + use[1] // 2)

        @block.scalar
        def _(act):
            act.sem_inc(exp_done, START)

            def split_high(n, b):
                at, w = piece(n)
                act.wait_ge(ct_in[n % NSTAGE], 16 * (NPIECE // NSTAGE * b + n // NSTAGE + 1))
                nc.scalar.activation(ct_hi[at], stage[n % NSTAGE][:, 0:w], ACT.Copy).then_inc(ct_hi_ready, 1)

            def split_q_high(b):
                for h in range(HPC):
                    r = slice(h * HD, (h + 1) * HD)
                    ins = nc.scalar.activation(q_hi[r, :, h // 2, (h % 2) * LAT:(h % 2 + 1) * LAT],
                                               qT[r, :, bass.ts(b, LAT)], ACT.Copy)
                ins.then_inc(q_hi_ready, 1)

            def empty_high(use, b, at=USE):
                view, hi, _ = out_tiles(use, at)
                reusable(act, use, b)
                act.wait_ge(filled, START + LEAD + NUSE * b + at[use] + 1)
                if use[0] == "k":
                    c = use[1] % KC
                    nc.scalar.activation(hi, view, ACT.Identity, bias=bk[:, c:c + 1]).then_inc(hi_out, 1)
                else:
                    nc.scalar.activation(hi, view, ACT.Copy).then_inc(hi_out, 1)

            def turn(b, body, at):
                for use in body:
                    if use[0] == "e":
                        p, i = use[1], use[1] % 2
                        act.wait_ge(nmax_ready, PAIRS * b + p + 1)
                        nc.scalar.activation(prob[:, i, 0:GROUPS_N * GW].rearrange("p (g w) -> p g w", g=GROUPS_N),
                                             score[:, :, 0:GW], ACT.Exp, bias=nmx[:, i:i + 1],
                                             accum_out=rsum[:, i:i + 1])
                        nc.scalar.activation(prob[:, i, GROUPS_N * GW:KEYS], score[:, GROUPS_N - 1, GW:KEYS - GROUPS[-1][0]],
                                             ACT.Exp, bias=nmx[:, i:i + 1]).then_inc(exp_done, 1)
                    elif use[0] == "u":
                        p = use[1]
                        view, hi, _ = tail_tiles(p)
                        act.wait_ge(pv_done, START + OGROUPS * b + p // 2)
                        act.wait_ge(tail_filled, PAIRS * b + p + 1)
                        nc.scalar.activation(hi, view, ACT.Copy).then_inc(tail_hi, 1)
                    elif use[0] == "q":
                        act.wait_ge(scored, START + PAIRS * b + PAIRS)
                        split_q_high(b + 1)
                    elif use[0] == "c":
                        split_high(use[1], b)
                    elif use[0] in "vkt":
                        empty_high(use, b, at)

            split_q_high(0)
            for use in BEFORE:
                empty_high(use, 0)
            with act.Fori(0, B - 1) as b:
                turn(b, BODY, USE)
            turn(B - 1, LAST, LAST_USE)

        @block.vector
        def _(dve):
            dve.sem_inc(freed, RING)
            dve.sem_inc(o_out, START)
            dve.sem_inc(ct_lo_ready[1], START)

            def empty_low(use, b, at=USE):
                view, hi, lo = out_tiles(use, at)
                dve.wait_ge(hi_out, LEAD + NUSE * b + at[use] + 1)
                if use[0] == "k":
                    c = use[1] % KC
                    nc.vector.scalar_tensor_tensor(lo, view, bk[:, c:c + 1], hi.bitcast(F32), ALU.add, ALU.subtract
                                                   ).then_inc(freed, 1)
                else:
                    nc.vector.tensor_tensor(lo, view, hi.bitcast(F32), ALU.subtract).then_inc(freed, 1)

            def normalise(p, b):
                i = p % 2
                dve.wait_ge(exp_done, START + PAIRS * b + p + 1)
                nc.vector.tensor_tensor(rtot[:, i:i + 1], rsum[:, i:i + 1], prob[:, i, KEYS - 1:KEYS], ALU.add
                                        ).then_inc(rtot_ready, 1)
                dve.wait_ge(rtot_ready, PAIRS * b + p + 1)
                nc.vector.reciprocal(rinv[:, i:i + 1], rtot[:, i:i + 1]).then_inc(rinv_ready, 1)
                dve.wait_ge(rinv_ready, PAIRS * b + p + 1)
                nc.vector.tensor_scalar(prob[:, i, :], prob[:, i, :], rinv[:, i:i + 1], None, ALU.mult
                                        ).then_inc(prob_ready, 1)

            def split_q_low(b, nth):
                dve.wait_ge(q_hi_ready, nth)
                for h in range(HPC):
                    r = slice(h * HD, (h + 1) * HD)
                    block_of = (r, slice(None), h // 2, slice((h % 2) * LAT, (h % 2 + 1) * LAT))
                    ins = nc.vector.tensor_tensor(q_lo[block_of], qT[r, :, bass.ts(b, LAT)], q_hi[block_of].bitcast(F32),
                                                  ALU.subtract)
                ins.then_inc(q_lo_ready, 1)

            def take_out(fc, b):
                dve.wait_ge(pv_done, START + OGROUPS * b + fc + 1)
                for h in range(HPC):
                    r = slice(h * HD, (h + 1) * HD)
                    ins = nc.vector.tensor_copy(oT[r, fc, bass.ts(b, LAT)], out_bank[r, h * LAT:(h + 1) * LAT])
                ins.then_inc(o_out, 1)

            def turn(b, body, at):
                for use in body:
                    if use[0] == "s":
                        i = use[1] % 2
                        dve.wait_ge(scored, START + PAIRS * b + use[1] + 1)
                        nc.vector.reduce_max(nmx[:, i:i + 1], score[:, :, 0:SW - 1], AX.XY, negate=True
                                             ).then_inc(nmax_ready, 1)
                    elif use[0] == "n":
                        normalise(use[1], b)
                    elif use[0] == "u":
                        view, hi, lo = tail_tiles(use[1])
                        dve.wait_ge(tail_hi, PAIRS * b + use[1] + 1)
                        nc.vector.tensor_tensor(lo, view, hi.bitcast(F32), ALU.subtract).then_inc(tail_freed, 1)
                    elif use[0] == "c":
                        if use[1] % 2:
                            split_low(dve, nc.vector, use[1], b)
                    elif use[0] == "q":
                        split_q_low(b + 1, b + 2)
                    elif use[0] == "o":
                        take_out(use[1], b)
                    elif use[0] in "vkt":
                        empty_low(use, b, at)

            split_q_low(0, 1)
            for use in BEFORE:
                empty_low(use, 0)
            with dve.Fori(0, B - 1) as b:
                turn(b, BODY, USE)
            turn(B - 1, LAST, LAST_USE)

        @block.tensor
        def _(pe):
            for counter in (filled, scored, pv_done):
                pe.sem_inc(counter, START)

            def written(use, b, at):
                pe.wait_ge(freed, LEAD + NUSE * b + at[use] + 1 + RING)

            def fill(use, b, at=USE):
                pe.wait_ge(freed, LEAD + NUSE * b + at[use] + 1)
                bank = ring[at[use] % RING]
                if use[0] == "v":
                    _, half, c0, n = use
                    for c in range(c0, c0 + n):
                        s, kk = CHUNKS[c]
                        f = slice(half * 2 * P, (half + 1) * 2 * P)
                        ins = product3(nc, bank[0:kk, (c - c0) * 2 * P:(c - c0 + 1) * 2 * P],
                                       [((ct_hi[:, k, s:s + kk], ct_lo[:, k, s:s + kk]),
                                         (w_hi[:, 1, k, f], w_lo[:, 1, k, f])) for k in range(KC)])
                elif use[0] == "k":
                    _, fc, g = use
                    s, w = GROUPS[g]
                    if fc == KC:
                        for i in range(2):
                            pe.wait_ge(ct_lo_ready[i], START + NPIECE // 2 * b + KC // 2 * (g + 1))
                    f = slice((fc % KC) * P, (fc % KC + 1) * P)
                    ins = product3(nc, bank[:, 0:w],
                                   [((w_hi[:, 0, k, f], w_lo[:, 0, k, f]),
                                     (ct_hi[:, k, s:s + w], ct_lo[:, k, s:s + w])) for k in range(KC)])
                else:
                    _, p, i = use
                    for c in range(4 * i, 4 * i + 4):
                        s = CHUNKS[c][0]
                        ins = nc.tensor.transpose(bank[:, (c - 4 * i) * P:(c - 4 * i + 1) * P],
                                                  prob[:, p % 2, s:s + P], ident[:])
                ins.then_inc(filled, 1)

            def fill_tail(p, b):
                s, kk = CHUNKS[NCH - 1]
                pe.wait_ge(prob_ready, PAIRS * b + p + 1)
                pe.wait_ge(o_out, START + OGROUPS * b + p // 2)
                if p % 2:
                    pe.wait_ge(tail_freed, PAIRS * b + p)
                nc.tensor.transpose(tail_tiles(p)[0], prob[:, p % 2, s:s + kk], ident[:]).then_inc(tail_filled, 1)

            def scores(p, b, at):
                fc, i = p // 2, p % 2
                pe.wait_ge(exp_done, START + PAIRS * b + p)
                for g, (s, _) in enumerate(GROUPS):
                    if i == 0:
                        pe.wait_ge(freed, LEAD + NUSE * b + RING + 1
                                   + k_position(fc, min(g + 1, GROUPS_N - 1), at))
                    ins = product3(nc, score[:, g, 0:SW],
                                   [((q_hi[:, fc, i, :], q_lo[:, fc, i, :]),
                                     (kt_hi[:, fc % 2, s:s + SW], kt_lo[:, fc % 2, s:s + SW]))])
                ins.then_inc(scored, 1)

            def k_position(fc, g, at):
                return at[("k", fc, g)] if fc else -1

            def weigh(fc, b, at):
                f = slice((fc % 2) * P, (fc % 2 + 1) * P)
                pe.wait_ge(o_out, START + OGROUPS * b + fc)
                pe.wait_ge(tail_freed, PAIRS * b + 2 * fc + 2)
                n = 0
                for c, (s, kk) in enumerate(CHUNKS):
                    if c % 4 == 0 and c + 4 <= NCH:
                        written(("t", 2 * fc + 1, c // 4), b, at)
                    for a, m in ((v_hi, pt_hi), (v_hi, pt_lo), (v_lo, pt_hi)):
                        ins = nc.tensor.matmul(out_bank[:, 0:2 * P], a[0:kk, c, f], m[0:kk, c, :], start=(n == 0),
                                               stop=(n == 3 * NCH - 1))
                        n += 1
                ins.then_inc(pv_done, 1)

            def turn(b, body, at):
                for use in body:
                    if use[0] == "s":
                        if use[1] == 0:
                            pe.wait_ge(q_lo_ready, b + 1)
                        scores(use[1], b, at)
                    elif use[0] == "u":
                        fill_tail(use[1], b)
                    elif use[0] == "o":
                        weigh(use[1], b, at)
                    elif use[0] in "vkt":
                        fill(use, b, at)

            for use in BEFORE:
                fill(use, 0)
            with pe.Fori(0, B - 1) as b:
                turn(b, BODY, USE)
            turn(B - 1, LAST, LAST_USE)


def phase_cross_out(nc, dram, res):
    with ExitStack() as ctx:
        sc = Scope(nc, ctx, "cro")
        wo = sc.sb("wo", [P, KC, D])
        bo = sc.sb("bo", [P, D])
        bv = sc.sb("bv", [P, KC])
        xb = sc.sb("xb", [P, TC, D])
        x, oT = res["x"], res["oT"]
        banks = [sc.ps(f"bank{i}", [P, D]) for i in range(TC)]
        x_in, w_in, bo_in, bv_in = sc.sem("x_in"), sc.sem("w_in"), sc.sem("bo_in"), sc.sem("bv_in")
        biased, o_biased, mm, out = sc.sem("biased"), sc.sem("o_biased"), sc.sem("mm"), sc.sem("out")
        block = ctx.enter_context(nc.Block())

        @block.sync
        def _(sp):
            sp.dma_start(bv[:], dram["L0_xattn_bv"]).then_inc(bv_in, 16)
            sp.dma_start(wo[:], dram["L0_xattn_Wo"]).then_inc(w_in, 16)
            sp.dma_start(x[:], dram["x"].rearrange("(t p) d -> p t d", p=P)).then_inc(x_in, 16)
            sp.dma_start(bo[:], dram["L0_xattn_bo"].partition_broadcast(P)).then_inc(bo_in, 16)

        @block.vector
        def _(dve):
            dve.wait_ge(bv_in, 16)
            for c in range(KC):
                nc.vector.tensor_scalar(oT[:, c, :], oT[:, c, :], bv[:, c:c + 1], None, ALU.add
                                        ).then_inc(o_biased, 1)
            dve.wait_ge(x_in, 16)
            dve.wait_ge(bo_in, 16)
            for t in range(TC):
                nc.vector.tensor_tensor(xb[:, t, :], x[:, t, :], bo[:], ALU.add).then_inc(biased, 1)
            for t in range(TC):
                dve.wait_ge(mm, t + 1)
                dve.wait_ge(biased, t + 1)
                nc.vector.tensor_tensor(x[:, t, :], xb[:, t, :], banks[t][:], ALU.add).then_inc(out, 1)

        @block.tensor
        def _(pe):
            pe.wait_ge(w_in, 16)
            pe.wait_ge(o_biased, KC)
            for t in range(TC):
                product(nc, banks[t][:], [(oT[:, c, t * P:(t + 1) * P], wo[:, c, :]) for c in range(KC)]
                        ).then_inc(mm, 1)


def phase_scan(nc, dram, ident, x, ahead):
    with ExitStack() as ctx:
        sc = Scope(nc, ctx, "scn")
        xn = sc.sb("xn", [P, TC, D])
        sq = sc.sb("sq", [P, D])
        ss = sc.sb("ss", [P, TC])
        nrm = sc.sb("nrm", [P, TC])
        rn = sc.sb("rn", [P, TC])
        xs = sc.sb("xs", [P, TC, D])
        xnT = sc.sb("xnT", [P, KC, T])
        w = sc.sb("w", [P, KC, 3 * D])
        gamma = sc.sb("gamma", [P, KC])
        decay = sc.sb("decay", [P, KC, T])
        y = sc.sb("y", [P, KC, T])
        yq = sc.sb("yq", [P, KC, T])
        norm = Norm(sc, "ln")
        banks = [sc.ps(f"bank{i}", [P, T]) for i in range(8)]
        g_in, w_in = sc.sem("g_in"), sc.sem("w_in")
        squared, nrm_ready, nrm_done = sc.sem("squared"), sc.sem("nrm_ready"), sc.sem("nrm_done")
        scaled, turned, turned_out, mm = sc.sem("scaled"), sc.sem("turned"), sc.sem("turned_out"), sc.sem("mm")
        decay_ready, decay_cut, scanned = sc.sem("decay_ready"), sc.sem("decay_cut"), sc.sem("scanned")
        gated, back, out = sc.sem("gated"), sc.sem("back"), sc.sem("out")
        KV, A, Q = range(3)
        column = {KV: 1, A: 2, Q: 0}

        def bank(f, part):
            return banks[(KC + 3 * f + part) % 8]

        block = ctx.enter_context(nc.Block())

        @block.sync
        def _(sp):
            sp.dma_start(gamma[:], dram["L0_attn_gamma"]).then_inc(g_in, 16)
            sp.dma_start(w[:], dram["L0_attn_W_qkva"]).then_inc(w_in, 16)
            ahead.load_turned(sp, 0)
            ahead.load_rows(sp, 0)

        @block.scalar
        def _(act):
            norm.scalar(nc, act)
            for t in range(TC):
                act.wait_ge(norm.done, t + 1)
                if t:
                    act.wait_ge(squared, t)
                nc.scalar.activation(sq[:], xn[:, t, :], ACT.Square, accum_out=ss[:, t:t + 1]).then_inc(squared, 1)
            act.wait_ge(squared, TC)
            nc.scalar.activation(nrm[:], ss[:], ACT.Sqrt).then_inc(nrm_ready, 1)
            act.wait_ge(g_in, 16)
            for c in range(KC):
                act.wait_ge(turned, c + 1)
                nc.scalar.activation(xnT[:, c, :], banks[c][:], ACT.Copy, scale=gamma[:, c:c + 1]
                                     ).then_inc(turned_out, 1)
            for f in range(KC):
                act.wait_ge(mm, 3 * f + A + 1)
                nc.scalar.activation(decay[:, f, :], bank(f, A)[:], ACT.Sigmoid).then_inc(decay_ready, 1)

        @block.vector
        def _(dve):
            norm.vector(nc, dve, x, xn)
            dve.wait_ge(nrm_ready, 1)
            nc.vector.tensor_scalar(nrm[:], nrm[:], 1e-12, D ** -0.5, ALU.max, ALU.mult).then_inc(nrm_done, 1)
            dve.wait_ge(nrm_done, 1)
            nc.vector.reciprocal(rn[:], nrm[:]).then_inc(nrm_done, 1)
            dve.wait_ge(nrm_done, 2)
            for t in range(TC):
                nc.vector.tensor_scalar(xs[:, t, :], xn[:, t, :], rn[:, t:t + 1], None, ALU.mult
                                        ).then_inc(scaled, 1)
            for f in range(KC):
                dve.wait_ge(decay_ready, f + 1)
                nc.vector.memset(decay[:, f, :].rearrange("p (b n) -> p b n", b=B)[:, :, 0:1], 0.0
                                 ).then_inc(decay_cut, 1)
                dve.wait_ge(decay_cut, f + 1)
                nc.vector.tensor_tensor_scan(y[:, f, :], decay[:, f, :], bank(f, KV)[:], 0.0, ALU.mult, ALU.add
                                             ).then_inc(scanned, 1)
                dve.wait_ge(scanned, f + 1)
                dve.wait_ge(mm, 3 * f + Q + 1)
                nc.vector.tensor_tensor(yq[:, f, :], y[:, f, :], bank(f, Q)[:], ALU.mult).then_inc(gated, 1)
            for t in range(TC):
                dve.wait_ge(back, t + 1)
                nc.vector.tensor_tensor(x[:, t, :], x[:, t, :], banks[t][:], ALU.add).then_inc(out, 1)

        @block.tensor
        def _(pe):
            pe.wait_ge(scaled, TC)
            for c in range(KC):
                transpose_rows(nc, banks[c], xs, c, ident).then_inc(turned, 1)
            pe.wait_ge(turned_out, KC)
            pe.wait_ge(w_in, 16)
            for f in range(KC):
                for part in (KV, A, Q):
                    n = 3 * f + part
                    if n >= 8:
                        pe.wait_ge(gated, (n - 8) // 3 + 1)
                    o = column[part] * D + f * P
                    product(nc, bank(f, part)[:], [(w[:, k, o:o + P], xnT[:, k, :]) for k in range(KC)]
                            ).then_inc(mm, 1)
            pe.wait_ge(gated, KC)
            for t in range(TC):
                for f in range(KC):
                    last = nc.tensor.transpose(banks[t][:, f * P:(f + 1) * P], yq[:, f, t * P:(t + 1) * P], ident[:])
                last.then_inc(back, 1)


class Route:

    def __init__(self, sc, dram, bias=None):
        self.dram, self.bias = dram, bias
        shape = [P, TC, E0]
        self.rank = sc.sb("rt_rank", shape)
        self.rb = sc.sb("rt_bias", [P, E0]) if bias is not None else None
        self.lg, self.dl, self.ex = (sc.sb(f"rt_{n}", shape) for n in ("lg", "dl", "ex"))
        self.eq, self.cand, self.mask, self.coef = (sc.sb(f"rt_{n}", shape) for n in ("eq", "cand", "mask", "coef"))
        self.mx, self.sum, self.gate, self.best = (sc.sb(f"rt_{n}", [P, TC]) for n in ("mx", "sum", "gate", "best"))
        self.const_in = sc.sem("rt_const_in")
        self.step = sc.sem("rt_step")
        self.dl_ready, self.ex_ready, self.done = (sc.sem(f"rt_{n}") for n in ("dl_ready", "ex_ready", "done"))

    def sync(self, sp):
        sp.dma_start(self.rank[:], self.dram["rank"].partition_broadcast(P)).then_inc(self.const_in, 16)
        if self.bias is not None:
            sp.dma_start(self.rb[:], self.bias.partition_broadcast(P)).then_inc(self.const_in, 16)

    def scalar(self, nc, act):
        act.wait_ge(self.dl_ready, 1)
        nc.scalar.activation(self.ex[:], self.dl[:], ACT.Exp).then_inc(self.ex_ready, 1)

    def vector(self, nc, dve, logits):
        n = [0]

        def step(ins):
            n[0] += 1
            ins.then_inc(self.step, 1)
            dve.wait_ge(self.step, n[0])

        wide = lambda a: a[:].unsqueeze(2).broadcast_to([P, TC, E0])
        dve.wait_ge(self.const_in, 32 if self.bias is not None else 16)
        if self.bias is not None:
            step(nc.vector.tensor_tensor(self.lg[:], logits, self.rb[:].unsqueeze(1).broadcast_to([P, TC, E0]),
                                         ALU.add))
        else:
            step(nc.vector.tensor_copy(self.lg[:], logits))
        step(nc.vector.reduce_max(self.mx[:], self.lg[:], AX.X))
        nc.vector.tensor_tensor(self.dl[:], self.lg[:], wide(self.mx), ALU.subtract).then_inc(self.dl_ready, 1)
        step(nc.vector.tensor_tensor(self.eq[:], self.lg[:], wide(self.mx), ALU.is_equal))
        step(nc.vector.tensor_tensor(self.cand[:], self.eq[:], self.rank[:], ALU.mult))
        step(nc.vector.reduce_max(self.best[:], self.cand[:], AX.X))
        step(nc.vector.tensor_tensor(self.mask[:], self.cand[:], wide(self.best), ALU.is_equal))
        dve.wait_ge(self.ex_ready, 1)
        step(nc.vector.reduce_sum(self.sum[:], self.ex[:], AX.X))
        step(nc.vector.reciprocal(self.gate[:], self.sum[:]))
        nc.vector.tensor_tensor(self.coef[:], self.mask[:], wide(self.gate), ALU.mult).then_inc(self.done, 1)


def phase_experts(nc, dram, ident, x):
    with ExitStack() as ctx:
        sc = Scope(nc, ctx, "moe")
        RINGW = 3
        xn = sc.sb("xn", [P, TC, D])
        xnT = sc.sb("xnT", [P, KC, T])
        wr = sc.sb("wr", [P, KC, E0])
        eb = sc.sb("eb", [E0, D])
        ew = [sc.sb(f"ew{i}", [P, KC, D]) for i in range(RINGW)]
        coefT = sc.sb("coefT", [E0, T])
        norm = Norm(sc, "ln")
        rt = Route(sc, dram, dram["L0_ffn_router_b"])
        banks = [sc.ps(f"bank{i}", [P, T]) for i in range(8)]
        wr_in, eb_in = sc.sem("wr_in"), sc.sem("eb_in")
        ew_in = [sc.sem(f"ew_in{i}") for i in range(RINGW)]
        turned, turned_out, routed = sc.sem("turned"), sc.sem("turned_out"), sc.sem("routed")
        coef_turned, coef_out = sc.sem("coef_turned"), sc.sem("coef_out")
        bias_mm, biased, mm, added = sc.sem("bias_mm"), sc.sem("biased"), sc.sem("mm"), sc.sem("added")
        block = ctx.enter_context(nc.Block())

        @block.sync
        def _(sp):
            sp.dma_start(wr[:], dram["L0_ffn_router_w"]).then_inc(wr_in, 16)
            rt.sync(sp)
            sp.dma_start(eb[:], dram["L0_ffn_expert_b"]).then_inc(eb_in, 16)
            for e in range(E0):
                if e >= RINGW:
                    sp.wait_ge(mm, TC * (e - RINGW + 1))
                sp.dma_start(ew[e % RINGW][:], dram["L0_ffn_expert_w"][e]).then_inc(ew_in[e % RINGW], 16)

        @block.scalar
        def _(act):
            norm.scalar(nc, act)
            for c in range(KC):
                act.wait_ge(turned, c + 1)
                nc.scalar.activation(xnT[:, c, :], banks[c][:], ACT.Copy).then_inc(turned_out, 1)
            rt.scalar(nc, act)
            act.wait_ge(coef_turned, 1)
            nc.scalar.activation(coefT[:], banks[5][0:E0, :], ACT.Copy).then_inc(coef_out, 1)

        @block.vector
        def _(dve):
            norm.vector(nc, dve, x, xn)
            dve.wait_ge(routed, 1)
            rt.vector(nc, dve, banks[4][:, 0:TC * E0].rearrange("p (t e) -> p t e", t=TC))
            dve.wait_ge(rt.done, 1)
            for t in range(TC):
                dve.wait_ge(bias_mm, t + 1)
                nc.vector.tensor_tensor(x[:, t, :], x[:, t, :], banks[t][:], ALU.add).then_inc(added, 1)
            for e in range(E0):
                for t in range(TC):
                    n = e * TC + t
                    dve.wait_ge(mm, n + 1)
                    dve.wait_ge(added, n + 1)
                    nc.vector.scalar_tensor_tensor(x[:, t, :], banks[4 + t][:] if e % 2 == 0 else banks[t][:],
                                                   rt.coef[:, t, e:e + 1], x[:, t, :], ALU.mult, ALU.add
                                                   ).then_inc(added, 1)

        @block.tensor
        def _(pe):
            pe.wait_ge(norm.done, TC)
            for c in range(KC):
                transpose_rows(nc, banks[c], xn, c, ident).then_inc(turned, 1)
            pe.wait_ge(turned_out, KC)
            pe.wait_ge(wr_in, 16)
            for t in range(TC):
                last = product(nc, banks[4][:, t * E0:(t + 1) * E0],
                               [(xnT[:, k, t * P:(t + 1) * P], wr[:, k, :]) for k in range(KC)])
            last.then_inc(routed, 1)
            pe.wait_ge(rt.done, 1)
            for t in range(TC):
                last = nc.tensor.transpose(banks[5][0:E0, t * P:(t + 1) * P], rt.coef[:, t, :], ident[:])
            last.then_inc(coef_turned, 1)
            pe.wait_ge(coef_out, 1)
            pe.wait_ge(eb_in, 16)
            for t in range(TC):
                product(nc, banks[t][:], [(coefT[:, t * P:(t + 1) * P], eb[:])]).then_inc(bias_mm, 1)
            for e in range(E0):
                pe.wait_ge(ew_in[e % RINGW], 16 * (e // RINGW + 1))
                for t in range(TC):
                    n = e * TC + t
                    pe.wait_ge(added, max(1, n - TC + 1))
                    product(nc, banks[4 + t][:] if e % 2 == 0 else banks[t][:],
                            [(xnT[:, k, t * P:(t + 1) * P], ew[e % RINGW][:, k, :]) for k in range(KC)]
                            ).then_inc(mm, 1)


class ContextAhead:

    def __init__(self, sc, dram):
        self.dram = dram
        self.ct = [sc.sb(f"ct{i}", [P, KC, KPAD]) for i in range(2)]
        self.cr = [sc.sb(f"cr{i}", [P, NCH, D]) for i in range(2)]
        self.ct_in = [sc.sem(f"ct_in{i}") for i in range(2)]
        self.cr_in = [sc.sem(f"cr_in{i}") for i in range(2)]

    def load_turned(self, sp, t):
        for i in range(2):
            sp.dma_start(self.ct[i][:], self.dram["ctxT"][2 * t + i]).then_inc(self.ct_in[i], 16)

    def load_rows(self, sp, t):
        for i in range(2):
            sp.dma_start(self.cr[i][:, 0:NCH - 1, :], self.dram["ctxR"][2 * t + i]).then_inc(self.cr_in[i], 16)
            sp.dma_start(self.cr[i][0:CHUNKS[-1][1], NCH - 1, :], self.dram["ctxL"][2 * t + i]
                         ).then_inc(self.cr_in[i], 16)


def phase_context(nc, dram, ident, x, ahead):
    ct, cr, ct_in, cr_in = ahead.ct, ahead.cr, ahead.ct_in, ahead.cr_in
    with ExitStack() as ctx:
        sc = Scope(nc, ctx, "ctx")
        qk = sc.sb("qk", [P, KC, T])
        u = sc.sb("u", [P, TC, D])
        with ExitStack() as c2:
            s2 = Scope(nc, c2, "ctq")
            xn = s2.sb("xn", [P, TC, D])
            xnT = s2.sb("xnT", [P, KC, T])
            qT = s2.sb("qT", [P, KC, T])
            wq, wk = s2.sb("wq", [P, KC, D]), s2.sb("wk", [P, KC, D])
            bq = s2.sb("bq", [P, KC])
            norm = Norm(s2, "ln")
            banks = [s2.ps(f"bank{i}", [P, T]) for i in range(8)]
            wq_in, wk_in, bq_in = s2.sem("wq_in"), s2.sem("wk_in"), s2.sem("bq_in")
            turned, turned_out = s2.sem("turned"), s2.sem("turned_out")
            q_mm, q_out, qk_mm, qk_out = s2.sem("q_mm"), s2.sem("q_out"), s2.sem("qk_mm"), s2.sem("qk_out")
            block = c2.enter_context(nc.Block())

            @block.sync
            def _(sp):
                sp.dma_start(wq[:], dram["L1_xattn_Wq"]).then_inc(wq_in, 16)
                sp.dma_start(bq[:], dram["L1_xattn_bq"]).then_inc(bq_in, 16)
                sp.dma_start(wk[:], dram["L1_xattn_Wk"]).then_inc(wk_in, 16)

            @block.scalar
            def _(act):
                norm.scalar(nc, act)
                for c in range(KC):
                    act.wait_ge(turned, c + 1)
                    nc.scalar.activation(xnT[:, c, :], banks[c][:], ACT.Copy).then_inc(turned_out, 1)
                for c in range(KC):
                    act.wait_ge(qk_mm, c + 1)
                    nc.scalar.activation(qk[:, c, :], banks[c][:], ACT.Copy, scale=D ** -0.5).then_inc(qk_out, 1)

            @block.vector
            def _(dve):
                norm.vector(nc, dve, x, xn)
                dve.wait_ge(bq_in, 16)
                for o in range(KC):
                    dve.wait_ge(q_mm, o + 1)
                    nc.vector.tensor_scalar(qT[:, o, :], banks[KC + o][:], bq[:, o:o + 1], None, ALU.add
                                            ).then_inc(q_out, 1)

            @block.tensor
            def _(pe):
                pe.wait_ge(norm.done, TC)
                for c in range(KC):
                    transpose_rows(nc, banks[c], xn, c, ident).then_inc(turned, 1)
                pe.wait_ge(turned_out, KC)
                pe.wait_ge(wq_in, 16)
                for o in range(KC):
                    product(nc, banks[KC + o][:], [(wq[:, k, o * P:(o + 1) * P], xnT[:, k, :]) for k in range(KC)]
                            ).then_inc(q_mm, 1)
                pe.wait_ge(q_out, KC)
                pe.wait_ge(wk_in, 16)
                for c in range(KC):
                    product(nc, banks[c][:], [(wk[:, k, c * P:(c + 1) * P], qT[:, k, :]) for k in range(KC)]
                            ).then_inc(qk_mm, 1)

        with ExitStack() as c3:
            s3 = Scope(nc, c3, "cta")
            qs = s3.sb("qs", [P, KC, P])
            prob = s3.sb("prob", [P, KEYS])
            pt = s3.sb("pt", [P, NCH, P])
            nmx, rsum, rinv = s3.sb("nmx", [P, 1]), s3.sb("rsum", [P, 1]), s3.sb("rinv", [P, 1])
            score = s3.ps("score", [P, GROUPS_N * BANK])
            tb = [s3.ps(f"tb{i}", [P, BANK]) for i in range(2)]
            ub = s3.ps("ub", [P, D])
            qs_ready, scored, max_ready, exp_done = (s3.sem(n) for n in ("qs_ready", "scored", "max_ready", "exp_done"))
            rinv_ready, turned, turned_out = s3.sem("rinv_ready"), s3.sem("turned"), s3.sem("turned_out")
            weighed, u_out = s3.sem("weighed"), s3.sem("u_out")
            NT = 4
            block = c3.enter_context(nc.Block())
            KL = CHUNKS[-1][1]

            @block.sync
            def _(sp):
                with sp.Fori(0, TC - 1) as t:
                    sp.wait_ge(scored, t + 1)
                    ahead.load_turned(sp, t + 1)
                    sp.wait_ge(weighed, t + 1)
                    ahead.load_rows(sp, t + 1)

            @block.scalar
            def _(act):
                act.sem_inc(turned_out, 2)
                with act.Fori(0, TC) as t:
                    nc.scalar.activation(qs[:], qk[:, :, bass.ts(t, P)], ACT.Copy).then_inc(qs_ready, 1)
                    act.wait_ge(max_ready, t + 1)
                    nc.scalar.activation(prob[:], score[:, 0:KEYS], ACT.Exp, bias=nmx[:], accum_out=rsum[:]
                                         ).then_inc(exp_done, 1)
                    for i in range(NT):
                        act.wait_ge(turned, NT * t + i + 1)
                        if i < 3:
                            nc.scalar.activation(pt[:, 4 * i:4 * i + 4, :],
                                                 tb[i % 2][:].rearrange("p (c f) -> p c f", c=4), ACT.Copy
                                                 ).then_inc(turned_out, 1)
                        else:
                            nc.scalar.activation(pt[0:KL, NCH - 1, :], tb[i % 2][0:KL, 0:P], ACT.Copy
                                                 ).then_inc(turned_out, 1)
                    act.wait_ge(weighed, t + 1)

            @block.vector
            def _(dve):
                with dve.Fori(0, TC) as t:
                    dve.wait_ge(scored, t + 1)
                    nc.vector.reduce_max(nmx[:], score[:, 0:KEYS], AX.X, negate=True).then_inc(max_ready, 1)
                    dve.wait_ge(exp_done, t + 1)
                    nc.vector.reciprocal(rinv[:], rsum[:]).then_inc(rinv_ready, 1)
                    dve.wait_ge(rinv_ready, t + 1)
                    dve.wait_ge(weighed, t + 1)
                    nc.vector.tensor_scalar(u[:, bass.ds(t, 1), :], ub[:].unsqueeze(1), rinv[:], None, ALU.mult
                                            ).then_inc(u_out, 1)

            @block.tensor
            def _(pe):
                pe.sem_inc(u_out, 1)
                with pe.Fori(0, TC) as t:
                    pe.wait_ge(qs_ready, t + 1)
                    for i in range(2):
                        pe.wait_ge(ct_in[i], 16 * t + 16)
                    for s in range(0, KPAD, BANK):
                        w = min(BANK, KPAD - s)
                        for k in range(KC):
                            for i in range(2):
                                r = slice(i * LAT, (i + 1) * LAT)
                                last = nc.tensor.matmul(score[r, s:s + w], qs[:, k, r], ct[i][:, k, s:s + w],
                                                        start=(k == 0), stop=(k == KC - 1))
                    last.then_inc(scored, 1)
                    pe.wait_ge(exp_done, t + 1)
                    for i in range(NT):
                        pe.wait_ge(turned_out, NT * t + i + 1)
                        for c in range(4 * i, min(4 * i + 4, NCH)):
                            s, kk = CHUNKS[c]
                            last = nc.tensor.transpose(tb[i % 2][0:kk, (c - 4 * i) * P:(c - 4 * i + 1) * P],
                                                       prob[:, s:s + kk], ident[:])
                        last.then_inc(turned, 1)
                    pe.wait_ge(turned_out, NT * t + NT + 2)
                    pe.wait_ge(u_out, t + 1)
                    for i in range(2):
                        pe.wait_ge(cr_in[i], 32 * t + 32)
                    for c, (s, kk) in enumerate(CHUNKS):
                        for i in range(2):
                            r = slice(i * LAT, (i + 1) * LAT)
                            last = nc.tensor.matmul(ub[r, :], pt[0:kk, c, r], cr[i][0:kk, c, :], start=(c == 0),
                                                    stop=(c == NCH - 1))
                    last.then_inc(weighed, 1)

        with ExitStack() as c4:
            s4 = Scope(nc, c4, "cto")
            uT, vT = s4.sb("uT", [P, KC, T]), s4.sb("vT", [P, KC, T])
            wv, wo = s4.sb("wv", [P, KC, D]), s4.sb("wo", [P, KC, D])
            bv, bo = s4.sb("bv", [P, KC]), s4.sb("bo", [P, D])
            banks = [s4.ps(f"bank{i}", [P, T]) for i in range(8)]
            wv_in, wo_in, bv_in, bo_in = s4.sem("wv_in"), s4.sem("wo_in"), s4.sem("bv_in"), s4.sem("bo_in")
            turned, turned_out, v_mm, v_out = s4.sem("turned"), s4.sem("turned_out"), s4.sem("v_mm"), s4.sem("v_out")
            o_mm, biased, out = s4.sem("o_mm"), s4.sem("biased"), s4.sem("out")
            block = c4.enter_context(nc.Block())

            @block.sync
            def _(sp):
                sp.dma_start(wv[:], dram["L1_xattn_Wv"]).then_inc(wv_in, 16)
                sp.dma_start(bv[:], dram["L1_xattn_bv"]).then_inc(bv_in, 16)
                sp.dma_start(wo[:], dram["L1_xattn_Wo"]).then_inc(wo_in, 16)
                sp.dma_start(bo[:], dram["L1_xattn_bo"].partition_broadcast(P)).then_inc(bo_in, 16)

            @block.scalar
            def _(act):
                for c in range(KC):
                    act.wait_ge(turned, c + 1)
                    nc.scalar.activation(uT[:, c, :], banks[c][:], ACT.Copy).then_inc(turned_out, 1)
                act.wait_ge(bv_in, 16)
                for c in range(KC):
                    act.wait_ge(v_mm, c + 1)
                    nc.scalar.activation(vT[:, c, :], banks[KC + c][:], ACT.Identity, bias=bv[:, c:c + 1]
                                         ).then_inc(v_out, 1)

            @block.vector
            def _(dve):
                dve.wait_ge(bo_in, 16)
                for t in range(TC):
                    nc.vector.tensor_tensor(x[:, t, :], x[:, t, :], bo[:], ALU.add).then_inc(biased, 1)
                for t in range(TC):
                    dve.wait_ge(o_mm, t + 1)
                    dve.wait_ge(biased, t + 1)
                    nc.vector.tensor_tensor(x[:, t, :], x[:, t, :], banks[t][:], ALU.add).then_inc(out, 1)

            @block.tensor
            def _(pe):
                for c in range(KC):
                    transpose_rows(nc, banks[c], u, c, ident).then_inc(turned, 1)
                pe.wait_ge(turned_out, KC)
                pe.wait_ge(wv_in, 16)
                for o in range(KC):
                    product(nc, banks[KC + o][:], [(wv[:, k, o * P:(o + 1) * P], uT[:, k, :]) for k in range(KC)]
                            ).then_inc(v_mm, 1)
                pe.wait_ge(v_out, KC)
                pe.wait_ge(wo_in, 16)
                for t in range(TC):
                    product(nc, banks[t][:], [(vT[:, k, t * P:(t + 1) * P], wo[:, k, :]) for k in range(KC)]
                            ).then_inc(o_mm, 1)


def phase_latent(nc, dram, ident, x):
    with ExitStack() as ctx:
        sc = Scope(nc, ctx, "lat")
        xn = sc.sb("xn", [P, TC, D])
        xnT = sc.sb("xnT", [P, KC, T])
        wq, wl = sc.sb("wq", [P, KC, D]), sc.sb("wl", [P, KC, P])
        wk, wv, wo = sc.sb("wk", [P, D]), sc.sb("wv", [P, D]), sc.sb("wo", [P, KC, D])
        bq, bl, bk, bv = sc.sb("bq", [P, KC]), sc.sb("bl", [P, 1]), sc.sb("bk", [P, KC]), sc.sb("bv", [P, KC])
        bo = sc.sb("bo", [P, D])
        qT, kT, lT = sc.sb("qT", [P, KC, T]), sc.sb("kT", [P, KC, T]), sc.sb("lT", [P, T])
        v = sc.sb("v", [P, TC, D])
        q_blk = sc.sb("q_blk", [P, KC, 2, B, P])
        dif = sc.sb("dif", [P, PAIRS, B, LAT])
        prob = sc.sb("prob", [P, PAIRS, B, LAT])
        nmx, rs, ri = (sc.sb(n, [P, PAIRS, B]) for n in ("nmx", "rs", "ri"))
        pt = sc.sb("pt", [P, PAIRS, TC, P])
        oT = sc.sb("oT", [P, KC, T])
        norm = Norm(sc, "ln")
        banks = [sc.ps(f"bank{i}", [P, T]) for i in range(8)]
        w_in = {n: sc.sem(f"{n}_in") for n in ("wq", "wl", "wk", "wv", "wo", "bq", "bl", "bk", "bv", "bo")}
        zeroed, turned, turned_out = sc.sem("zeroed"), sc.sem("turned"), sc.sem("turned_out")
        q_mm, q_out, l_mm, l_out = sc.sem("q_mm"), sc.sem("q_out"), sc.sem("l_mm"), sc.sem("l_out")
        k_mm, k_out, v_mm, v_out = sc.sem("k_mm"), sc.sem("k_out"), sc.sem("v_mm"), sc.sem("v_out")
        blk_ready, scored, max_ready, dif_ready = (sc.sem(n) for n in ("blk_ready", "scored", "max_ready", "dif_ready"))
        exp_done, sum_ready, inv_ready, prob_ready = (sc.sem(n) for n in ("exp_done", "sum_ready", "inv_ready",
                                                                          "prob_ready"))
        p_turned, pt_out, weighed, o_out = (sc.sem(n) for n in ("p_turned", "pt_out", "weighed", "o_out"))
        biased, o_mm, out = sc.sem("biased"), sc.sem("o_mm"), sc.sem("out")
        block = ctx.enter_context(nc.Block())

        @block.sync
        def _(sp):
            tiles = dict(wq=wq, bq=bq, wl=wl, bl=bl, wk=wk, bk=bk, wv=wv, bv=bv, wo=wo)
            for n, tile in tiles.items():
                sp.dma_start(tile[:], dram[f"L1_attn_{n[0].upper() + n[1] if n[0] == 'w' else n}"]
                             ).then_inc(w_in[n], 16)
            sp.dma_start(bo[:], dram["L1_attn_bo"].partition_broadcast(P)).then_inc(w_in["bo"], 16)

        @block.gpsimd
        def _(pool):
            nc.gpsimd.memset(q_blk[:], 0.0).then_inc(zeroed, 1)

        @block.scalar
        def _(act):
            norm.scalar(nc, act)
            for c in range(KC):
                act.wait_ge(turned, c + 1)
                nc.scalar.activation(xnT[:, c, :], banks[c][:], ACT.Copy).then_inc(turned_out, 1)
            act.wait_ge(w_in["bl"], 16)
            act.wait_ge(l_mm, 1)
            nc.scalar.activation(lT[:], banks[4][:], ACT.Identity, bias=bl[:]).then_inc(l_out, 1)
            act.wait_ge(w_in["bk"], 16)
            for c in range(KC):
                act.wait_ge(k_mm, c + 1)
                nc.scalar.activation(kT[:, c, :], banks[c][:], ACT.Identity, bias=bk[:, c:c + 1]).then_inc(k_out, 1)
            for t in range(TC):
                act.wait_ge(v_mm, t + 1)
                nc.scalar.activation(v[:, t, :], banks[4 + t][:], ACT.Copy).then_inc(v_out, 1)
            for u in range(PAIRS):
                act.wait_ge(dif_ready, u + 1)
                nc.scalar.activation(prob[:, u], dif[:, u], ACT.Exp).then_inc(exp_done, 1)
            for u in range(PAIRS):
                act.wait_ge(p_turned, u + 1)
                nc.scalar.activation(pt[:, u], banks[u][:].rearrange("p (t f) -> p t f", t=TC), ACT.Copy
                                     ).then_inc(pt_out, 1)

        @block.vector
        def _(dve):
            norm.vector(nc, dve, x, xn)
            dve.wait_ge(w_in["bq"], 16)
            for c in range(KC):
                dve.wait_ge(q_mm, c + 1)
                nc.vector.tensor_scalar(qT[:, c, :], banks[(5 + c) % 8][:], bq[:, c:c + 1], HD ** -0.5, ALU.add,
                                        ALU.mult).then_inc(q_out, 1)
            dve.wait_ge(zeroed, 1)
            dve.wait_ge(q_out, KC)
            for h in range(HPC):
                r = slice(h * HD, (h + 1) * HD)
                for c in range(KC):
                    last = nc.vector.tensor_copy(q_blk[r, c, h // 2, :, (h % 2) * LAT:(h % 2 + 1) * LAT],
                                                 qT[r, c, :].rearrange("p (b n) -> p b n", b=B))
            last.then_inc(blk_ready, 1)
            for u in range(PAIRS):
                dve.wait_ge(scored, u + 1)
                s = banks[u][:].rearrange("p (b n) -> p b n", b=B)
                nc.vector.reduce_max(nmx[:, u], s, AX.X, negate=True).then_inc(max_ready, 1)
                dve.wait_ge(max_ready, u + 1)
                nc.vector.tensor_tensor(dif[:, u], s, nmx[:, u].unsqueeze(2).broadcast_to([P, B, LAT]), ALU.add
                                        ).then_inc(dif_ready, 1)
            for u in range(PAIRS):
                dve.wait_ge(exp_done, u + 1)
                nc.vector.reduce_sum(rs[:, u], prob[:, u], AX.X).then_inc(sum_ready, 1)
                dve.wait_ge(sum_ready, u + 1)
                nc.vector.reciprocal(ri[:, u], rs[:, u]).then_inc(inv_ready, 1)
                dve.wait_ge(inv_ready, u + 1)
                nc.vector.tensor_tensor(prob[:, u], prob[:, u], ri[:, u].unsqueeze(2).broadcast_to([P, B, LAT]),
                                        ALU.mult).then_inc(prob_ready, 1)
            dve.wait_ge(w_in["bv"], 16)
            for n in range(4 * KC):
                c, half, par = n // 4, (n // 2) % 2, n % 2
                dve.wait_ge(weighed, n + 1)
                s = banks[n % 8][:].rearrange("p (t h n) -> p t h n", t=2, h=HPC)
                o = oT[:, c, :].rearrange("p (t r n) -> p t r n", t=TC, r=2)
                for h in range(HPC):
                    r = slice(h * HD, (h + 1) * HD)
                    last = nc.vector.tensor_scalar(o[r, 2 * half:2 * half + 2, par, :], s[r, :, h, :],
                                                   bv[r, c:c + 1], None, ALU.add)
                last.then_inc(o_out, 1)
            dve.wait_ge(w_in["bo"], 16)
            for t in range(TC):
                nc.vector.tensor_tensor(x[:, t, :], x[:, t, :], bo[:], ALU.add).then_inc(biased, 1)
            for t in range(TC):
                dve.wait_ge(o_mm, t + 1)
                dve.wait_ge(biased, t + 1)
                nc.vector.tensor_tensor(x[:, t, :], x[:, t, :], banks[t][:], ALU.add).then_inc(out, 1)

        @block.tensor
        def _(pe):
            pe.wait_ge(norm.done, TC)
            for c in range(KC):
                transpose_rows(nc, banks[c], xn, c, ident).then_inc(turned, 1)
            pe.wait_ge(turned_out, KC)
            pe.wait_ge(w_in["wl"], 16)
            product(nc, banks[4][:], [(wl[:, k, :], xnT[:, k, :]) for k in range(KC)]).then_inc(l_mm, 1)
            pe.wait_ge(w_in["wq"], 16)
            for c in range(KC):
                product(nc, banks[(5 + c) % 8][:], [(wq[:, k, c * P:(c + 1) * P], xnT[:, k, :]) for k in range(KC)]
                        ).then_inc(q_mm, 1)
            pe.wait_ge(l_out, 1)
            pe.wait_ge(q_out, KC)
            pe.wait_ge(w_in["wk"], 16)
            for c in range(KC):
                product(nc, banks[c][:], [(wk[:, c * P:(c + 1) * P], lT[:])]).then_inc(k_mm, 1)
            pe.wait_ge(w_in["wv"], 16)
            for t in range(TC):
                product(nc, banks[4 + t][:], [(lT[:, t * P:(t + 1) * P], wv[:])]).then_inc(v_mm, 1)
            pe.wait_ge(blk_ready, 1)
            pe.wait_ge(k_out, KC)
            for u in range(PAIRS):
                if u == 4:
                    pe.wait_ge(v_out, TC)
                for b in range(B):
                    last = product(nc, banks[u][:, b * LAT:(b + 1) * LAT],
                                   [(q_blk[:, u // 2, u % 2, b, :], kT[:, u // 2, b * LAT:(b + 1) * LAT])])
                last.then_inc(scored, 1)
            for u in range(PAIRS):
                pe.wait_ge(exp_done, u + 1)
                pe.wait_ge(prob_ready, u + 1)
                for t in range(TC):
                    last = nc.tensor.transpose(banks[u][:, t * P:(t + 1) * P],
                                               prob[:, u, 2 * t:2 * t + 2, :].rearrange("p b n -> p (b n)"), ident[:])
                last.then_inc(p_turned, 1)
            pe.wait_ge(pt_out, PAIRS)
            for n in range(4 * KC):
                c, half, par = n // 4, (n // 2) % 2, n % 2
                if n >= 8:
                    pe.wait_ge(o_out, n - 7)
                r = slice(par * LAT, (par + 1) * LAT)
                for j in range(2):
                    t = 2 * half + j
                    last = product(nc, banks[n % 8][:, j * 2 * P:(j + 1) * 2 * P],
                                   [(v[r, t, c * P:(c + 1) * P], pt[r, 2 * c:2 * c + 2, t, :])])
                last.then_inc(weighed, 1)
            pe.wait_ge(o_out, 4 * KC)
            pe.wait_ge(w_in["wo"], 16)
            for t in range(TC):
                product(nc, banks[t][:], [(oT[:, c, t * P:(t + 1) * P], wo[:, c, :]) for c in range(KC)]
                        ).then_inc(o_mm, 1)


def phase_rows(nc, dram, ident, x, y1):
    NH, SC = KC, P ** -0.5
    with ExitStack() as ctx:
        sc = Scope(nc, ctx, "row")
        xn = sc.sb("xn", [P, TC, D])
        xnT = sc.sb("xnT", [P, KC, T])
        w, wo = sc.sb("w", [P, KC, 3 * D]), sc.sb("wo", [P, KC, D])
        bc = sc.sb("bc", [P, 3 * KC])
        bqs = sc.sb("bqs", [P, KC])
        bo, g, bb = sc.sb("bo", [P, D]), sc.sb("g", [P, D]), sc.sb("bb", [P, D])
        same = sc.sb("same", [P, LAT])
        qT, kT, v = sc.sb("qT", [P, NH, T]), sc.sb("kT", [P, NH, T]), sc.sb("v", [P, TC, D])
        cut = sc.sb("cut", [P, 2, T])
        N = NH * TC
        s8, d8, e8, p8 = (sc.sb(n, [P, N, B]) for n in ("s8", "d8", "e8", "p8"))
        nm8, sm8, iv8 = (sc.sb(n, [P, N]) for n in ("nm8", "sm8", "iv8"))
        full = sc.sb("full", [P, 2, TC, T])
        pt = sc.sb("pt", [P, 2, TC, T])
        oT = sc.sb("oT", [P, NH, T])
        r = sc.sb("r", [P, TC, D])
        rn = sc.sb("rn", [P, TC, D])
        norm, norm1 = Norm(sc, "ln"), Norm(sc, "ln1")
        banks = [sc.ps(f"bank{i}", [P, T]) for i in range(8)]
        w_in, bc_in, wo_in, same_in = sc.sem("w_in"), sc.sem("bc_in"), sc.sem("wo_in"), sc.sem("same_in")
        bo_in, g_in, bb_in = sc.sem("bo_in"), sc.sem("g_in"), sc.sem("bb_in")
        turned, turned_out = sc.sem("turned"), sc.sem("turned_out")
        bqs_ready, mm, q_out, k_out, v_out = (sc.sem(n) for n in ("bqs_ready", "mm", "q_out", "k_out", "v_out"))
        scored, cut_ready, picked, step = (sc.sem(n) for n in ("scored", "cut_ready", "picked", "step"))
        d_ready, e_ready, spread, p_turned, pt_out = (sc.sem(n) for n in ("d_ready", "e_ready", "spread", "p_turned",
                                                                          "pt_out"))
        weighed, o_out, biased, o_mm, r_ready = (sc.sem(n) for n in ("weighed", "o_out", "biased", "o_mm", "r_ready"))
        geared = sc.sem("geared")
        block = ctx.enter_context(nc.Block())
        by_batch = lambda a: a.rearrange("p (b n) -> p b n", b=B)
        same_all = same[:].unsqueeze(1).broadcast_to([P, B, LAT])

        @block.sync
        def _(sp):
            sp.dma_start(bc[:], dram["L1_ffn_in_proj_b"]).then_inc(bc_in, 16)
            sp.dma_start(same[:], dram["same_latent"]).then_inc(same_in, 16)
            sp.dma_start(w[:], dram["L1_ffn_in_proj_w"]).then_inc(w_in, 16)
            sp.dma_start(wo[:], dram["L1_ffn_out_proj_w"]).then_inc(wo_in, 16)
            sp.dma_start(bo[:], dram["L1_ffn_out_proj_b"].partition_broadcast(P)).then_inc(bo_in, 16)
            sp.dma_start(g[:], dram["L1_ffn_ln1_g"].partition_broadcast(P)).then_inc(g_in, 16)
            sp.dma_start(bb[:], dram["L1_ffn_ln1_b"].partition_broadcast(P)).then_inc(bb_in, 16)

        @block.scalar
        def _(act):
            norm.scalar(nc, act)
            for c in range(KC):
                act.wait_ge(turned, c + 1)
                nc.scalar.activation(xnT[:, c, :], banks[c][:], ACT.Copy).then_inc(turned_out, 1)
            act.wait_ge(bc_in, 16)
            for h in range(NH):
                act.wait_ge(mm, h + 1)
                nc.scalar.activation(kT[:, h, :], banks[4 + h][:], ACT.Identity, bias=bc[:, KC + h:KC + h + 1]
                                     ).then_inc(k_out, 1)
            for t in range(TC):
                act.wait_ge(mm, 2 * NH + t + 1)
                nc.scalar.activation(v[:, t, :], banks[4 + t][:], ACT.Copy).then_inc(v_out, 1)
            act.wait_ge(d_ready, 1)
            nc.scalar.activation(e8[:], d8[:], ACT.Exp).then_inc(e_ready, 1)
            for h in range(NH):
                if h >= 2:
                    act.wait_ge(weighed, h - 1)
                for k in range(TC):
                    act.wait_ge(p_turned, TC * h + k + 1)
                    nc.scalar.activation(pt[:, h % 2, k, :], banks[k][:], ACT.Copy).then_inc(pt_out, 1)
                act.wait_ge(weighed, h + 1)
                nc.scalar.activation(oT[:, h, :], banks[4 + h % 2][:], ACT.Identity,
                                     bias=bc[:, 2 * KC + h:2 * KC + h + 1]).then_inc(o_out, 1)
            norm1.scalar(nc, act)

        @block.vector
        def _(dve):
            norm.vector(nc, dve, x, xn)
            dve.wait_ge(bc_in, 16)
            for h in range(NH):
                dve.wait_ge(mm, NH + h + 1)
                nc.vector.tensor_scalar(qT[:, h, :], banks[h][:], bc[:, h:h + 1], SC, ALU.add, ALU.mult
                                        ).then_inc(q_out, 1)
            dve.wait_ge(same_in, 16)
            for n in range(N):
                dve.wait_ge(scored, n + 1)
                nc.vector.tensor_tensor(by_batch(cut[:, n % 2, :]), by_batch(banks[n % 4][:]), same_all, ALU.mult
                                        ).then_inc(cut_ready, 1)
                dve.wait_ge(cut_ready, n + 1)
                nc.vector.reduce_sum(s8[:, n, :], by_batch(cut[:, n % 2, :]), AX.X).then_inc(picked, 1)
            dve.wait_ge(picked, N)
            wide = lambda a: a[:].unsqueeze(2).broadcast_to([P, N, B])
            nc.vector.reduce_max(nm8[:], s8[:], AX.X, negate=True).then_inc(step, 1)
            dve.wait_ge(step, 1)
            nc.vector.tensor_tensor(d8[:], s8[:], wide(nm8), ALU.add).then_inc(d_ready, 1)
            dve.wait_ge(e_ready, 1)
            nc.vector.reduce_sum(sm8[:], e8[:], AX.X).then_inc(step, 1)
            dve.wait_ge(step, 2)
            nc.vector.reciprocal(iv8[:], sm8[:]).then_inc(step, 1)
            dve.wait_ge(step, 3)
            nc.vector.tensor_tensor(p8[:], e8[:], wide(iv8), ALU.mult).then_inc(step, 1)
            dve.wait_ge(step, 4)
            for h in range(NH):
                if h >= 2:
                    dve.wait_ge(p_turned, TC * (h - 1))
                for t in range(TC):
                    nc.vector.tensor_tensor(by_batch(full[:, h % 2, t, :]),
                                            p8[:, h * TC + t, :].unsqueeze(2).broadcast_to([P, B, LAT]), same_all,
                                            ALU.mult).then_inc(spread, 1)
            dve.wait_ge(bo_in, 16)
            for t in range(TC):
                nc.vector.tensor_tensor(xn[:, t, :], xn[:, t, :], bo[:], ALU.add).then_inc(biased, 1)
            for t in range(TC):
                dve.wait_ge(o_mm, t + 1)
                dve.wait_ge(biased, t + 1)
                nc.vector.tensor_tensor(r[:, t, :], xn[:, t, :], banks[t][:], ALU.add).then_inc(r_ready, 1)
            dve.wait_ge(r_ready, TC)
            norm1.vector(nc, dve, r, rn)
            dve.wait_ge(norm1.done, TC)
            dve.wait_ge(g_in, 16)
            dve.wait_ge(bb_in, 16)
            for t in range(TC):
                nc.vector.tensor_tensor(rn[:, t, :], rn[:, t, :], g[:], ALU.mult).then_inc(geared, 1)
            for t in range(TC):
                dve.wait_ge(geared, t + 1)
                nc.vector.tensor_tensor(y1[:, t, :], rn[:, t, :], bb[:], ALU.add)

        @block.tensor
        def _(pe):
            pe.wait_ge(norm.done, TC)
            for c in range(KC):
                transpose_rows(nc, banks[c], xn, c, ident).then_inc(turned, 1)
            pe.wait_ge(turned_out, KC)
            pe.wait_ge(w_in, 16)
            for h in range(NH):
                o = D + h * P
                product(nc, banks[4 + h][:], [(w[:, k, o:o + P], xnT[:, k, :]) for k in range(KC)]).then_inc(mm, 1)
            for h in range(NH):
                o = h * P
                product(nc, banks[h][:], [(w[:, k, o:o + P], xnT[:, k, :]) for k in range(KC)]).then_inc(mm, 1)
            pe.wait_ge(k_out, NH)
            for t in range(TC):
                product(nc, banks[4 + t][:], [(xnT[:, k, t * P:(t + 1) * P], w[:, k, 2 * D:3 * D]) for k in range(KC)]
                        ).then_inc(mm, 1)
            pe.wait_ge(q_out, NH)
            for n in range(N):
                h, t = n // TC, n % TC
                if n >= 4:
                    pe.wait_ge(cut_ready, n - 3)
                product(nc, banks[n % 4][:], [(qT[:, h, t * P:(t + 1) * P], kT[:, h, :])]).then_inc(scored, 1)
            pe.wait_ge(v_out, TC)
            pe.wait_ge(cut_ready, N)
            for h in range(NH):
                pe.wait_ge(spread, TC * (h + 1))
                for k in range(TC):
                    if h:
                        pe.wait_ge(pt_out, TC * (h - 1) + k + 1)
                    for t in range(TC):
                        last = nc.tensor.transpose(banks[k][:, t * P:(t + 1) * P],
                                                   full[:, h % 2, t, k * P:(k + 1) * P], ident[:])
                    last.then_inc(p_turned, 1)
                pe.wait_ge(pt_out, TC * (h + 1))
                if h >= 2:
                    pe.wait_ge(o_out, h - 1)
                product(nc, banks[4 + h % 2][:], [(v[:, k, h * P:(h + 1) * P], pt[:, h % 2, k, :])
                                                  for k in range(TC)]).then_inc(weighed, 1)
            pe.wait_ge(o_out, NH)
            pe.wait_ge(wo_in, 16)
            for t in range(TC):
                product(nc, banks[t][:], [(oT[:, h, t * P:(t + 1) * P], wo[:, h, :]) for h in range(NH)]
                        ).then_inc(o_mm, 1)


def phase_dispatch(nc, dram, ident, x, y1):
    with ExitStack() as ctx:
        sc = Scope(nc, ctx, "dsp")
        w1 = [sc.sb(f"w1_{i}", [P, KC, FF]) for i in range(2)]
        w2 = [sc.sb(f"w2_{i}", [P, FC, D]) for i in range(2)]
        b1 = sc.sb("b1", [P, E0 // 2, FC, 2])
        b2 = sc.sb("b2", [P, E0 // 2, D])
        dT = sc.sb("dT", [P, KC, T])
        hot = sc.sb("hot", [P, TC, T])
        hotT = sc.sb("hotT", [P, TC, T])
        gate = sc.sb("gate", [P, TC])
        w1_in = [sc.sem(f"w1_in{i}") for i in range(2)]
        w2_in = [sc.sem(f"w2_in{i}") for i in range(2)]
        b1_in, b2_in = sc.sem("b1_in"), sc.sem("b2_in")
        W1, W2 = dram["L1_ffn_w1"], dram["L1_ffn_w2"]
        with ExitStack() as c1:
            s1 = Scope(nc, c1, "dsr")
            wg = s1.sb("wg", [P, KC, E0])
            before, ones = s1.sb("before", [P, P]), s1.sb("ones", [P, P])
            slots = s1.sb("slots", [P, T])
            first = s1.sb("first", [P, TC, E0])
            cnt, cm, at = (s1.sb(n, [P, TC, E0]) for n in ("cnt", "cm", "at"))
            loc, pos, over, slot = (s1.sb(n, [P, TC]) for n in ("loc", "pos", "over", "slot"))
            rt = Route(s1, dram)
            banks = [s1.ps(f"bank{i}", [P, T]) for i in range(8)]
            c_in, ones_ready = s1.sem("c_in"), s1.sem("ones_ready")
            turned, turned_out, routed, counted = (s1.sem(n) for n in ("turned", "turned_out", "routed", "counted"))
            step, hot_ready, moved, moved_out = (s1.sem(n) for n in ("step", "hot_ready", "moved", "moved_out"))
            hot_turned, hot_out = s1.sem("hot_turned"), s1.sem("hot_out")
            block = c1.enter_context(nc.Block())

            @block.sync
            def _(sp):
                sp.dma_start(wg[:], dram["L1_ffn_wg"]).then_inc(c_in, 16)
                rt.sync(sp)
                sp.dma_start(before[:], dram["before"]).then_inc(c_in, 16)
                sp.dma_start(slots[:], dram["slots"].partition_broadcast(P)).then_inc(c_in, 16)
                sp.dma_start(first[:], dram["first_slot"].partition_broadcast(P)).then_inc(c_in, 16)
                for i in range(2):
                    sp.dma_start(w1[i][:], W1[i]).then_inc(w1_in[i], 16)
                    sp.dma_start(w2[i][:], W2[i]).then_inc(w2_in[i], 16)
                sp.dma_start(b1[:], dram["L1_ffn_b1"]).then_inc(b1_in, 16)
                for i in range(2):
                    sp.dma_start(b2[i * CAP:(i + 1) * CAP],
                                 dram["L1_ffn_b2"].rearrange("(j r) d -> r j d", r=2)[i].partition_broadcast(CAP)
                                 ).then_inc(b2_in, 16)

            @block.gpsimd
            def _(pool):
                nc.gpsimd.memset(ones[:], 1.0).then_inc(ones_ready, 1)

            @block.scalar
            def _(act):
                for c in range(KC):
                    act.wait_ge(turned, c + 1)
                    nc.scalar.activation(dT[:, c, :], banks[c][:], ACT.Copy).then_inc(turned_out, 1)
                rt.scalar(nc, act)
                for c in range(TC):
                    act.wait_ge(hot_turned, c + 1)
                    nc.scalar.activation(hotT[:, c, :], banks[c][:], ACT.Copy).then_inc(hot_out, 1)

            @block.vector
            def _(dve):
                dve.wait_ge(routed, 1)
                rt.vector(nc, dve, banks[4][:, 0:TC * E0].rearrange("p (t e) -> p t e", t=TC))
                n = [0]

                def step_(ins):
                    n[0] += 1
                    ins.then_inc(step, 1)
                    dve.wait_ge(step, n[0])

                dve.wait_ge(c_in, 64)
                dve.wait_ge(counted, 1)
                step_(nc.vector.tensor_copy(cnt[:], banks[5][:, 0:TC * E0].rearrange("p (t e) -> p t e", t=TC)))
                step_(nc.vector.tensor_tensor(cm[:], cnt[:], rt.mask[:], ALU.mult))
                step_(nc.vector.reduce_sum(loc[:], cm[:], AX.X))
                step_(nc.vector.tensor_tensor(at[:], first[:], rt.mask[:], ALU.mult))
                step_(nc.vector.reduce_sum(pos[:], at[:], AX.X))
                step_(nc.vector.tensor_scalar(over[:], loc[:], float(CAP), float(4 * T), ALU.is_ge, ALU.mult))
                step_(nc.vector.tensor_tensor(pos[:], pos[:], loc[:], ALU.add))
                step_(nc.vector.tensor_tensor(slot[:], pos[:], over[:], ALU.add))
                step_(nc.vector.tensor_copy(gate[:], rt.gate[:]))
                for t in range(TC):
                    nc.vector.tensor_scalar(hot[:, t, :], slots[:], slot[:, t:t + 1], None, ALU.is_equal
                                            ).then_inc(hot_ready, 1)
                for c in range(KC):
                    dve.wait_ge(moved, c + 1)
                    nc.vector.tensor_copy(dT[:, c, :], banks[4 + c][:]).then_inc(moved_out, 1)

            @block.tensor
            def _(pe):
                for c in range(KC):
                    transpose_rows(nc, banks[c], y1, c, ident).then_inc(turned, 1)
                pe.wait_ge(turned_out, KC)
                pe.wait_ge(c_in, 64)
                for t in range(TC):
                    last = product(nc, banks[4][:, t * E0:(t + 1) * E0],
                                   [(dT[:, k, t * P:(t + 1) * P], wg[:, k, :]) for k in range(KC)])
                last.then_inc(routed, 1)
                pe.wait_ge(rt.done, 1)
                pe.wait_ge(ones_ready, 1)
                for t in range(TC):
                    last = product(nc, banks[5][:, t * E0:(t + 1) * E0],
                                   [(ones[:], rt.mask[:, s, :]) for s in range(t)] + [(before[:], rt.mask[:, t, :])])
                last.then_inc(counted, 1)
                pe.wait_ge(hot_ready, TC)
                for c in range(KC):
                    product(nc, banks[4 + c][:], [(y1[:, t, c * P:(c + 1) * P], hot[:, t, :]) for t in range(TC)]
                            ).then_inc(moved, 1)
                for c in range(TC):
                    transpose_rows(nc, banks[c], hot, c, ident).then_inc(hot_turned, 1)

        with ExitStack() as c2:
            s2 = Scope(nc, c2, "dse")
            ds_ = s2.sb("ds", [P, KC, P])
            hr = hot[:].rearrange("p t s -> p (t s)")
            hT = s2.sb("hT", [P, FC, P])
            ys = s2.sb("ys", [P, E0 // 2, D])
            mixed, rn = w1[0][:, 0, :].rearrange("p (t d) -> p t d", t=TC), w1[0][:, 1, :].rearrange("p (t d) -> p t d", t=TC)
            g, bb = s2.sb("g", [P, D]), s2.sb("bb", [P, D])
            norm2 = Norm(s2, "ln2")
            g_in, bb_in, back, r_ready, geared, out = (s2.sem(n) for n in ("g_in", "bb_in", "back", "r_ready",
                                                                           "geared", "out"))
            NB = FF // 512
            hb = [s2.ps(f"hb{i}", [P, 512]) for i in range(NB)]
            tb = [s2.ps(f"tb{i}", [P, 512]) for i in range(3)]
            yb = s2.ps("yb", [P, D])
            ds_ready, h_mm, h_out = s2.sem("ds_ready"), s2.sem("h_mm"), s2.sem("h_out")
            h_turned, hT_out, y_mm, y_out = (s2.sem(n) for n in ("h_turned", "hT_out", "y_mm", "y_out"))
            both = [slice(i * CAP, (i + 1) * CAP) for i in range(2)]
            block = c2.enter_context(nc.Block())

            @block.sync
            def _(sp):
                sp.dma_start(g[:], dram["L1_ffn_ln2_g"].partition_broadcast(P)).then_inc(g_in, 16)
                sp.dma_start(bb[:], dram["L1_ffn_ln2_b"].partition_broadcast(P)).then_inc(bb_in, 16)
                with sp.Fori(0, E0 // 2 - 1) as j:
                    sp.wait_ge(h_mm, NB * j + NB)
                    for i in range(2):
                        sp.dma_start(w1[i][:], W1[2 * j + 2 + i]).then_inc(w1_in[i], 16)
                    sp.wait_ge(y_mm, j + 1)
                    for i in range(2):
                        sp.dma_start(w2[i][:], W2[2 * j + 2 + i]).then_inc(w2_in[i], 16)

            @block.scalar
            def _(act):
                with act.Fori(0, E0 // 2) as j:
                    for q in range(NB):
                        act.wait_ge(h_mm, NB * j + q + 1)
                        nc.scalar.activation(hr[:, q * 512:(q + 1) * 512], hb[q][:], ACT.Copy).then_inc(h_out, 1)
                norm2.scalar(nc, act)

            @block.vector
            def _(dve):
                dve.sem_inc(y_out, 1)
                dve.sem_inc(hT_out, 1)
                dve.wait_ge(b1_in, 16)
                dve.wait_ge(b2_in, 32)
                with dve.Fori(0, E0 // 2) as j:
                    nc.vector.tensor_copy(ds_[:], dT[:, :, bass.ds(P * j, P)]).then_inc(ds_ready, 1)
                    for q in range(NB):
                        dve.wait_ge(h_turned, NB * j + q + 1)
                        fs = slice(4 * q, 4 * q + 4)
                        nc.vector.tensor_tensor(
                            hT[:, fs, :].rearrange("p f (i c) -> p f i c", i=2),
                            tb[q % 3][:].rearrange("p (f i c) -> p f i c", f=4, i=2),
                            b1[:, bass.ds(j, 1), fs, :].rearrange("p o f i -> p (o f) i").unsqueeze(3)
                            .broadcast_to([P, 4, 2, CAP]), ALU.add).then_inc(hT_out, 1)
                    dve.wait_ge(y_mm, j + 1)
                    nc.vector.tensor_tensor(ys[:, bass.ds(j, 1), :], yb[:].unsqueeze(1), b2[:, bass.ds(j, 1), :],
                                            ALU.add).then_inc(y_out, 1)
                for t in range(TC):
                    dve.wait_ge(back, t + 1)
                    nc.vector.scalar_tensor_tensor(mixed[:, t, :], hb[t][:], gate[:, t:t + 1], y1[:, t, :],
                                                   ALU.mult, ALU.add).then_inc(r_ready, 1)
                dve.wait_ge(r_ready, TC)
                norm2.vector(nc, dve, mixed, rn)
                dve.wait_ge(norm2.done, TC)
                dve.wait_ge(g_in, 16)
                dve.wait_ge(bb_in, 16)
                for t in range(TC):
                    nc.vector.tensor_tensor(rn[:, t, :], rn[:, t, :], g[:], ALU.mult).then_inc(geared, 1)
                for t in range(TC):
                    dve.wait_ge(geared, t + 1)
                    nc.vector.tensor_tensor(rn[:, t, :], rn[:, t, :], bb[:], ALU.add).then_inc(geared, 1)
                for t in range(TC):
                    dve.wait_ge(geared, TC + t + 1)
                    nc.vector.tensor_tensor(x[:, t, :], x[:, t, :], rn[:, t, :], ALU.add).then_inc(out, 1)

            @block.tensor
            def _(pe):
                with pe.Fori(0, E0 // 2) as j:
                    pe.wait_ge(ds_ready, j + 1)
                    for i in range(2):
                        pe.wait_ge(w1_in[i], 16 * j + 16)
                    for q in range(NB):
                        for k in range(KC):
                            for r, w in zip(both, w1):
                                last = nc.tensor.matmul(hb[q][r, :], ds_[:, k, r], w[:, k, q * 512:(q + 1) * 512],
                                                        start=(k == 0), stop=(k == KC - 1))
                        last.then_inc(h_mm, 1)
                    for q in range(NB):
                        pe.wait_ge(h_out, NB * j + q + 1)
                        pe.wait_ge(hT_out, NB * j + max(0, q - 3) + 1 + (1 if q == 3 else 0))
                        for c in range(4):
                            f = 4 * q + c
                            last = nc.tensor.transpose(tb[q % 3][:, c * P:(c + 1) * P], hr[:, f * P:(f + 1) * P],
                                                       ident[:])
                        last.then_inc(h_turned, 1)
                    for i in range(2):
                        pe.wait_ge(w2_in[i], 16 * j + 16)
                    pe.wait_ge(y_out, j + 1)
                    for f in range(FC):
                        if f % 4 == 0:
                            pe.wait_ge(hT_out, NB * j + f // 4 + 2)
                        for r, w in zip(both, w2):
                            last = nc.tensor.matmul(yb[r, :], hT[:, f, r], w[:, f, :], start=(f == 0),
                                                    stop=(f == FC - 1))
                    last.then_inc(y_mm, 1)
                pe.wait_ge(y_out, E0 // 2 + 1)
                for t in range(TC):
                    product(nc, hb[t][:], [(hotT[:, c, t * P:(t + 1) * P], ys[:, c, :]) for c in range(TC)]
                            ).then_inc(back, 1)


def phase_block(nc, dram, ident, x):
    with ExitStack() as ctx:
        y1 = ctx.enter_context(nc.sbuf_tensor("y1", [P, TC, D], F32))
        phase_rows(nc, dram, ident, x, y1)
        phase_dispatch(nc, dram, ident, x, y1)


def rest(nc, dram, ident, x):
    with ExitStack() as ctx:
        ahead = ContextAhead(Scope(nc, ctx, "ahead"), dram)
        phase_scan(nc, dram, ident, x, ahead)
        phase_experts(nc, dram, ident, x)
        phase_context(nc, dram, ident, x, ahead)
    phase_latent(nc, dram, ident, x)
    phase_block(nc, dram, ident, x)


def lay_rest(n, put, rows, cols):
    import numpy as np
    ctx = n["ctx_1024"]
    put["ctxR"] = ctx[:, :P * (NCH - 1)].reshape(B, NCH - 1, P, D).transpose(0, 2, 1, 3)
    put["ctxL"] = ctx[:, P * (NCH - 1):]
    put["rank"] = np.tile(np.arange(E0, 0, -1, dtype=np.float32), (TC, 1))
    put["L0_attn_W_qkva"] = rows(n["L0_attn_W_qkva"].T)
    put["L0_attn_gamma"] = cols(n["L0_attn_gamma"])
    put["L0_ffn_router_w"] = rows(n["L0_ffn_router_w"])
    put["L0_ffn_router_b"] = n["L0_ffn_router_b"]
    put["L0_ffn_expert_b"] = n["L0_ffn_expert_b"]
    put["L0_ffn_expert_w"] = n["L0_ffn_expert_w"].reshape(E0, KC, P, D).transpose(0, 2, 1, 3)
    put["L1_xattn_Wq"] = rows(n["L1_xattn_Wq"].T)
    put["L1_xattn_Wk"] = rows(n["L1_xattn_Wk"])
    put["L1_xattn_Wv"] = rows(n["L1_xattn_Wv"].T)
    put["L1_xattn_Wo"] = rows(n["L1_xattn_Wo"].T)
    put["L1_xattn_bq"] = cols(n["L1_xattn_bq"])
    put["L1_xattn_bv"] = cols(n["L1_xattn_bv"])
    put["L1_xattn_bo"] = n["L1_xattn_bo"]
    put["L1_attn_Wq"] = rows(n["L1_attn_Wq"])
    put["L1_attn_Wl"] = rows(n["L1_attn_Wl"])
    put["L1_attn_Wk"] = n["L1_attn_Wk"]
    put["L1_attn_Wv"] = n["L1_attn_Wv"]
    put["L1_attn_Wo"] = rows(n["L1_attn_Wo"])
    for k in ("bq", "bl", "bk", "bv"):
        put[f"L1_attn_{k}"] = cols(n[f"L1_attn_{k}"])
    put["L1_attn_bo"] = n["L1_attn_bo"]
    put["L1_ffn_in_proj_w"] = rows(n["L1_ffn_in_proj_w"].T)
    put["L1_ffn_in_proj_b"] = cols(n["L1_ffn_in_proj_b"])
    put["L1_ffn_in_proj_bv"] = n["L1_ffn_in_proj_b"][2 * D:]
    put["L1_ffn_out_proj_w"] = rows(n["L1_ffn_out_proj_w"].T)
    for k in ("out_proj_b", "ln1_g", "ln1_b", "ln2_g", "ln2_b"):
        put[f"L1_ffn_{k}"] = n[f"L1_ffn_{k}"]
    put["L1_ffn_wg"] = rows(n["L1_ffn_wg"])
    put["L1_ffn_w1"] = n["L1_ffn_w1"].reshape(E0, KC, P, FF).transpose(0, 2, 1, 3)
    put["L1_ffn_w2"] = n["L1_ffn_w2"].reshape(E0, FC, P, D).transpose(0, 2, 1, 3)
    put["L1_ffn_b1"] = n["L1_ffn_b1"].reshape(E0 // 2, 2, FC, P).transpose(3, 0, 2, 1)
    put["L1_ffn_b2"] = n["L1_ffn_b2"]
    at = np.arange(T)
    put["same_latent"] = (np.arange(LAT)[None, :] == (np.arange(P) % LAT)[:, None]).astype(np.float32)
    put["before"] = (np.arange(P)[:, None] < np.arange(P)[None, :]).astype(np.float32)
    put["slots"] = at.astype(np.float32)
    put["first_slot"] = np.tile(np.arange(0, T, CAP, dtype=np.float32), (TC, 1))


def store_rows(nc, dst, rows):
    with ExitStack() as ctx:
        sc = Scope(nc, ctx, "sto")
        stored = sc.sem("stored")
        block = ctx.enter_context(nc.Block())

        @block.sync
        def _(sp):
            sp.dma_start(dst.rearrange("(t p) d -> p t d", p=P), rows[:]).then_inc(stored, 16)
            sp.wait_ge(stored, 16)


def build(nc, dram, out):
    with ExitStack() as whole:
        keep = Scope(nc, whole, "all")
        ident = keep.sb("ident", [P, P])
        oT = keep.sb("oT", [P, KC, T])
        res = {"ident": ident, "oT": oT}
        with ExitStack() as attn:
            at = Scope(nc, attn, "crossin")
            res["qT"] = at.sb("qT", [P, KC, T])
            res["w_hi"] = at.sb("w_hi", [P, 2, KC, D], F32R)
            res["w_lo"] = at.sb("w_lo", [P, 2, KC, D], F32R)
            res["q_blk_hi"] = at.sb("q_blk_hi", [P, KC, 2, P], F32R)
            res["q_blk_lo"] = at.sb("q_blk_lo", [P, KC, 2, P], F32R)
            res["bk"] = at.sb("bk", [P, KC])
            res["ct_hi"] = at.sb("ct_hi", [P, KC, KPAD], F32R)
            res["ct_lo"] = at.sb("ct_lo", [P, KC, KPAD], F32R)
            phase_queries(nc, dram, res)
            phase_cross(nc, dram, res)
        x = res["x"] = keep.sb("x", [P, TC, D])
        phase_cross_out(nc, dram, res)
        rest(nc, dram, ident, x)
        store_rows(nc, out, x)


def kernel(**inputs):
    import numpy as np
    import concourse.bacc as bacc
    from concourse.bass_utils import run_bass_kernel_spmd

    arrays = {}

    def rows(w):
        k, n = w.shape
        return w.reshape(k // P, P, n).transpose(1, 0, 2)

    def cols(v):
        return v.reshape(-1, P).T

    n = {k: np.asarray(v) for k, v in inputs.items()}
    put = dict(x=n["x"].reshape(T, D))
    ctxT = np.zeros((B, P, KC, KPAD), n["ctx_1024"].dtype)
    ctxT[..., :KEYS] = n["ctx_1024"].transpose(0, 2, 1).reshape(B, KC, P, KEYS).transpose(0, 2, 1, 3)
    put["ctxT"] = ctxT
    for k in ("L0_xattn_Wq", "L0_xattn_Wk", "L0_xattn_Wv", "L0_xattn_Wo"):
        put[k] = rows(n[k].T)
    for k in ("L0_xattn_bq", "L0_xattn_bk", "L0_xattn_bv"):
        put[k] = cols(n[k])
    put["L0_xattn_bo"] = n["L0_xattn_bo"]
    lay_rest(n, put, rows, cols)

    nc = bacc.Bacc("TRN2", target_bir_lowering=False, num_devices=1)
    dram = {}
    for name, a in put.items():
        a = np.ascontiguousarray(a)
        arrays[f"in_{name}"] = a
        dram[name] = nc.dram_tensor(f"in_{name}", a.shape, mybir.dt.from_np(a.dtype), kind="ExternalInput").ap()
    out = nc.dram_tensor("out_0", (T, D), F32, kind="ExternalOutput").ap()
    build(nc, dram, out)
    r = run_bass_kernel_spmd(nc, [arrays], core_ids=[0])
    return r.results[0]["out_0"].reshape(B, LAT, D)
```

```python
from contextlib import ExitStack

import concourse.bass as bass
from concourse import mybir

F32 = mybir.dt.float32
F32R = mybir.dt.float32r
ALU = mybir.AluOpType
ACT = mybir.ActivationFunctionType
AX = mybir.AxisListType

P = 128
D = 512
KC = D // P
B = 8
LAT = 64
T = B * LAT
TC = T // P
KEYS = 1601
KPAD = KEYS + 1
BANK = 512
GROUPS_N = -(-KPAD // BANK)
GW = KPAD // GROUPS_N // 2 * 2
GROUPS = [(g * GW, GW if g + 1 < GROUPS_N else KPAD - g * GW) for g in range(GROUPS_N)]
SW = GROUPS[-1][1]
CHUNKS = [(s, min(P, KEYS - s)) for s in range(0, KEYS, P)]
NCH = len(CHUNKS)
HEADS = 16
HD = D // HEADS
HPC = P // HD
PAIRS = HEADS // 2
E0 = 8
CAP = T // E0
FF = 2048
FC = FF // P
EPS = 1e-5


class Scope:

    def __init__(self, nc, ctx, name):
        self.nc, self.ctx, self.name = nc, ctx, name
        self.sems = []
        ctx.callback(self.close)

    def close(self):
        if self.sems:
            self.nc.clear_and_free_semaphores(self.sems)
            self.nc.all_engine_barrier()

    def sb(self, name, shape, dt=F32):
        return self.ctx.enter_context(self.nc.sbuf_tensor(f"{self.name}_{name}", shape, dt))

    def ps(self, name, shape, dt=F32):
        return self.ctx.enter_context(self.nc.psum_tensor(f"{self.name}_{name}", shape, dt))

    def sem(self, name):
        self.sems.append(self.nc.alloc_semaphore(name=f"{self.name}_{name}"))
        return self.sems[-1]


class Norm:

    def __init__(self, sc, tag):
        self.stats = sc.sb(f"{tag}_stats", [P, TC, 6])
        self.mv = sc.sb(f"{tag}_mv", [P, TC, 2])
        self.std = sc.sb(f"{tag}_std", [P, TC])
        self.rstd = sc.sb(f"{tag}_rstd", [P, TC])
        self.stats_ready = sc.sem(f"{tag}_stats_ready")
        self.var_ready = sc.sem(f"{tag}_var_ready")
        self.std_ready = sc.sem(f"{tag}_std_ready")
        self.rstd_ready = sc.sem(f"{tag}_rstd_ready")
        self.done = sc.sem(f"{tag}_done")

    def statistics(self, nc, dve, x):
        for t in range(TC):
            nc.vector.bn_stats(self.stats[:, t, :], x[:, t, :]).then_inc(self.stats_ready, 1)
        dve.wait_ge(self.stats_ready, TC)
        for t in range(TC):
            nc.vector.bn_aggr(self.mv[:, t, :], self.stats[:, t, :]).then_inc(self.stats_ready, 1)
        dve.wait_ge(self.stats_ready, 2 * TC)
        nc.vector.tensor_scalar(self.std[:], self.mv[:, :, 1], EPS, None, ALU.add).then_inc(self.var_ready, 1)
        dve.wait_ge(self.std_ready, 1)
        nc.vector.reciprocal(self.rstd[:], self.std[:]).then_inc(self.rstd_ready, 1)
        dve.wait_ge(self.rstd_ready, 1)

    def vector(self, nc, dve, x, xn):
        self.statistics(nc, dve, x)
        for t in range(TC):
            nc.vector.tensor_scalar(xn[:, t, :], x[:, t, :], self.mv[:, t, 0:1], self.rstd[:, t:t + 1],
                                    ALU.subtract, ALU.mult).then_inc(self.done, 1)

    def gear(self, nc, x, t, g):
        return nc.vector.scalar_tensor_tensor(x[:, t, :], x[:, t, :], self.mv[:, t, 0:1], g[:], ALU.subtract, ALU.mult)

    def finish(self, nc, out, x, t, add):
        return nc.vector.scalar_tensor_tensor(out, x[:, t, :], self.rstd[:, t:t + 1], add, ALU.mult, ALU.add)

    def scalar(self, nc, act):
        act.wait_ge(self.var_ready, 1)
        nc.scalar.activation(self.std[:], self.std[:], ACT.Sqrt).then_inc(self.std_ready, 1)


def transpose_rows(nc, out_bank, rows, c, ident):
    for t in range(TC):
        last = nc.tensor.transpose(out_bank[:, t * P:(t + 1) * P], rows[:, t, c * P:(c + 1) * P], ident[:])
    return last


def product(nc, out, pairs):
    for n, (lhsT, rhs) in enumerate(pairs):
        last = nc.tensor.matmul(out, lhsT, rhs, start=(n == 0), stop=(n == len(pairs) - 1))
    return last


def product3(nc, out, parts):
    n, N = 0, 3 * len(parts)
    for (ah, al), (bh, bl) in parts:
        for a, b in ((ah, bh), (ah, bl), (al, bh)):
            last = nc.tensor.matmul(out, a, b, start=(n == 0), stop=(n == N - 1))
            n += 1
    return last


def phase_queries(nc, dram, res):
    with ExitStack() as ctx:
        sc = Scope(nc, ctx, "qry")
        x = sc.sb("x", [P, TC, D])
        xn = sc.sb("xn", [P, TC, D])
        xnT = sc.sb("xnT", [P, KC, T])
        wq = sc.sb("wq", [P, KC, D])
        wkv = sc.sb("wkv", [P, 2, KC, D])
        bq = sc.sb("bq", [P, KC])
        ct = sc.sb("ct", [P, KC, KPAD])
        norm = Norm(sc, "ln")
        banks = [sc.ps(f"bank{i}", [P, T]) for i in range(2 * KC)]
        ct_in = [sc.sem(f"ct_in{g}") for g in range(len(GROUPS))]
        x_in, wq_in, bq_in, wkv_in = sc.sem("x_in"), sc.sem("wq_in"), sc.sem("bq_in"), sc.sem("wkv_in")
        bk_in = sc.sem("bk_in")
        ident0, ident_ready = sc.sem("ident0"), sc.sem("ident_ready")
        turned, turned_out, q_mm, q_out = sc.sem("turned"), sc.sem("turned_out"), sc.sem("q_mm"), sc.sem("q_out")
        w_hi, w_lo, ct_hi, ct_lo = (sc.sem(n) for n in ("w_hi", "w_lo", "ct_hi", "ct_lo"))
        block = ctx.enter_context(nc.Block())

        @block.sync
        def _(sp):
            sp.dma_start(x[:], dram["x"].rearrange("(t p) d -> p t d", p=P)).then_inc(x_in, 16)
            sp.dma_start(wq[:], dram["L0_xattn_Wq"]).then_inc(wq_in, 16)
            sp.dma_start(bq[:], dram["L0_xattn_bq"]).then_inc(bq_in, 16)
            sp.dma_start(res["bk"][:], dram["L0_xattn_bk"]).then_inc(bk_in, 16)
            sp.dma_start(wkv[:, 0], dram["L0_xattn_Wk"]).then_inc(wkv_in, 16)
            sp.dma_start(wkv[:, 1], dram["L0_xattn_Wv"]).then_inc(wkv_in, 16)
            for g, (s, w) in enumerate(GROUPS):
                sp.dma_start(ct[:, :, s:s + w], dram["ctxT"][0, :, :, s:s + w]).then_inc(ct_in[g], 16)
            sp.wait_ge(bk_in, 16)

        @block.gpsimd
        def _(pool):
            nc.gpsimd.memset(res["ident"][:], 0.0).then_inc(ident0, 1)
            pool.wait_ge(ident0, 1)
            nc.gpsimd.affine_select(out=res["ident"][:], in_=res["ident"][:], compare_op=ALU.not_equal, fill=1.0,
                                    base=0, pattern=[[-1, P]], channel_multiplier=1).then_inc(ident_ready, 1)
            nc.gpsimd.memset(res["q_blk_hi"][:].bitcast(F32), 0.0)
            nc.gpsimd.memset(res["q_blk_lo"][:].bitcast(F32), 0.0)
            for i in range(2):
                pool.wait_ge(w_hi, i + 1)
                nc.gpsimd.tensor_tensor(res["w_lo"][:, i], wkv[:, i], res["w_hi"][:, i].bitcast(F32),
                                        ALU.subtract).then_inc(w_lo, 1)

        @block.scalar
        def _(act):
            norm.scalar(nc, act)
            for c in range(KC):
                act.wait_ge(turned, c + 1)
                nc.scalar.activation(xnT[:, c, :], banks[c][:], ACT.Copy).then_inc(turned_out, 1)
            act.wait_ge(wkv_in, 32)
            for i in range(2):
                nc.scalar.activation(res["w_hi"][:, i], wkv[:, i], ACT.Copy).then_inc(w_hi, 1)
            for g, (s, w) in enumerate(GROUPS):
                act.wait_ge(ct_in[g], 16)
                nc.scalar.activation(res["ct_hi"][:, :, s:s + w], ct[:, :, s:s + w], ACT.Copy).then_inc(ct_hi, 1)

        @block.vector
        def _(dve):
            dve.wait_ge(x_in, 16)
            norm.vector(nc, dve, x, xn)
            dve.wait_ge(bq_in, 16)
            for o in range(KC):
                dve.wait_ge(q_mm, o + 1)
                nc.vector.tensor_scalar(res["qT"][:, o, :], banks[KC + o][:], bq[:, o:o + 1], HD ** -0.5,
                                        ALU.add, ALU.mult).then_inc(q_out, 1)
            for g, (s, w) in enumerate(GROUPS):
                dve.wait_ge(ct_hi, g + 1)
                nc.vector.tensor_tensor(res["ct_lo"][:, :, s:s + w], ct[:, :, s:s + w],
                                        res["ct_hi"][:, :, s:s + w].bitcast(F32), ALU.subtract).then_inc(ct_lo, 1)

        @block.tensor
        def _(pe):
            pe.wait_ge(ident_ready, 1)
            pe.wait_ge(norm.done, TC)
            for c in range(KC):
                transpose_rows(nc, banks[c], xn, c, res["ident"]).then_inc(turned, 1)
            pe.wait_ge(wq_in, 16)
            pe.wait_ge(turned_out, KC)
            for o in range(KC):
                product(nc, banks[KC + o][:], [(wq[:, k, o * P:(o + 1) * P], xnT[:, k, :]) for k in range(KC)]
                        ).then_inc(q_mm, 1)


V_SIZES = [2] * 6 + [1]


def order(text):
    uses = []
    for word in text.split():
        kind = word[0]
        at = [int(word[1:])] if kind == "c" else [int(a) for a in word[1:]]
        if kind == "v":
            half, n = at
            at = [half, sum(V_SIZES[:n]), V_SIZES[n]]
        uses.append((kind, *at))
    return uses


BODY = order("""
    s0 v00 e0 n0 v01 s1 v02 e1 u0 t00 v03 n1 t01 v04 t02 v05 u1 t10 v06 t11 k10 o0 k11 k12 k13 t12
    s2 o1 e2 n2 k20 k21 s3 u2 t20 e3 k22 t21 n3 k23 t22 k30 o2 t30 k31 u3 t31 k32 t32 k33
    s4 o3 e4 n4 v10 s5 v11 e5 u4 t40 c0 c1 v12 n5 t41 c2 c3 v13 t42 c4 c5 s6 v14 e6 u5 t50 c6 c7 v15 n6 t51
    c8 c9 v16 t52 s7 o4 e7 k40 c10 c11 u6 t60 n7 k41 c12 c13 o5 t61 c14 c15 k42 t62 u7 t70 t71 o6 q t72 k43 o7""")
BEFORE = order("k00 k01 k02 k03")
BANKED = [u for u in BEFORE + BODY if u[0] in "vkt"]
V_AT = {u[:3]: u for u in BANKED if u[0] == "v"}
USE = {u: n - len(BEFORE) for n, u in enumerate(BANKED)}
NUSE = len(BANKED) - len(BEFORE)
LAST = [u for u in BODY if u[0] not in "cq" and u[:2] != ("k", KC)]
LAST_USE = {u: n for n, u in enumerate(u for u in LAST if u[0] in "vkt")}
RING = 3
assert NUSE % RING == 0


NPIECE = KC * GROUPS_N
NSTAGE = 4


def piece(n):
    s, w = GROUPS[n // KC]
    return (slice(None), n % KC, slice(s, s + w)), w


START = 1


def phase_cross(nc, dram, res):
    with ExitStack() as ctx:
        sc = Scope(nc, ctx, "crs")
        ct_hi, ct_lo = res["ct_hi"], res["ct_lo"]
        stage = [sc.sb(f"stage{i}", [P, SW]) for i in range(NSTAGE)]
        kt_hi = sc.sb("kt_hi", [P, 2, KPAD], F32R)
        kt_lo = sc.sb("kt_lo", [P, 2, KPAD], F32R)
        v = sc.sb("v", [P, NCH, PAIRS // 2, 2, 2 * HD], F32R)
        pt = sc.sb("pt", [P, NCH, 2, 2, P], F32R)
        osum = sc.sb("osum", [2 * HD, 2, P])
        prob = sc.sb("prob", [P, 2, KEYS])
        nmx = sc.sb("nmx", [P, 2])
        rsum, rtot = sc.sb("rsum", [P, 2]), sc.sb("rtot", [P, 2])
        rinv = sc.sb("rinv", [P, 2])
        w_hi, w_lo, q_hi, q_lo = res["w_hi"], res["w_lo"], res["q_blk_hi"], res["q_blk_lo"]
        qT, oT, bk, ident = res["qT"], res["oT"], res["bk"], res["ident"]

        score = sc.ps("score", [P, GROUPS_N, BANK])
        ring = [sc.ps(f"ring{i}", [P, BANK]) for i in range(RING)]
        out_bank = sc.ps("out_bank", [P, BANK])

        ct_hi_ready = sc.sem("ct_hi_ready")
        ct_lo_ready = [sc.sem(f"ct_lo_ready{i}") for i in range(2)]
        ct_in = [sc.sem(f"ct_in{i}") for i in range(NSTAGE)]
        q_hi_ready, q_lo_ready = sc.sem("q_hi_ready"), sc.sem("q_lo_ready")
        filled = sc.sem("filled")
        hi_out = sc.sem("hi_out")
        freed = sc.sem("freed")
        tail_filled, tail_hi, tail_freed = sc.sem("tail_filled"), sc.sem("tail_hi"), sc.sem("tail_freed")
        rtot_ready, osum_ready = sc.sem("rtot_ready"), sc.sem("osum_ready")
        scored = sc.sem("scored")
        nmax_ready, exp_done = sc.sem("nmax_ready"), sc.sem("exp_done")
        rinv_ready, prob_ready = sc.sem("rinv_ready"), sc.sem("prob_ready")
        pv_done, o_out = sc.sem("pv_done"), sc.sem("o_out")
        block = ctx.enter_context(nc.Block())
        LEAD = len(BEFORE)

        def split_low(eng, engine, n, b):
            at, w = piece(n)
            eng.wait_ge(ct_hi_ready, NPIECE * b + n + 1)
            engine.tensor_tensor(ct_lo[at], stage[n % NSTAGE][:, 0:w], ct_hi[at].bitcast(F32), ALU.subtract
                                 ).then_inc(ct_lo_ready[n % 2], 1)

        @block.sync
        def _(sp):
            with sp.Fori(0, B - 1) as b:
                for n in range(NPIECE):
                    sp.wait_ge(ct_lo_ready[n % 2], START + NPIECE // 2 * b + max(0, (n - NSTAGE) // 2 + 1))
                    at, w = piece(n)
                    sp.dma_start(stage[n % NSTAGE][:, 0:w], dram["ctxT"][(b + 1, *at)]).then_inc(ct_in[n % NSTAGE], 16)

        @block.gpsimd
        def _(pool):
            pool.sem_inc(ct_lo_ready[0], START)
            with pool.Fori(0, B - 1) as b:
                for n in range(0, NPIECE, 2):
                    split_low(pool, nc.gpsimd, n, b)

        def out_tiles(use, at):
            bank = ring[at[use] % RING]
            if use[0] == "v":
                _, half, c0, n = use
                kk = CHUNKS[c0][1]
                view = bank[0:kk, 0:n * 2 * P].rearrange("p (c q f) -> p c q f", c=n, q=PAIRS // 2)
                return view, v[0:kk, c0:c0 + n, :, 0, :], v[0:kk, c0:c0 + n, :, 1, :]
            if use[0] == "k":
                _, fc, g = use
                s, w = GROUPS[g]
                return bank[:, 0:w], kt_hi[:, fc % 2, s:s + w], kt_lo[:, fc % 2, s:s + w]
            _, p, i = use
            view = bank[:].rearrange("p (c f) -> p c f", c=4)
            return view, pt[:, 4 * i:4 * i + 4, p % 2, 0, :], pt[:, 4 * i:4 * i + 4, p % 2, 1, :]

        def tail_tiles(p):
            kk, i = CHUNKS[NCH - 1][1], p % 2
            return out_bank[0:kk, (2 + i) * P:(3 + i) * P], pt[0:kk, NCH - 1, i, 0, :], pt[0:kk, NCH - 1, i, 1, :]

        def reusable(eng, use, b):
            if use[0] == "v":
                eng.wait_ge(pv_done, START + PAIRS * b + PAIRS // 2 * use[1])
            elif use[0] == "k":
                eng.wait_ge(scored, START + PAIRS * b + max(0, 2 * use[1] - 2))
            else:
                eng.wait_ge(pv_done, START + PAIRS * b + max(0, use[1] - 1))

        @block.scalar
        def _(act):
            act.sem_inc(exp_done, START)

            def split_high(n, b):
                at, w = piece(n)
                act.wait_ge(ct_in[n % NSTAGE], 16 * (NPIECE // NSTAGE * b + n // NSTAGE + 1))
                nc.scalar.activation(ct_hi[at], stage[n % NSTAGE][:, 0:w], ACT.Copy).then_inc(ct_hi_ready, 1)

            def split_q_high(b):
                for h in range(HPC):
                    r = slice(h * HD, (h + 1) * HD)
                    ins = nc.scalar.activation(q_hi[r, :, h // 2, (h % 2) * LAT:(h % 2 + 1) * LAT],
                                               qT[r, :, bass.ts(b, LAT)], ACT.Copy)
                ins.then_inc(q_hi_ready, 1)

            def empty_high(use, b, at=USE):
                view, hi, _ = out_tiles(use, at)
                reusable(act, use, b)
                act.wait_ge(filled, START + LEAD + NUSE * b + at[use] + 1)
                if use[0] == "k":
                    c = use[1] % KC
                    nc.scalar.activation(hi, view, ACT.Identity, bias=bk[:, c:c + 1]).then_inc(hi_out, 1)
                else:
                    nc.scalar.activation(hi, view, ACT.Copy).then_inc(hi_out, 1)

            def turn(b, body, at):
                for use in body:
                    if use[0] == "e":
                        p, i = use[1], use[1] % 2
                        act.wait_ge(nmax_ready, PAIRS * b + p + 1)
                        nc.scalar.activation(prob[:, i, 0:GROUPS_N * GW].rearrange("p (g w) -> p g w", g=GROUPS_N),
                                             score[:, :, 0:GW], ACT.Exp, bias=nmx[:, i:i + 1],
                                             accum_out=rsum[:, i:i + 1])
                        nc.scalar.activation(prob[:, i, GROUPS_N * GW:KEYS],
                                             score[:, GROUPS_N - 1, GW:KEYS - GROUPS[-1][0]], ACT.Exp,
                                             bias=nmx[:, i:i + 1]).then_inc(exp_done, 1)
                    elif use[0] == "u":
                        p = use[1]
                        view, hi, _ = tail_tiles(p)
                        act.wait_ge(pv_done, START + PAIRS * b + max(0, p - 1))
                        act.wait_ge(tail_filled, PAIRS * b + p + 1)
                        nc.scalar.activation(hi, view, ACT.Copy).then_inc(tail_hi, 1)
                    elif use[0] == "q":
                        act.wait_ge(scored, START + PAIRS * b + PAIRS)
                        split_q_high(b + 1)
                    elif use[0] == "c":
                        split_high(use[1], b)
                    elif use[0] in "vkt":
                        empty_high(use, b, at)

            split_q_high(0)
            for use in BEFORE:
                empty_high(use, 0)
            with act.Fori(0, B - 1) as b:
                turn(b, BODY, USE)
            turn(B - 1, LAST, LAST_USE)

        @block.vector
        def _(dve):
            dve.sem_inc(freed, RING)
            dve.sem_inc(o_out, START)
            dve.sem_inc(ct_lo_ready[1], START)

            def empty_low(use, b, at=USE):
                view, hi, lo = out_tiles(use, at)
                dve.wait_ge(hi_out, LEAD + NUSE * b + at[use] + 1)
                if use[0] == "k":
                    c = use[1] % KC
                    nc.vector.scalar_tensor_tensor(lo, view, bk[:, c:c + 1], hi.bitcast(F32), ALU.add, ALU.subtract
                                                   ).then_inc(freed, 1)
                else:
                    nc.vector.tensor_tensor(lo, view, hi.bitcast(F32), ALU.subtract).then_inc(freed, 1)

            def normalise(p, b):
                i = p % 2
                dve.wait_ge(exp_done, START + PAIRS * b + p + 1)
                nc.vector.tensor_tensor(rtot[:, i:i + 1], rsum[:, i:i + 1], prob[:, i, KEYS - 1:KEYS], ALU.add
                                        ).then_inc(rtot_ready, 1)
                dve.wait_ge(rtot_ready, PAIRS * b + p + 1)
                nc.vector.reciprocal(rinv[:, i:i + 1], rtot[:, i:i + 1]).then_inc(rinv_ready, 1)
                dve.wait_ge(rinv_ready, PAIRS * b + p + 1)
                nc.vector.tensor_scalar(prob[:, i, :], prob[:, i, :], rinv[:, i:i + 1], None, ALU.mult
                                        ).then_inc(prob_ready, 1)

            def split_q_low(b, nth):
                dve.wait_ge(q_hi_ready, nth)
                for h in range(HPC):
                    r = slice(h * HD, (h + 1) * HD)
                    block_of = (r, slice(None), h // 2, slice((h % 2) * LAT, (h % 2 + 1) * LAT))
                    ins = nc.vector.tensor_tensor(q_lo[block_of], qT[r, :, bass.ts(b, LAT)],
                                                  q_hi[block_of].bitcast(F32), ALU.subtract)
                ins.then_inc(q_lo_ready, 1)

            def take_out(p, b):
                dve.wait_ge(pv_done, START + PAIRS * b + p + 1)
                for i in range(2):
                    nc.vector.reduce_sum(osum[:, i], out_bank[i * 2 * HD:(i + 1) * 2 * HD, 0:2 * P]
                                         .rearrange("p (i l) -> p l i", i=2), AX.X).then_inc(osum_ready, 1)
                dve.wait_ge(osum_ready, 2 * PAIRS * b + 2 * p + 2)
                for h in range(2):
                    at = (p % 2) * 2 * HD + h * HD
                    f, lat = slice(h * HD, (h + 1) * HD), slice(h * LAT, (h + 1) * LAT)
                    ins = nc.vector.tensor_tensor(oT[at:at + HD, p // 2, bass.ts(b, LAT)], osum[f, 0, lat],
                                                  osum[f, 1, lat], ALU.add)
                ins.then_inc(o_out, 1)

            def turn(b, body, at):
                for use in body:
                    if use[0] == "s":
                        i = use[1] % 2
                        dve.wait_ge(scored, START + PAIRS * b + use[1] + 1)
                        nc.vector.reduce_max(nmx[:, i:i + 1], score[:, :, 0:SW - 1], AX.XY, negate=True
                                             ).then_inc(nmax_ready, 1)
                    elif use[0] == "n":
                        normalise(use[1], b)
                    elif use[0] == "u":
                        view, hi, lo = tail_tiles(use[1])
                        dve.wait_ge(tail_hi, PAIRS * b + use[1] + 1)
                        nc.vector.tensor_tensor(lo, view, hi.bitcast(F32), ALU.subtract).then_inc(tail_freed, 1)
                    elif use[0] == "c":
                        if use[1] % 2:
                            split_low(dve, nc.vector, use[1], b)
                    elif use[0] == "q":
                        split_q_low(b + 1, b + 2)
                    elif use[0] == "o":
                        take_out(use[1], b)
                    elif use[0] in "vkt":
                        empty_low(use, b, at)

            split_q_low(0, 1)
            for use in BEFORE:
                empty_low(use, 0)
            with dve.Fori(0, B - 1) as b:
                turn(b, BODY, USE)
            turn(B - 1, LAST, LAST_USE)

        @block.tensor
        def _(pe):
            for counter in (filled, scored, pv_done):
                pe.sem_inc(counter, START)

            def written(use, b, at):
                pe.wait_ge(freed, LEAD + NUSE * b + at[use] + 1 + RING)

            def fill(use, b, at=USE):
                pe.wait_ge(freed, LEAD + NUSE * b + at[use] + 1)
                bank = ring[at[use] % RING]
                if use[0] == "v":
                    _, half, c0, n = use
                    for c in range(c0, c0 + n):
                        s, kk = CHUNKS[c]
                        f = slice(half * 2 * P, (half + 1) * 2 * P)
                        ins = product3(nc, bank[0:kk, (c - c0) * 2 * P:(c - c0 + 1) * 2 * P],
                                       [((ct_hi[:, k, s:s + kk], ct_lo[:, k, s:s + kk]),
                                         (w_hi[:, 1, k, f], w_lo[:, 1, k, f])) for k in range(KC)])
                elif use[0] == "k":
                    _, fc, g = use
                    s, w = GROUPS[g]
                    if fc == KC:
                        for i in range(2):
                            pe.wait_ge(ct_lo_ready[i], START + NPIECE // 2 * b + KC // 2 * (g + 1))
                    f = slice((fc % KC) * P, (fc % KC + 1) * P)
                    ins = product3(nc, bank[:, 0:w],
                                   [((w_hi[:, 0, k, f], w_lo[:, 0, k, f]),
                                     (ct_hi[:, k, s:s + w], ct_lo[:, k, s:s + w])) for k in range(KC)])
                else:
                    _, p, i = use
                    pe.wait_ge(prob_ready, PAIRS * b + p + 1)
                    for c in range(4 * i, 4 * i + 4):
                        s = CHUNKS[c][0]
                        ins = nc.tensor.transpose(bank[:, (c - 4 * i) * P:(c - 4 * i + 1) * P],
                                                  prob[:, p % 2, s:s + P], ident[:])
                ins.then_inc(filled, 1)

            def fill_tail(p, b, outs):
                s, kk = CHUNKS[NCH - 1]
                pe.wait_ge(prob_ready, PAIRS * b + p + 1)
                pe.wait_ge(o_out, START + PAIRS * b + outs)
                if p:
                    pe.wait_ge(tail_freed, PAIRS * b + p)
                nc.tensor.transpose(tail_tiles(p)[0], prob[:, p % 2, s:s + kk], ident[:]).then_inc(tail_filled, 1)

            def scores(p, b, at):
                fc, i = p // 2, p % 2
                pe.wait_ge(exp_done, START + PAIRS * b + p)
                for g, (s, _) in enumerate(GROUPS):
                    if i == 0:
                        pe.wait_ge(freed, LEAD + NUSE * b + RING + 1
                                   + k_position(fc, min(g + 1, GROUPS_N - 1), at))
                    ins = product3(nc, score[:, g, 0:SW],
                                   [((q_hi[:, fc, i, :], q_lo[:, fc, i, :]),
                                     (kt_hi[:, fc % 2, s:s + SW], kt_lo[:, fc % 2, s:s + SW]))])
                ins.then_inc(scored, 1)

            def k_position(fc, g, at):
                return at[("k", fc, g)] if fc else -1

            def weigh(p, b, at, tails):
                pe.wait_ge(o_out, START + PAIRS * b + p)
                pe.wait_ge(tail_freed, PAIRS * b + tails)
                for c, (s, kk) in enumerate(CHUNKS):
                    if c % 4 == 0 and c + 4 <= NCH:
                        written(("t", p, c // 4), b, at)
                    half, new = divmod(p, PAIRS // 2)
                    if new == 0 and ("v", half, c) in V_AT:
                        written(V_AT["v", half, c], b, at)
                    ins = nc.tensor.matmul(out_bank[:, 0:2 * P],
                                           v[0:kk, c, p % (PAIRS // 2)].rearrange("k i f -> k (i f)"),
                                           pt[0:kk, c, p % 2].rearrange("k i f -> k (i f)"), start=(c == 0),
                                           stop=(c == NCH - 1))
                ins.then_inc(pv_done, 1)

            def turn(b, body, at):
                outs = tails = 0
                for use in body:
                    if use[0] == "s":
                        if use[1] == 0:
                            pe.wait_ge(q_lo_ready, b + 1)
                        scores(use[1], b, at)
                    elif use[0] == "u":
                        fill_tail(use[1], b, outs)
                        tails += 1
                    elif use[0] == "o":
                        weigh(use[1], b, at, tails)
                        outs += 1
                    elif use[0] in "vkt":
                        fill(use, b, at)

            for use in BEFORE:
                fill(use, 0)
            with pe.Fori(0, B - 1) as b:
                turn(b, BODY, USE)
            turn(B - 1, LAST, LAST_USE)


def phase_cross_out(nc, dram, res):
    with ExitStack() as ctx:
        sc = Scope(nc, ctx, "cro")
        wo = sc.sb("wo", [P, KC, D])
        bo = sc.sb("bo", [P, D])
        bv = sc.sb("bv", [P, KC])
        xb = sc.sb("xb", [P, TC, D])
        x, oT = res["x"], res["oT"]
        banks = [sc.ps(f"bank{i}", [P, D]) for i in range(TC)]
        x_in, w_in, bo_in, bv_in = sc.sem("x_in"), sc.sem("w_in"), sc.sem("bo_in"), sc.sem("bv_in")
        biased, o_biased, mm, out = sc.sem("biased"), sc.sem("o_biased"), sc.sem("mm"), sc.sem("out")
        block = ctx.enter_context(nc.Block())

        @block.sync
        def _(sp):
            sp.dma_start(bv[:], dram["L0_xattn_bv"]).then_inc(bv_in, 16)
            sp.dma_start(wo[:], dram["L0_xattn_Wo"]).then_inc(w_in, 16)
            sp.dma_start(x[:], dram["x"].rearrange("(t p) d -> p t d", p=P)).then_inc(x_in, 16)
            sp.dma_start(bo[:], dram["L0_xattn_bo"].partition_broadcast(P)).then_inc(bo_in, 16)

        @block.vector
        def _(dve):
            dve.wait_ge(bv_in, 16)
            for c in range(KC):
                nc.vector.tensor_scalar(oT[:, c, :], oT[:, c, :], bv[:, c:c + 1], None, ALU.add
                                        ).then_inc(o_biased, 1)
            dve.wait_ge(x_in, 16)
            dve.wait_ge(bo_in, 16)
            for t in range(TC):
                nc.vector.tensor_tensor(xb[:, t, :], x[:, t, :], bo[:], ALU.add).then_inc(biased, 1)
            for t in range(TC):
                dve.wait_ge(mm, t + 1)
                dve.wait_ge(biased, t + 1)
                nc.vector.tensor_tensor(x[:, t, :], xb[:, t, :], banks[t][:], ALU.add).then_inc(out, 1)

        @block.tensor
        def _(pe):
            pe.wait_ge(w_in, 16)
            pe.wait_ge(o_biased, KC)
            for t in range(TC):
                product(nc, banks[t][:], [(oT[:, c, t * P:(t + 1) * P], wo[:, c, :]) for c in range(KC)]
                        ).then_inc(mm, 1)


def phase_scan(nc, dram, ident, x, ahead):
    with ExitStack() as ctx:
        sc = Scope(nc, ctx, "scn")
        xn = sc.sb("xn", [P, TC, D])
        sq = sc.sb("sq", [P, D])
        ss = sc.sb("ss", [P, TC])
        nrm = sc.sb("nrm", [P, TC])
        rn = sc.sb("rn", [P, TC])
        xs = sc.sb("xs", [P, TC, D])
        xnT = sc.sb("xnT", [P, KC, T])
        w = sc.sb("w", [P, KC, 3 * D])
        gamma = sc.sb("gamma", [P, KC])
        decay = sc.sb("decay", [P, KC, T])
        y = sc.sb("y", [P, KC, T])
        yq = sc.sb("yq", [P, KC, T])
        norm = Norm(sc, "ln")
        banks = [sc.ps(f"bank{i}", [P, T]) for i in range(8)]
        g_in, w_in = sc.sem("g_in"), sc.sem("w_in")
        squared, nrm_ready, nrm_done = sc.sem("squared"), sc.sem("nrm_ready"), sc.sem("nrm_done")
        scaled, turned, turned_out, mm = sc.sem("scaled"), sc.sem("turned"), sc.sem("turned_out"), sc.sem("mm")
        decay_ready, decay_cut, scanned = sc.sem("decay_ready"), sc.sem("decay_cut"), sc.sem("scanned")
        gated, back, out = sc.sem("gated"), sc.sem("back"), sc.sem("out")
        KV, A, Q = range(3)
        column = {KV: 1, A: 2, Q: 0}

        def bank(f, part):
            return banks[(KC + 3 * f + part) % 8]

        block = ctx.enter_context(nc.Block())

        @block.sync
        def _(sp):
            sp.dma_start(gamma[:], dram["L0_attn_gamma"]).then_inc(g_in, 16)
            sp.dma_start(w[:], dram["L0_attn_W_qkva"]).then_inc(w_in, 16)
            for half in range(2):
                ahead.load_turned(sp, 0, half)
            for half in range(2):
                ahead.load_rows(sp, 0, half)

        @block.scalar
        def _(act):
            norm.scalar(nc, act)
            for t in range(TC):
                act.wait_ge(norm.done, t + 1)
                if t:
                    act.wait_ge(squared, t)
                nc.scalar.activation(sq[:], xn[:, t, :], ACT.Square, accum_out=ss[:, t:t + 1]).then_inc(squared, 1)
            act.wait_ge(squared, TC)
            nc.scalar.activation(nrm[:], ss[:], ACT.Sqrt).then_inc(nrm_ready, 1)
            act.wait_ge(g_in, 16)
            for c in range(KC):
                act.wait_ge(turned, c + 1)
                nc.scalar.activation(xnT[:, c, :], banks[c][:], ACT.Copy, scale=gamma[:, c:c + 1]
                                     ).then_inc(turned_out, 1)
            for f in range(KC):
                act.wait_ge(mm, 3 * f + A + 1)
                nc.scalar.activation(decay[:, f, :], bank(f, A)[:], ACT.Sigmoid).then_inc(decay_ready, 1)

        @block.vector
        def _(dve):
            norm.vector(nc, dve, x, xn)
            dve.wait_ge(nrm_ready, 1)
            nc.vector.tensor_scalar(nrm[:], nrm[:], 1e-12, D ** -0.5, ALU.max, ALU.mult).then_inc(nrm_done, 1)
            dve.wait_ge(nrm_done, 1)
            nc.vector.reciprocal(rn[:], nrm[:]).then_inc(nrm_done, 1)
            dve.wait_ge(nrm_done, 2)
            for t in range(TC):
                nc.vector.tensor_scalar(xs[:, t, :], xn[:, t, :], rn[:, t:t + 1], None, ALU.mult
                                        ).then_inc(scaled, 1)
            for f in range(KC):
                dve.wait_ge(decay_ready, f + 1)
                nc.vector.memset(decay[:, f, :].rearrange("p (b n) -> p b n", b=B)[:, :, 0:1], 0.0
                                 ).then_inc(decay_cut, 1)
                dve.wait_ge(decay_cut, f + 1)
                nc.vector.tensor_tensor_scan(y[:, f, :], decay[:, f, :], bank(f, KV)[:], 0.0, ALU.mult, ALU.add
                                             ).then_inc(scanned, 1)
                dve.wait_ge(scanned, f + 1)
                dve.wait_ge(mm, 3 * f + Q + 1)
                nc.vector.tensor_tensor(yq[:, f, :], y[:, f, :], bank(f, Q)[:], ALU.mult).then_inc(gated, 1)
            for t in range(TC):
                dve.wait_ge(back, t + 1)
                nc.vector.tensor_tensor(x[:, t, :], x[:, t, :], banks[t][:], ALU.add).then_inc(out, 1)

        @block.tensor
        def _(pe):
            pe.wait_ge(scaled, TC)
            for c in range(KC):
                transpose_rows(nc, banks[c], xs, c, ident).then_inc(turned, 1)
            pe.wait_ge(turned_out, KC)
            pe.wait_ge(w_in, 16)
            for f in range(KC):
                for part in (KV, A, Q):
                    n = 3 * f + part
                    if n >= 8:
                        pe.wait_ge(gated, (n - 8) // 3 + 1)
                    o = column[part] * D + f * P
                    product(nc, bank(f, part)[:], [(w[:, k, o:o + P], xnT[:, k, :]) for k in range(KC)]
                            ).then_inc(mm, 1)
            pe.wait_ge(gated, KC)
            for t in range(TC):
                for f in range(KC):
                    last = nc.tensor.transpose(banks[t][:, f * P:(f + 1) * P], yq[:, f, t * P:(t + 1) * P], ident[:])
                last.then_inc(back, 1)


class Route:

    def __init__(self, sc, dram, bias=None):
        self.dram, self.bias = dram, bias
        shape = [P, TC, E0]
        self.rank = sc.sb("rt_rank", shape)
        self.rb = sc.sb("rt_bias", [P, E0]) if bias is not None else None
        self.lg, self.dl, self.ex = (sc.sb(f"rt_{n}", shape) for n in ("lg", "dl", "ex"))
        self.eq, self.cand, self.mask, self.coef = (sc.sb(f"rt_{n}", shape) for n in ("eq", "cand", "mask", "coef"))
        self.mx, self.sum, self.gate, self.best = (sc.sb(f"rt_{n}", [P, TC]) for n in ("mx", "sum", "gate", "best"))
        self.const_in = sc.sem("rt_const_in")
        self.step = sc.sem("rt_step")
        self.dl_ready, self.ex_ready, self.done = (sc.sem(f"rt_{n}") for n in ("dl_ready", "ex_ready", "done"))

    def sync(self, sp):
        sp.dma_start(self.rank[:], self.dram["rank"].partition_broadcast(P)).then_inc(self.const_in, 16)
        if self.bias is not None:
            sp.dma_start(self.rb[:], self.bias.partition_broadcast(P)).then_inc(self.const_in, 16)

    def scalar(self, nc, act):
        act.wait_ge(self.dl_ready, 1)
        nc.scalar.activation(self.ex[:], self.dl[:], ACT.Exp).then_inc(self.ex_ready, 1)

    def vector(self, nc, dve, logits):
        n = [0]

        def step(ins):
            n[0] += 1
            ins.then_inc(self.step, 1)
            dve.wait_ge(self.step, n[0])

        wide = lambda a: a[:].unsqueeze(2).broadcast_to([P, TC, E0])
        dve.wait_ge(self.const_in, 32 if self.bias is not None else 16)
        if self.bias is not None:
            step(nc.vector.tensor_tensor(self.lg[:], logits, self.rb[:].unsqueeze(1).broadcast_to([P, TC, E0]),
                                         ALU.add))
        else:
            step(nc.vector.tensor_copy(self.lg[:], logits))
        step(nc.vector.reduce_max(self.mx[:], self.lg[:], AX.X))
        nc.vector.tensor_tensor(self.dl[:], self.lg[:], wide(self.mx), ALU.subtract).then_inc(self.dl_ready, 1)
        step(nc.vector.tensor_tensor(self.eq[:], self.lg[:], wide(self.mx), ALU.is_equal))
        step(nc.vector.tensor_tensor(self.cand[:], self.eq[:], self.rank[:], ALU.mult))
        step(nc.vector.reduce_max(self.best[:], self.cand[:], AX.X))
        step(nc.vector.tensor_tensor(self.mask[:], self.cand[:], wide(self.best), ALU.is_equal))
        dve.wait_ge(self.ex_ready, 1)
        step(nc.vector.reduce_sum(self.sum[:], self.ex[:], AX.X))
        step(nc.vector.reciprocal(self.gate[:], self.sum[:]))
        nc.vector.tensor_tensor(self.coef[:], self.mask[:], wide(self.gate), ALU.mult).then_inc(self.done, 1)


def phase_experts(nc, dram, ident, x):
    with ExitStack() as ctx:
        sc = Scope(nc, ctx, "moe")
        RINGW, RINGS = 2, 2
        xn = sc.sb("xn", [P, TC, D])
        xnT = sc.sb("xnT", [P, KC, T])
        xh, xl = sc.sb("xh", [P, KC, T], F32R), sc.sb("xl", [P, KC, T], F32R)
        wr = sc.sb("wr", [P, KC, E0])
        eb = sc.sb("eb", [E0, D])
        ew = [sc.sb(f"ew{i}", [P, KC, D]) for i in range(RINGW)]
        eh = [sc.sb(f"eh{i}", [P, KC, D], F32R) for i in range(RINGS)]
        el = [sc.sb(f"el{i}", [P, KC, D], F32R) for i in range(RINGS)]
        coefT = sc.sb("coefT", [E0, T])
        norm = Norm(sc, "ln")
        rt = Route(sc, dram, dram["L0_ffn_router_b"])
        banks = [sc.ps(f"bank{i}", [P, T]) for i in range(8)]
        wr_in, eb_in = sc.sem("wr_in"), sc.sem("eb_in")
        ew_in = [sc.sem(f"ew_in{i}") for i in range(RINGW)]
        turned, turned_out, routed = sc.sem("turned"), sc.sem("turned_out"), sc.sem("routed")
        xh_ready, xl_ready, eh_ready, el_ready = (sc.sem(n) for n in ("xh_ready", "xl_ready", "eh_ready", "el_ready"))
        coef_turned, coef_out = sc.sem("coef_turned"), sc.sem("coef_out")
        bias_mm, biased, mm, added = sc.sem("bias_mm"), sc.sem("biased"), sc.sem("mm"), sc.sem("added")
        block = ctx.enter_context(nc.Block())

        @block.sync
        def _(sp):
            sp.dma_start(wr[:], dram["L0_ffn_router_w"]).then_inc(wr_in, 16)
            rt.sync(sp)
            sp.dma_start(eb[:], dram["L0_ffn_expert_b"]).then_inc(eb_in, 16)
            for e in range(E0):
                if e >= RINGW:
                    sp.wait_ge(el_ready, e - RINGW + 1)
                sp.dma_start(ew[e % RINGW][:], dram["L0_ffn_expert_w"][e]).then_inc(ew_in[e % RINGW], 16)

        @block.scalar
        def _(act):
            norm.scalar(nc, act)
            for c in range(KC):
                act.wait_ge(turned, c + 1)
                nc.scalar.activation(xnT[:, c, :], banks[c][:], ACT.Copy).then_inc(turned_out, 1)
                nc.scalar.activation(xh[:, c, :], banks[c][:], ACT.Copy).then_inc(xh_ready, 1)
            rt.scalar(nc, act)
            act.wait_ge(coef_turned, 1)
            nc.scalar.activation(coefT[:], banks[5][0:E0, :], ACT.Copy).then_inc(coef_out, 1)
            for e in range(E0):
                act.wait_ge(ew_in[e % RINGW], 16 * (e // RINGW + 1))
                if e >= RINGS:
                    act.wait_ge(mm, TC * (e - RINGS + 1))
                nc.scalar.activation(eh[e % RINGS][:], ew[e % RINGW][:], ACT.Copy).then_inc(eh_ready, 1)

        @block.gpsimd
        def _(pool):
            for e in range(E0):
                pool.wait_ge(eh_ready, e + 1)
                nc.gpsimd.tensor_tensor(el[e % RINGS][:], ew[e % RINGW][:], eh[e % RINGS][:].bitcast(F32),
                                        ALU.subtract).then_inc(el_ready, 1)

        @block.vector
        def _(dve):
            norm.vector(nc, dve, x, xn)
            for c in range(KC):
                dve.wait_ge(xh_ready, c + 1)
                nc.vector.tensor_tensor(xl[:, c, :], xnT[:, c, :], xh[:, c, :].bitcast(F32), ALU.subtract
                                        ).then_inc(xl_ready, 1)
            dve.wait_ge(routed, 1)
            rt.vector(nc, dve, banks[4][:, 0:TC * E0].rearrange("p (t e) -> p t e", t=TC))
            dve.wait_ge(rt.done, 1)
            for t in range(TC):
                dve.wait_ge(bias_mm, t + 1)
                nc.vector.tensor_tensor(x[:, t, :], x[:, t, :], banks[t][:], ALU.add).then_inc(added, 1)
            for e in range(E0):
                for t in range(TC):
                    n = e * TC + t
                    dve.wait_ge(mm, n + 1)
                    dve.wait_ge(added, n + 1)
                    nc.vector.scalar_tensor_tensor(x[:, t, :], banks[4 + t][:] if e % 2 == 0 else banks[t][:],
                                                   rt.coef[:, t, e:e + 1], x[:, t, :], ALU.mult, ALU.add
                                                   ).then_inc(added, 1)

        @block.tensor
        def _(pe):
            pe.wait_ge(norm.done, TC)
            for c in range(KC):
                transpose_rows(nc, banks[c], xn, c, ident).then_inc(turned, 1)
            pe.wait_ge(turned_out, KC)
            pe.wait_ge(wr_in, 16)
            for t in range(TC):
                last = product(nc, banks[4][:, t * E0:(t + 1) * E0],
                               [(xnT[:, k, t * P:(t + 1) * P], wr[:, k, :]) for k in range(KC)])
            last.then_inc(routed, 1)
            pe.wait_ge(rt.done, 1)
            for t in range(TC):
                last = nc.tensor.transpose(banks[5][0:E0, t * P:(t + 1) * P], rt.coef[:, t, :], ident[:])
            last.then_inc(coef_turned, 1)
            pe.wait_ge(coef_out, 1)
            pe.wait_ge(eb_in, 16)
            for t in range(TC):
                product(nc, banks[t][:], [(coefT[:, t * P:(t + 1) * P], eb[:])]).then_inc(bias_mm, 1)
            pe.wait_ge(xl_ready, KC)
            for e in range(E0):
                pe.wait_ge(el_ready, e + 1)
                for t in range(TC):
                    n = e * TC + t
                    pe.wait_ge(added, max(1, n - TC + 1))
                    rows = slice(t * P, (t + 1) * P)
                    product3(nc, banks[4 + t][:] if e % 2 == 0 else banks[t][:],
                             [((xh[:, k, rows], xl[:, k, rows]), (eh[e % RINGS][:, k, :], el[e % RINGS][:, k, :]))
                              for k in range(KC)]).then_inc(mm, 1)


class ContextAhead:
    KEYS_AT = [slice(0, 2 * BANK), slice(2 * BANK, KPAD)]
    CHUNKS_AT = [slice(0, NCH // 2), slice(NCH // 2, NCH - 1)]

    def __init__(self, sc, dram):
        self.dram = dram
        self.ct = [sc.sb(f"ct{i}", [P, KC, KPAD]) for i in range(2)]
        self.cr = [sc.sb(f"cr{i}", [P, NCH, D]) for i in range(2)]
        self.ct_in = [sc.sem(f"ct_in{half}") for half in range(2)]
        self.cr_in = [sc.sem(f"cr_in{half}") for half in range(2)]

    def load_turned(self, sp, t, half):
        at = self.KEYS_AT[half]
        for i in range(2):
            sp.dma_start(self.ct[i][:, :, at], self.dram["ctxT"][2 * t + i, :, :, at]).then_inc(self.ct_in[half], 16)

    def load_rows(self, sp, t, half):
        at = self.CHUNKS_AT[half]
        for i in range(2):
            sp.dma_start(self.cr[i][:, at, :], self.dram["ctxR"][2 * t + i, :, at, :]).then_inc(self.cr_in[half], 16)
            if half:
                sp.dma_start(self.cr[i][0:CHUNKS[-1][1], NCH - 1, :], self.dram["ctxL"][2 * t + i]
                             ).then_inc(self.cr_in[half], 16)


def phase_context(nc, dram, ident, x, ahead):
    ct, cr, ct_in, cr_in = ahead.ct, ahead.cr, ahead.ct_in, ahead.cr_in
    with ExitStack() as ctx:
        sc = Scope(nc, ctx, "ctx")
        qk = sc.sb("qk", [P, KC, T])
        u = sc.sb("u", [P, TC, D])
        with ExitStack() as c2:
            s2 = Scope(nc, c2, "ctq")
            xn = s2.sb("xn", [P, TC, D])
            xnT = s2.sb("xnT", [P, KC, T])
            qT = s2.sb("qT", [P, KC, T])
            wq, wk = s2.sb("wq", [P, KC, D]), s2.sb("wk", [P, KC, D])
            bq = s2.sb("bq", [P, KC])
            norm = Norm(s2, "ln")
            banks = [s2.ps(f"bank{i}", [P, T]) for i in range(8)]
            wq_in, wk_in, bq_in = s2.sem("wq_in"), s2.sem("wk_in"), s2.sem("bq_in")
            turned, turned_out = s2.sem("turned"), s2.sem("turned_out")
            q_mm, q_out, qk_mm, qk_out = s2.sem("q_mm"), s2.sem("q_out"), s2.sem("qk_mm"), s2.sem("qk_out")
            block = c2.enter_context(nc.Block())

            @block.sync
            def _(sp):
                sp.dma_start(wq[:], dram["L1_xattn_Wq"]).then_inc(wq_in, 16)
                sp.dma_start(bq[:], dram["L1_xattn_bq"]).then_inc(bq_in, 16)
                sp.dma_start(wk[:], dram["L1_xattn_Wk"]).then_inc(wk_in, 16)

            @block.scalar
            def _(act):
                norm.scalar(nc, act)
                for c in range(KC):
                    act.wait_ge(turned, c + 1)
                    nc.scalar.activation(xnT[:, c, :], banks[c][:], ACT.Copy).then_inc(turned_out, 1)
                for c in range(KC):
                    act.wait_ge(qk_mm, c + 1)
                    nc.scalar.activation(qk[:, c, :], banks[c][:], ACT.Copy, scale=D ** -0.5).then_inc(qk_out, 1)

            @block.vector
            def _(dve):
                norm.vector(nc, dve, x, xn)
                dve.wait_ge(bq_in, 16)
                for o in range(KC):
                    dve.wait_ge(q_mm, o + 1)
                    nc.vector.tensor_scalar(qT[:, o, :], banks[KC + o][:], bq[:, o:o + 1], None, ALU.add
                                            ).then_inc(q_out, 1)

            @block.tensor
            def _(pe):
                pe.wait_ge(norm.done, TC)
                for c in range(KC):
                    transpose_rows(nc, banks[c], xn, c, ident).then_inc(turned, 1)
                pe.wait_ge(turned_out, KC)
                pe.wait_ge(wq_in, 16)
                for o in range(KC):
                    product(nc, banks[KC + o][:], [(wq[:, k, o * P:(o + 1) * P], xnT[:, k, :]) for k in range(KC)]
                            ).then_inc(q_mm, 1)
                pe.wait_ge(q_out, KC)
                pe.wait_ge(wk_in, 16)
                for c in range(KC):
                    product(nc, banks[c][:], [(wk[:, k, c * P:(c + 1) * P], qT[:, k, :]) for k in range(KC)]
                            ).then_inc(qk_mm, 1)

        with ExitStack() as c3:
            s3 = Scope(nc, c3, "cta")
            qs = s3.sb("qs", [P, KC, P])
            prob = s3.sb("prob", [P, KEYS])
            pt = s3.sb("pt", [P, NCH, P])
            nmx, rsum, rinv = s3.sb("nmx", [P, 1]), s3.sb("rsum", [P, 1]), s3.sb("rinv", [P, 1])
            score = s3.ps("score", [P, GROUPS_N * BANK])
            tb = [s3.ps(f"tb{i}", [P, BANK]) for i in range(2)]
            ub = s3.ps("ub", [P, D])
            qs_ready, scored, max_ready, exp_done = (s3.sem(n) for n in ("qs_ready", "scored", "max_ready", "exp_done"))
            rinv_ready, turned, turned_out = s3.sem("rinv_ready"), s3.sem("turned"), s3.sem("turned_out")
            weighed, u_out = s3.sem("weighed"), s3.sem("u_out")
            NT = 4
            block = c3.enter_context(nc.Block())
            KL = CHUNKS[-1][1]

            @block.sync
            def _(sp):
                with sp.Fori(0, TC - 1) as t:
                    for half in range(2):
                        sp.wait_ge(scored, 2 * t + half + 1)
                        ahead.load_turned(sp, t + 1, half)
                    for half in range(2):
                        sp.wait_ge(weighed, 2 * t + half + 1)
                        ahead.load_rows(sp, t + 1, half)

            @block.scalar
            def _(act):
                act.sem_inc(turned_out, 2)
                with act.Fori(0, TC) as t:
                    nc.scalar.activation(qs[:], qk[:, :, bass.ts(t, P)], ACT.Copy).then_inc(qs_ready, 1)
                    act.wait_ge(max_ready, t + 1)
                    nc.scalar.activation(prob[:], score[:, 0:KEYS], ACT.Exp, bias=nmx[:], accum_out=rsum[:]
                                         ).then_inc(exp_done, 1)
                    for i in range(NT):
                        act.wait_ge(turned, NT * t + i + 1)
                        if i < 3:
                            nc.scalar.activation(pt[:, 4 * i:4 * i + 4, :],
                                                 tb[i % 2][:].rearrange("p (c f) -> p c f", c=4), ACT.Copy
                                                 ).then_inc(turned_out, 1)
                        else:
                            nc.scalar.activation(pt[0:KL, NCH - 1, :], tb[i % 2][0:KL, 0:P], ACT.Copy
                                                 ).then_inc(turned_out, 1)

            @block.vector
            def _(dve):
                with dve.Fori(0, TC) as t:
                    dve.wait_ge(scored, 2 * t + 2)
                    nc.vector.reduce_max(nmx[:], score[:, 0:KEYS], AX.X, negate=True).then_inc(max_ready, 1)
                    dve.wait_ge(exp_done, t + 1)
                    nc.vector.reciprocal(rinv[:], rsum[:]).then_inc(rinv_ready, 1)
                    dve.wait_ge(rinv_ready, t + 1)
                    dve.wait_ge(weighed, 2 * t + 2)
                    nc.vector.tensor_scalar(u[:, bass.ds(t, 1), :], ub[:].unsqueeze(1), rinv[:], None, ALU.mult
                                            ).then_inc(u_out, 1)

            @block.tensor
            def _(pe):
                pe.sem_inc(u_out, 1)
                with pe.Fori(0, TC) as t:
                    pe.wait_ge(qs_ready, t + 1)
                    for s in range(0, KPAD, BANK):
                        w = min(BANK, KPAD - s)
                        if s == 0:
                            pe.wait_ge(ct_in[0], 32 * t + 32)
                        if s == ahead.KEYS_AT[1].start:
                            last.then_inc(scored, 1)
                            pe.wait_ge(ct_in[1], 32 * t + 32)
                        for k in range(KC):
                            for i in range(2):
                                r = slice(i * LAT, (i + 1) * LAT)
                                last = nc.tensor.matmul(score[r, s:s + w], qs[:, k, r], ct[i][:, k, s:s + w],
                                                        start=(k == 0), stop=(k == KC - 1))
                    last.then_inc(scored, 1)
                    pe.wait_ge(exp_done, t + 1)
                    for i in range(NT):
                        pe.wait_ge(turned_out, NT * t + i + 1)
                        for c in range(4 * i, min(4 * i + 4, NCH)):
                            s, kk = CHUNKS[c]
                            last = nc.tensor.transpose(tb[i % 2][0:kk, (c - 4 * i) * P:(c - 4 * i + 1) * P],
                                                       prob[:, s:s + kk], ident[:])
                        last.then_inc(turned, 1)
                    pe.wait_ge(turned_out, NT * t + NT + 2)
                    pe.wait_ge(u_out, t + 1)
                    for c, (s, kk) in enumerate(CHUNKS):
                        if c == 0:
                            pe.wait_ge(cr_in[0], 32 * t + 32)
                        if c == ahead.CHUNKS_AT[1].start:
                            last.then_inc(weighed, 1)
                            pe.wait_ge(cr_in[1], 64 * t + 64)
                        for i in range(2):
                            r = slice(i * LAT, (i + 1) * LAT)
                            last = nc.tensor.matmul(ub[r, :], pt[0:kk, c, r], cr[i][0:kk, c, :], start=(c == 0),
                                                    stop=(c == NCH - 1))
                    last.then_inc(weighed, 1)

        with ExitStack() as c4:
            s4 = Scope(nc, c4, "cto")
            uT, vT = s4.sb("uT", [P, KC, T]), s4.sb("vT", [P, KC, T])
            wv, wo = s4.sb("wv", [P, KC, D]), s4.sb("wo", [P, KC, D])
            bv, bo = s4.sb("bv", [P, KC]), s4.sb("bo", [P, D])
            banks = [s4.ps(f"bank{i}", [P, T]) for i in range(8)]
            wv_in, wo_in, bv_in, bo_in = s4.sem("wv_in"), s4.sem("wo_in"), s4.sem("bv_in"), s4.sem("bo_in")
            turned, turned_out, v_mm, v_out = s4.sem("turned"), s4.sem("turned_out"), s4.sem("v_mm"), s4.sem("v_out")
            o_mm, biased, out = s4.sem("o_mm"), s4.sem("biased"), s4.sem("out")
            block = c4.enter_context(nc.Block())

            @block.sync
            def _(sp):
                sp.dma_start(wv[:], dram["L1_xattn_Wv"]).then_inc(wv_in, 16)
                sp.dma_start(bv[:], dram["L1_xattn_bv"]).then_inc(bv_in, 16)
                sp.dma_start(wo[:], dram["L1_xattn_Wo"]).then_inc(wo_in, 16)
                sp.dma_start(bo[:], dram["L1_xattn_bo"].partition_broadcast(P)).then_inc(bo_in, 16)

            @block.scalar
            def _(act):
                for c in range(KC):
                    act.wait_ge(turned, c + 1)
                    nc.scalar.activation(uT[:, c, :], banks[c][:], ACT.Copy).then_inc(turned_out, 1)
                act.wait_ge(bv_in, 16)
                for c in range(KC):
                    act.wait_ge(v_mm, c + 1)
                    nc.scalar.activation(vT[:, c, :], banks[KC + c][:], ACT.Identity, bias=bv[:, c:c + 1]
                                         ).then_inc(v_out, 1)

            @block.vector
            def _(dve):
                dve.wait_ge(bo_in, 16)
                for t in range(TC):
                    nc.vector.tensor_tensor(x[:, t, :], x[:, t, :], bo[:], ALU.add).then_inc(biased, 1)
                for t in range(TC):
                    dve.wait_ge(o_mm, t + 1)
                    dve.wait_ge(biased, t + 1)
                    nc.vector.tensor_tensor(x[:, t, :], x[:, t, :], banks[t][:], ALU.add).then_inc(out, 1)

            @block.tensor
            def _(pe):
                for c in range(KC):
                    transpose_rows(nc, banks[c], u, c, ident).then_inc(turned, 1)
                pe.wait_ge(turned_out, KC)
                pe.wait_ge(wv_in, 16)
                for o in range(KC):
                    product(nc, banks[KC + o][:], [(wv[:, k, o * P:(o + 1) * P], uT[:, k, :]) for k in range(KC)]
                            ).then_inc(v_mm, 1)
                pe.wait_ge(v_out, KC)
                pe.wait_ge(wo_in, 16)
                for t in range(TC):
                    product(nc, banks[t][:], [(vT[:, k, t * P:(t + 1) * P], wo[:, k, :]) for k in range(KC)]
                            ).then_inc(o_mm, 1)


def phase_latent(nc, dram, ident, x):
    with ExitStack() as ctx:
        sc = Scope(nc, ctx, "lat")
        xn = sc.sb("xn", [P, TC, D])
        xnT = sc.sb("xnT", [P, KC, T])
        wq, wl = sc.sb("wq", [P, KC, D]), sc.sb("wl", [P, KC, P])
        wk, wv, wo = sc.sb("wk", [P, D]), sc.sb("wv", [P, D]), sc.sb("wo", [P, KC, D])
        bq, bl, bk, bv = sc.sb("bq", [P, KC]), sc.sb("bl", [P, 1]), sc.sb("bk", [P, KC]), sc.sb("bv", [P, KC])
        bo = sc.sb("bo", [P, D])
        qT, kT, lT = sc.sb("qT", [P, KC, T]), sc.sb("kT", [P, KC, T]), sc.sb("lT", [P, T])
        v = sc.sb("v", [P, TC, D])
        q_blk = sc.sb("q_blk", [P, KC, 2, B, P])
        dif = sc.sb("dif", [P, PAIRS, B, LAT])
        prob = sc.sb("prob", [P, PAIRS, B, LAT])
        nmx, rs, ri = (sc.sb(n, [P, PAIRS, B]) for n in ("nmx", "rs", "ri"))
        pt = sc.sb("pt", [P, PAIRS, TC, P])
        oT = sc.sb("oT", [P, KC, T])
        norm = Norm(sc, "ln")
        banks = [sc.ps(f"bank{i}", [P, T]) for i in range(8)]
        w_in = {n: sc.sem(f"{n}_in") for n in ("wq", "wl", "wk", "wv", "wo", "bq", "bl", "bk", "bv", "bo")}
        zeroed, turned, turned_out = sc.sem("zeroed"), sc.sem("turned"), sc.sem("turned_out")
        q_mm, q_out, l_mm, l_out = sc.sem("q_mm"), sc.sem("q_out"), sc.sem("l_mm"), sc.sem("l_out")
        k_mm, k_out, v_mm, v_out = sc.sem("k_mm"), sc.sem("k_out"), sc.sem("v_mm"), sc.sem("v_out")
        blk_ready, scored, max_ready, dif_ready = (sc.sem(n) for n in ("blk_ready", "scored", "max_ready", "dif_ready"))
        exp_done, sum_ready, inv_ready, prob_ready = (sc.sem(n) for n in ("exp_done", "sum_ready", "inv_ready",
                                                                          "prob_ready"))
        p_turned, pt_out, weighed, o_out = (sc.sem(n) for n in ("p_turned", "pt_out", "weighed", "o_out"))
        biased, o_mm, out = sc.sem("biased"), sc.sem("o_mm"), sc.sem("out")
        block = ctx.enter_context(nc.Block())

        @block.sync
        def _(sp):
            tiles = dict(wq=wq, bq=bq, wl=wl, bl=bl, wk=wk, bk=bk, wv=wv, bv=bv, wo=wo)
            for n, tile in tiles.items():
                sp.dma_start(tile[:], dram[f"L1_attn_{n[0].upper() + n[1] if n[0] == 'w' else n}"]
                             ).then_inc(w_in[n], 16)
            sp.dma_start(bo[:], dram["L1_attn_bo"].partition_broadcast(P)).then_inc(w_in["bo"], 16)

        @block.gpsimd
        def _(pool):
            nc.gpsimd.memset(q_blk[:], 0.0).then_inc(zeroed, 1)

        @block.scalar
        def _(act):
            norm.scalar(nc, act)
            for c in range(KC):
                act.wait_ge(turned, c + 1)
                nc.scalar.activation(xnT[:, c, :], banks[c][:], ACT.Copy).then_inc(turned_out, 1)
            act.wait_ge(w_in["bl"], 16)
            act.wait_ge(l_mm, 1)
            nc.scalar.activation(lT[:], banks[4][:], ACT.Identity, bias=bl[:]).then_inc(l_out, 1)
            act.wait_ge(w_in["bk"], 16)
            for c in range(KC):
                act.wait_ge(k_mm, c + 1)
                nc.scalar.activation(kT[:, c, :], banks[c][:], ACT.Identity, bias=bk[:, c:c + 1]).then_inc(k_out, 1)
            for t in range(TC):
                act.wait_ge(v_mm, t + 1)
                nc.scalar.activation(v[:, t, :], banks[4 + t][:], ACT.Copy).then_inc(v_out, 1)
            for u in range(PAIRS):
                act.wait_ge(dif_ready, u + 1)
                nc.scalar.activation(prob[:, u], dif[:, u], ACT.Exp).then_inc(exp_done, 1)
            for u in range(PAIRS):
                act.wait_ge(p_turned, u + 1)
                nc.scalar.activation(pt[:, u], banks[u][:].rearrange("p (t f) -> p t f", t=TC), ACT.Copy
                                     ).then_inc(pt_out, 1)

        @block.vector
        def _(dve):
            norm.vector(nc, dve, x, xn)
            dve.wait_ge(w_in["bq"], 16)
            for c in range(KC):
                dve.wait_ge(q_mm, c + 1)
                nc.vector.tensor_scalar(qT[:, c, :], banks[(5 + c) % 8][:], bq[:, c:c + 1], HD ** -0.5, ALU.add,
                                        ALU.mult).then_inc(q_out, 1)
            dve.wait_ge(zeroed, 1)
            dve.wait_ge(q_out, KC)
            for h in range(HPC):
                r = slice(h * HD, (h + 1) * HD)
                for c in range(KC):
                    last = nc.vector.tensor_copy(q_blk[r, c, h // 2, :, (h % 2) * LAT:(h % 2 + 1) * LAT],
                                                 qT[r, c, :].rearrange("p (b n) -> p b n", b=B))
            last.then_inc(blk_ready, 1)
            for u in range(PAIRS):
                dve.wait_ge(scored, u + 1)
                s = banks[u][:].rearrange("p (b n) -> p b n", b=B)
                nc.vector.reduce_max(nmx[:, u], s, AX.X, negate=True).then_inc(max_ready, 1)
                dve.wait_ge(max_ready, u + 1)
                nc.vector.tensor_tensor(dif[:, u], s, nmx[:, u].unsqueeze(2).broadcast_to([P, B, LAT]), ALU.add
                                        ).then_inc(dif_ready, 1)
            for u in range(PAIRS):
                dve.wait_ge(exp_done, u + 1)
                nc.vector.reduce_sum(rs[:, u], prob[:, u], AX.X).then_inc(sum_ready, 1)
                dve.wait_ge(sum_ready, u + 1)
                nc.vector.reciprocal(ri[:, u], rs[:, u]).then_inc(inv_ready, 1)
                dve.wait_ge(inv_ready, u + 1)
                nc.vector.tensor_tensor(prob[:, u], prob[:, u], ri[:, u].unsqueeze(2).broadcast_to([P, B, LAT]),
                                        ALU.mult).then_inc(prob_ready, 1)
            dve.wait_ge(w_in["bv"], 16)
            for n in range(4 * KC):
                c, half, par = n // 4, (n // 2) % 2, n % 2
                dve.wait_ge(weighed, n + 1)
                s = banks[n % 8][:].rearrange("p (t h n) -> p t h n", t=2, h=HPC)
                o = oT[:, c, :].rearrange("p (t r n) -> p t r n", t=TC, r=2)
                for h in range(HPC):
                    r = slice(h * HD, (h + 1) * HD)
                    last = nc.vector.tensor_scalar(o[r, 2 * half:2 * half + 2, par, :], s[r, :, h, :],
                                                   bv[r, c:c + 1], None, ALU.add)
                last.then_inc(o_out, 1)
            dve.wait_ge(w_in["bo"], 16)
            for t in range(TC):
                nc.vector.tensor_tensor(x[:, t, :], x[:, t, :], bo[:], ALU.add).then_inc(biased, 1)
            for t in range(TC):
                dve.wait_ge(o_mm, t + 1)
                dve.wait_ge(biased, t + 1)
                nc.vector.tensor_tensor(x[:, t, :], x[:, t, :], banks[t][:], ALU.add).then_inc(out, 1)

        @block.tensor
        def _(pe):
            pe.wait_ge(norm.done, TC)
            for c in range(KC):
                transpose_rows(nc, banks[c], xn, c, ident).then_inc(turned, 1)
            pe.wait_ge(turned_out, KC)
            pe.wait_ge(w_in["wl"], 16)
            product(nc, banks[4][:], [(wl[:, k, :], xnT[:, k, :]) for k in range(KC)]).then_inc(l_mm, 1)
            pe.wait_ge(w_in["wq"], 16)
            for c in range(KC):
                product(nc, banks[(5 + c) % 8][:], [(wq[:, k, c * P:(c + 1) * P], xnT[:, k, :]) for k in range(KC)]
                        ).then_inc(q_mm, 1)
            pe.wait_ge(l_out, 1)
            pe.wait_ge(q_out, KC)
            pe.wait_ge(w_in["wk"], 16)
            for c in range(KC):
                product(nc, banks[c][:], [(wk[:, c * P:(c + 1) * P], lT[:])]).then_inc(k_mm, 1)
            pe.wait_ge(w_in["wv"], 16)
            for t in range(TC):
                product(nc, banks[4 + t][:], [(lT[:, t * P:(t + 1) * P], wv[:])]).then_inc(v_mm, 1)
            pe.wait_ge(blk_ready, 1)
            pe.wait_ge(k_out, KC)
            for u in range(PAIRS):
                if u == 4:
                    pe.wait_ge(v_out, TC)
                for b in range(B):
                    last = product(nc, banks[u][:, b * LAT:(b + 1) * LAT],
                                   [(q_blk[:, u // 2, u % 2, b, :], kT[:, u // 2, b * LAT:(b + 1) * LAT])])
                last.then_inc(scored, 1)
            for u in range(PAIRS):
                pe.wait_ge(exp_done, u + 1)
                pe.wait_ge(prob_ready, u + 1)
                for t in range(TC):
                    last = nc.tensor.transpose(banks[u][:, t * P:(t + 1) * P],
                                               prob[:, u, 2 * t:2 * t + 2, :].rearrange("p b n -> p (b n)"), ident[:])
                last.then_inc(p_turned, 1)
            pe.wait_ge(pt_out, PAIRS)
            for n in range(4 * KC):
                c, half, par = n // 4, (n // 2) % 2, n % 2
                if n >= 8:
                    pe.wait_ge(o_out, n - 7)
                r = slice(par * LAT, (par + 1) * LAT)
                for j in range(2):
                    t = 2 * half + j
                    last = product(nc, banks[n % 8][:, j * 2 * P:(j + 1) * 2 * P],
                                   [(v[r, t, c * P:(c + 1) * P], pt[r, 2 * c:2 * c + 2, t, :])])
                last.then_inc(weighed, 1)
            pe.wait_ge(o_out, 4 * KC)
            pe.wait_ge(w_in["wo"], 16)
            for t in range(TC):
                product(nc, banks[t][:], [(oT[:, c, t * P:(t + 1) * P], wo[:, c, :]) for c in range(KC)]
                        ).then_inc(o_mm, 1)


def phase_rows(nc, dram, ident, x, y1, ew):
    NH, SC = KC, P ** -0.5
    with ExitStack() as ctx:
        sc = Scope(nc, ctx, "row")
        xn = sc.sb("xn", [P, TC, D])
        xnT = sc.sb("xnT", [P, KC, T])
        w, wo = sc.sb("w", [P, KC, 3 * D]), sc.sb("wo", [P, KC, D])
        bc = sc.sb("bc", [P, 3 * KC])
        bo, g, bb = sc.sb("bo", [P, D]), sc.sb("g", [P, D]), sc.sb("bb", [P, D])
        same = sc.sb("same", [P, LAT])
        qT, kT, v = sc.sb("qT", [P, NH, T]), sc.sb("kT", [P, NH, T]), sc.sb("v", [P, TC, D])
        cut = sc.sb("cut", [P, 2, T])
        N = NH * TC
        s8, d8, e8, p8 = (sc.sb(n, [P, N, B]) for n in ("s8", "d8", "e8", "p8"))
        nm8, sm8, iv8 = (sc.sb(n, [P, N]) for n in ("nm8", "sm8", "iv8"))
        full = sc.sb("full", [P, 2, TC, T])
        flat = w[:].rearrange("p k f -> p (k f)")
        pt = flat[:, 0:2 * TC * T].rearrange("p (i t f) -> p i t f", i=2, t=TC)
        r = flat[:, 2 * TC * T:].rearrange("p (t d) -> p t d", t=TC)
        oT = qT
        norm, norm1 = Norm(sc, "ln"), Norm(sc, "ln1")
        banks = [sc.ps(f"bank{i}", [P, T]) for i in range(8)]
        w_in, bc_in, wo_in, same_in = sc.sem("w_in"), sc.sem("bc_in"), sc.sem("wo_in"), sc.sem("same_in")
        bo_in, g_in, bb_in = sc.sem("bo_in"), sc.sem("g_in"), sc.sem("bb_in")
        turned, turned_out = sc.sem("turned"), sc.sem("turned_out")
        mm, q_out, k_out, v_out = (sc.sem(n) for n in ("mm", "q_out", "k_out", "v_out"))
        scored, cut_ready, picked, step = (sc.sem(n) for n in ("scored", "cut_ready", "picked", "step"))
        d_ready, e_ready, spread, p_turned, pt_out = (sc.sem(n) for n in ("d_ready", "e_ready", "spread", "p_turned",
                                                                          "pt_out"))
        weighed, o_out, biased, o_mm, r_ready = (sc.sem(n) for n in ("weighed", "o_out", "biased", "o_mm", "r_ready"))
        geared = sc.sem("geared")
        block = ctx.enter_context(nc.Block())
        by_batch = lambda a: a.rearrange("p (b n) -> p b n", b=B)
        same_all = same[:].unsqueeze(1).broadcast_to([P, B, LAT])

        @block.sync
        def _(sp):
            sp.dma_start(bc[:], dram["L1_ffn_in_proj_b"]).then_inc(bc_in, 16)
            sp.dma_start(same[:], dram["same_latent"]).then_inc(same_in, 16)
            sp.dma_start(w[:], dram["L1_ffn_in_proj_w"]).then_inc(w_in, 16)
            sp.dma_start(wo[:], dram["L1_ffn_out_proj_w"]).then_inc(wo_in, 16)
            sp.dma_start(bo[:], dram["L1_ffn_out_proj_b"].partition_broadcast(P)).then_inc(bo_in, 16)
            sp.dma_start(g[:], dram["L1_ffn_ln1_g"].partition_broadcast(P)).then_inc(g_in, 16)
            sp.dma_start(bb[:], dram["L1_ffn_ln1_b"].partition_broadcast(P)).then_inc(bb_in, 16)
            for half in range(2):
                ew.load_w1(sp, 0, half)

        @block.scalar
        def _(act):
            norm.scalar(nc, act)
            for c in range(KC):
                act.wait_ge(turned, c + 1)
                nc.scalar.activation(xnT[:, c, :], banks[c][:], ACT.Copy).then_inc(turned_out, 1)
            act.wait_ge(bc_in, 16)
            for h in range(NH):
                act.wait_ge(mm, h + 1)
                nc.scalar.activation(kT[:, h, :], banks[4 + h][:], ACT.Identity, bias=bc[:, KC + h:KC + h + 1]
                                     ).then_inc(k_out, 1)
            act.wait_ge(d_ready, 1)
            nc.scalar.activation(e8[:], d8[:], ACT.Exp).then_inc(e_ready, 1)
            for t in range(TC):
                act.wait_ge(mm, 2 * NH + t + 1)
                nc.scalar.activation(v[:, t, :], banks[4 + t][:], ACT.Copy).then_inc(v_out, 1)
            for h in range(NH):
                if h >= 2:
                    act.wait_ge(weighed, h - 1)
                for k in range(TC):
                    act.wait_ge(p_turned, TC * h + k + 1)
                    nc.scalar.activation(pt[:, h % 2, k, :], banks[k][:], ACT.Copy).then_inc(pt_out, 1)
                act.wait_ge(weighed, h + 1)
                nc.scalar.activation(oT[:, h, :], banks[4 + h % 2][:], ACT.Identity,
                                     bias=bc[:, 2 * KC + h:2 * KC + h + 1]).then_inc(o_out, 1)
            norm1.scalar(nc, act)

        @block.vector
        def _(dve):
            norm.vector(nc, dve, x, xn)
            dve.wait_ge(bc_in, 16)
            for h in range(NH):
                dve.wait_ge(mm, NH + h + 1)
                nc.vector.tensor_scalar(qT[:, h, :], banks[h][:], bc[:, h:h + 1], SC, ALU.add, ALU.mult
                                        ).then_inc(q_out, 1)
            dve.wait_ge(same_in, 16)
            for n in range(N):
                dve.wait_ge(scored, n + 1)
                nc.vector.tensor_tensor(by_batch(cut[:, n % 2, :]), by_batch(banks[n % 4][:]), same_all, ALU.mult
                                        ).then_inc(cut_ready, 1)
                dve.wait_ge(cut_ready, n + 1)
                nc.vector.reduce_sum(s8[:, n, :], by_batch(cut[:, n % 2, :]), AX.X).then_inc(picked, 1)
            dve.wait_ge(picked, N)
            wide = lambda a: a[:].unsqueeze(2).broadcast_to([P, N, B])
            nc.vector.reduce_max(nm8[:], s8[:], AX.X, negate=True).then_inc(step, 1)
            dve.wait_ge(step, 1)
            nc.vector.tensor_tensor(d8[:], s8[:], wide(nm8), ALU.add).then_inc(d_ready, 1)
            dve.wait_ge(e_ready, 1)
            nc.vector.reduce_sum(sm8[:], e8[:], AX.X).then_inc(step, 1)
            dve.wait_ge(step, 2)
            nc.vector.reciprocal(iv8[:], sm8[:]).then_inc(step, 1)
            dve.wait_ge(step, 3)
            nc.vector.tensor_tensor(p8[:], e8[:], wide(iv8), ALU.mult).then_inc(step, 1)
            dve.wait_ge(step, 4)
            for h in range(NH):
                if h >= 2:
                    dve.wait_ge(p_turned, TC * (h - 1))
                for t in range(TC):
                    nc.vector.tensor_tensor(by_batch(full[:, h % 2, t, :]),
                                            p8[:, h * TC + t, :].unsqueeze(2).broadcast_to([P, B, LAT]), same_all,
                                            ALU.mult).then_inc(spread, 1)
            dve.wait_ge(bo_in, 16)
            for t in range(TC):
                nc.vector.tensor_tensor(xn[:, t, :], xn[:, t, :], bo[:], ALU.add).then_inc(biased, 1)
            for t in range(TC):
                dve.wait_ge(o_mm, t + 1)
                dve.wait_ge(biased, t + 1)
                nc.vector.tensor_tensor(r[:, t, :], xn[:, t, :], banks[t][:], ALU.add).then_inc(r_ready, 1)
            dve.wait_ge(r_ready, TC)
            norm1.statistics(nc, dve, r)
            dve.wait_ge(g_in, 16)
            dve.wait_ge(bb_in, 16)
            for t in range(TC):
                norm1.gear(nc, r, t, g).then_inc(geared, 1)
            for t in range(TC):
                dve.wait_ge(geared, t + 1)
                norm1.finish(nc, y1[:, t, :], r, t, bb[:])

        @block.tensor
        def _(pe):
            pe.wait_ge(norm.done, TC)
            for c in range(KC):
                transpose_rows(nc, banks[c], xn, c, ident).then_inc(turned, 1)
            pe.wait_ge(turned_out, KC)
            pe.wait_ge(w_in, 16)
            for h in range(NH):
                o = D + h * P
                product(nc, banks[4 + h][:], [(w[:, k, o:o + P], xnT[:, k, :]) for k in range(KC)]).then_inc(mm, 1)
            for h in range(NH):
                o = h * P
                product(nc, banks[h][:], [(w[:, k, o:o + P], xnT[:, k, :]) for k in range(KC)]).then_inc(mm, 1)
            pe.wait_ge(k_out, NH)
            pe.wait_ge(q_out, NH)
            for n in range(N):
                h, t = n // TC, n % TC
                if n >= 4:
                    pe.wait_ge(cut_ready, n - 3)
                product(nc, banks[n % 4][:], [(qT[:, h, t * P:(t + 1) * P], kT[:, h, :])]).then_inc(scored, 1)
            for t in range(TC):
                product(nc, banks[4 + t][:], [(xnT[:, k, t * P:(t + 1) * P], w[:, k, 2 * D:3 * D]) for k in range(KC)]
                        ).then_inc(mm, 1)
            pe.wait_ge(cut_ready, N)
            for h in range(NH):
                pe.wait_ge(spread, TC * (h + 1))
                for k in range(TC):
                    if h:
                        pe.wait_ge(pt_out, TC * (h - 1) + k + 1)
                    for t in range(TC):
                        last = nc.tensor.transpose(banks[k][:, t * P:(t + 1) * P],
                                                   full[:, h % 2, t, k * P:(k + 1) * P], ident[:])
                    last.then_inc(p_turned, 1)
                pe.wait_ge(pt_out, TC * (h + 1))
                if h == 0:
                    pe.wait_ge(v_out, TC)
                if h >= 2:
                    pe.wait_ge(o_out, h - 1)
                product(nc, banks[4 + h % 2][:], [(v[:, k, h * P:(h + 1) * P], pt[:, h % 2, k, :])
                                                  for k in range(TC)]).then_inc(weighed, 1)
            pe.wait_ge(o_out, NH)
            pe.wait_ge(wo_in, 16)
            for t in range(TC):
                product(nc, banks[t][:], [(oT[:, h, t * P:(t + 1) * P], wo[:, h, :]) for h in range(NH)]
                        ).then_inc(o_mm, 1)


class ExpertWeights:

    def __init__(self, sc, dram):
        self.dram = dram
        self.w1 = [sc.sb(f"w1_{i}", [P, KC, FF]) for i in range(2)]
        self.w1_in = [sc.sem(f"w1_in{half}") for half in range(2)]

    def load_w1(self, sp, j, half):
        f = slice(half * FF // 2, (half + 1) * FF // 2)
        for i in range(2):
            sp.dma_start(self.w1[i][:, :, f], self.dram["L1_ffn_w1"][2 * j + i, :, :, f]).then_inc(self.w1_in[half], 16)


def phase_dispatch(nc, dram, ident, x, y1, ew, spare):
    with ExitStack() as ctx:
        sc = Scope(nc, ctx, "dsp")
        w1, w1_in = ew.w1, ew.w1_in
        w2 = [sc.sb(f"w2_{i}", [P, FC, D]) for i in range(2)]
        b1 = sc.sb("b1", [P, E0 // 2, FC, 2])
        b2 = sc.sb("b2", [P, E0 // 2, D])
        dT = sc.sb("dT", [P, KC, T])
        hotT = spare
        gate = sc.sb("gate", [P, TC])
        g, bb = sc.sb("g", [P, D]), sc.sb("bb", [P, D])
        w2_in = [sc.sem(f"w2_in{half}") for half in range(2)]
        g_in, bb_in = sc.sem("g_in"), sc.sem("bb_in")
        b1_in, b2_in = sc.sem("b1_in"), sc.sem("b2_in")
        W2 = dram["L1_ffn_w2"]

        def load_w2(sp, j, half):
            f = slice(half * FC // 2, (half + 1) * FC // 2)
            for i in range(2):
                sp.dma_start(w2[i][:, f, :], W2[2 * j + i, :, f, :]).then_inc(w2_in[half], 16)

        with ExitStack() as c1:
            s1 = Scope(nc, c1, "dsr")
            wg = s1.sb("wg", [P, KC, E0])
            hot = s1.sb("hot", [P, TC, T], F32R)
            yh, yl = s1.sb("yh", [P, TC, D], F32R), s1.sb("yl", [P, TC, D], F32R)
            earlier = s1.sb("earlier", [P, TC, E0])
            before, ones = s1.sb("before", [P, P]), s1.sb("ones", [P, P])
            slots = s1.sb("slots", [P, T])
            first = s1.sb("first", [P, TC, E0])
            cnt, cm, at = (s1.sb(n, [P, TC, E0]) for n in ("cnt", "cm", "at"))
            loc, pos, over, slot = (s1.sb(n, [P, TC]) for n in ("loc", "pos", "over", "slot"))
            rt = Route(s1, dram)
            banks = [s1.ps(f"bank{i}", [P, T]) for i in range(8)]
            c_in, ones_ready = s1.sem("c_in"), s1.sem("ones_ready")
            turned, turned_out, routed, counted = (s1.sem(n) for n in ("turned", "turned_out", "routed", "counted"))
            step, hot_ready, moved, moved_out = (s1.sem(n) for n in ("step", "hot_ready", "moved", "moved_out"))
            yh_ready, yl_ready, summed = s1.sem("yh_ready"), s1.sem("yl_ready"), s1.sem("summed")
            hot_turned, hot_out = s1.sem("hot_turned"), s1.sem("hot_out")
            block = c1.enter_context(nc.Block())

            @block.sync
            def _(sp):
                sp.dma_start(wg[:], dram["L1_ffn_wg"]).then_inc(c_in, 16)
                rt.sync(sp)
                sp.dma_start(before[:], dram["before"]).then_inc(c_in, 16)
                sp.dma_start(slots[:], dram["slots"].partition_broadcast(P)).then_inc(c_in, 16)
                sp.dma_start(first[:], dram["first_slot"].partition_broadcast(P)).then_inc(c_in, 16)
                sp.dma_start(b1[:], dram["L1_ffn_b1"]).then_inc(b1_in, 16)
                for i in range(2):
                    sp.dma_start(b2[i * CAP:(i + 1) * CAP],
                                 dram["L1_ffn_b2"].rearrange("(j r) d -> r j d", r=2)[i].partition_broadcast(CAP)
                                 ).then_inc(b2_in, 16)
                sp.dma_start(g[:], dram["L1_ffn_ln2_g"].partition_broadcast(P)).then_inc(g_in, 16)
                sp.dma_start(bb[:], dram["L1_ffn_ln2_b"].partition_broadcast(P)).then_inc(bb_in, 16)
                for half in range(2):
                    load_w2(sp, 0, half)

            @block.gpsimd
            def _(pool):
                nc.gpsimd.memset(ones[:], 1.0).then_inc(ones_ready, 1)
                nc.gpsimd.memset(earlier[:, 0, :], 0.0).then_inc(ones_ready, 1)
                pool.wait_ge(yh_ready, 1)
                nc.gpsimd.tensor_tensor(yl[:], y1[:], yh[:].bitcast(F32), ALU.subtract).then_inc(yl_ready, 1)

            @block.scalar
            def _(act):
                for c in range(KC):
                    act.wait_ge(turned, c + 1)
                    nc.scalar.activation(dT[:, c, :], banks[c][:], ACT.Copy).then_inc(turned_out, 1)
                nc.scalar.activation(yh[:], y1[:], ACT.Copy).then_inc(yh_ready, 1)
                rt.scalar(nc, act)
                for c in range(TC):
                    act.wait_ge(hot_turned, c + 1)
                    nc.scalar.activation(hotT[:, c, :], banks[c][:], ACT.Copy).then_inc(hot_out, 1)

            @block.vector
            def _(dve):
                dve.wait_ge(routed, 1)
                rt.vector(nc, dve, banks[4][:, 0:TC * E0].rearrange("p (t e) -> p t e", t=TC))
                n = [0]

                def step_(ins):
                    n[0] += 1
                    ins.then_inc(step, 1)
                    dve.wait_ge(step, n[0])

                dve.wait_ge(rt.done, 1)
                dve.wait_ge(ones_ready, 2)
                for t in range(1, TC):
                    step_(nc.vector.tensor_tensor(earlier[:, t, :], earlier[:, t - 1, :], rt.mask[:, t - 1, :],
                                                  ALU.add))
                dve.sem_inc(summed, 1)
                dve.wait_ge(c_in, 64)
                dve.wait_ge(counted, 1)
                step_(nc.vector.tensor_copy(cnt[:], banks[5][:, 0:TC * E0].rearrange("p (t e) -> p t e", t=TC)))
                step_(nc.vector.tensor_tensor(cm[:], cnt[:], rt.mask[:], ALU.mult))
                step_(nc.vector.reduce_sum(loc[:], cm[:], AX.X))
                step_(nc.vector.tensor_tensor(at[:], first[:], rt.mask[:], ALU.mult))
                step_(nc.vector.reduce_sum(pos[:], at[:], AX.X))
                step_(nc.vector.tensor_scalar(over[:], loc[:], float(CAP), float(4 * T), ALU.is_ge, ALU.mult))
                step_(nc.vector.tensor_tensor(pos[:], pos[:], loc[:], ALU.add))
                step_(nc.vector.tensor_tensor(slot[:], pos[:], over[:], ALU.add))
                step_(nc.vector.tensor_copy(gate[:], rt.gate[:]))
                for t in range(TC):
                    nc.vector.tensor_scalar(hot[:, t, :], slots[:], slot[:, t:t + 1], None, ALU.is_equal
                                            ).then_inc(hot_ready, 1)
                for c in range(KC):
                    dve.wait_ge(moved, c + 1)
                    nc.vector.tensor_copy(dT[:, c, :], banks[4 + c][:]).then_inc(moved_out, 1)

            @block.tensor
            def _(pe):
                for c in range(KC):
                    transpose_rows(nc, banks[c], y1, c, ident).then_inc(turned, 1)
                pe.wait_ge(turned_out, KC)
                pe.wait_ge(c_in, 64)
                for t in range(TC):
                    last = product(nc, banks[4][:, t * E0:(t + 1) * E0],
                                   [(dT[:, k, t * P:(t + 1) * P], wg[:, k, :]) for k in range(KC)])
                last.then_inc(routed, 1)
                pe.wait_ge(rt.done, 1)
                pe.wait_ge(ones_ready, 2)
                pe.wait_ge(summed, 1)
                flat = lambda a: a[:].rearrange("p t e -> p (t e)")
                product(nc, banks[5][:, 0:TC * E0], [(before[:], flat(rt.mask)), (ones[:], flat(earlier))]
                        ).then_inc(counted, 1)
                pe.wait_ge(hot_ready, TC)
                pe.wait_ge(yl_ready, 1)
                for c in range(KC):
                    f = slice(c * P, (c + 1) * P)
                    product(nc, banks[4 + c][:], [(y[:, t, f], hot[:, t, :]) for y in (yh, yl) for t in range(TC)]
                            ).then_inc(moved, 1)
                for c in range(TC):
                    for t in range(TC):
                        last = nc.tensor.transpose(banks[c][:, t * P:(t + 1) * P],
                                                   hot[:, t, c * P:(c + 1) * P].bitcast(F32), ident[:])
                    last.then_inc(hot_turned, 1)

        with ExitStack() as c2:
            s2 = Scope(nc, c2, "dse")
            ds_ = s2.sb("ds", [P, KC, P])
            hr = s2.sb("hr", [P, FF])
            hT = s2.sb("hT", [P, FC, P])
            ys = s2.sb("ys", [P, E0 // 2, D])
            mixed = w1[0][:, 0, :].rearrange("p (t d) -> p t d", t=TC)
            norm2 = Norm(s2, "ln2")
            back, r_ready, geared, out = (s2.sem(n) for n in ("back", "r_ready", "geared", "out"))
            NB = FF // 512
            hb = [s2.ps(f"hb{i}", [P, 512]) for i in range(NB)]
            tb = [s2.ps(f"tb{i}", [P, 512]) for i in range(3)]
            yb = s2.ps("yb", [P, D])
            ds_ready, h_mm, h_out = s2.sem("ds_ready"), s2.sem("h_mm"), s2.sem("h_out")
            h_turned, hT_out, y_mm, y_out = (s2.sem(n) for n in ("h_turned", "hT_out", "y_mm", "y_out"))
            both = [slice(i * CAP, (i + 1) * CAP) for i in range(2)]
            block = c2.enter_context(nc.Block())

            @block.sync
            def _(sp):
                with sp.Fori(0, E0 // 2 - 1) as j:
                    for half in range(2):
                        sp.wait_ge(h_mm, NB * j + NB // 2 * (half + 1))
                        ew.load_w1(sp, j + 1, half)
                    for half in range(2):
                        sp.wait_ge(y_mm, 2 * j + half + 1)
                        load_w2(sp, j + 1, half)

            @block.scalar
            def _(act):
                with act.Fori(0, E0 // 2) as j:
                    for q in range(NB):
                        act.wait_ge(h_mm, NB * j + q + 1)
                        nc.scalar.activation(hr[:, q * 512:(q + 1) * 512], hb[q][:], ACT.Copy).then_inc(h_out, 1)
                norm2.scalar(nc, act)

            @block.vector
            def _(dve):
                dve.sem_inc(y_out, 1)
                dve.sem_inc(hT_out, 1)
                dve.wait_ge(b1_in, 16)
                dve.wait_ge(b2_in, 32)
                with dve.Fori(0, E0 // 2) as j:
                    nc.vector.tensor_copy(ds_[:], dT[:, :, bass.ds(P * j, P)]).then_inc(ds_ready, 1)
                    for q in range(NB):
                        dve.wait_ge(h_turned, NB * j + q + 1)
                        fs = slice(4 * q, 4 * q + 4)
                        nc.vector.tensor_tensor(
                            hT[:, fs, :].rearrange("p f (i c) -> p f i c", i=2),
                            tb[q % 3][:].rearrange("p (f i c) -> p f i c", f=4, i=2),
                            b1[:, bass.ds(j, 1), fs, :].rearrange("p o f i -> p (o f) i").unsqueeze(3)
                            .broadcast_to([P, 4, 2, CAP]), ALU.add).then_inc(hT_out, 1)
                    dve.wait_ge(y_mm, 2 * j + 2)
                    nc.vector.tensor_tensor(ys[:, bass.ds(j, 1), :], yb[:].unsqueeze(1), b2[:, bass.ds(j, 1), :],
                                            ALU.add).then_inc(y_out, 1)
                dve.wait_ge(g_in, 16)
                dve.wait_ge(bb_in, 16)
                for t in range(TC):
                    nc.vector.tensor_tensor(x[:, t, :], x[:, t, :], bb[:], ALU.add).then_inc(geared, 1)
                for t in range(TC):
                    dve.wait_ge(back, t + 1)
                    nc.vector.scalar_tensor_tensor(mixed[:, t, :], hb[t][:], gate[:, t:t + 1], y1[:, t, :],
                                                   ALU.mult, ALU.add).then_inc(r_ready, 1)
                dve.wait_ge(r_ready, TC)
                norm2.statistics(nc, dve, mixed)
                dve.wait_ge(geared, TC)
                for t in range(TC):
                    norm2.gear(nc, mixed, t, g).then_inc(geared, 1)
                for t in range(TC):
                    dve.wait_ge(geared, TC + t + 1)
                    norm2.finish(nc, x[:, t, :], mixed, t, x[:, t, :]).then_inc(out, 1)

            @block.tensor
            def _(pe):
                def turn(j, last_turn):
                    pe.wait_ge(ds_ready, j + 1)
                    for q in range(NB):
                        if q % (NB // 2) == 0:
                            pe.wait_ge(w1_in[q // (NB // 2)], 32 * j + 32)
                        for k in range(KC):
                            for r, w in zip(both, w1):
                                last = nc.tensor.matmul(hb[q][r, :], ds_[:, k, r], w[:, k, q * 512:(q + 1) * 512],
                                                        start=(k == 0), stop=(k == KC - 1))
                        last.then_inc(h_mm, 1)
                    for q in range(NB):
                        pe.wait_ge(h_out, NB * j + q + 1)
                        pe.wait_ge(hT_out, NB * j + max(0, q - 3) + 1 + (1 if q == 3 else 0))
                        for c in range(4):
                            f = 4 * q + c
                            last = nc.tensor.transpose(tb[q % 3][:, c * P:(c + 1) * P], hr[:, f * P:(f + 1) * P],
                                                       ident[:])
                        last.then_inc(h_turned, 1)
                    pe.wait_ge(y_out, j + 1)
                    if last_turn:
                        for c in range(TC - 1):
                            send_back(c)
                    for f in range(FC):
                        if f % (FC // 2) == 0:
                            pe.wait_ge(w2_in[f // (FC // 2)], 32 * j + 32)
                        if f % 4 == 0:
                            pe.wait_ge(hT_out, NB * j + f // 4 + 2)
                        for r, w in zip(both, w2):
                            last = nc.tensor.matmul(yb[r, :], hT[:, f, r], w[:, f, :], start=(f == 0),
                                                    stop=(f == FC - 1))
                        if f % (FC // 2) == FC // 2 - 1:
                            last.then_inc(y_mm, 1)

                def send_back(c):
                    for t in range(TC):
                        last = nc.tensor.matmul(hb[t][:], hotT[:, c, t * P:(t + 1) * P], ys[:, c, :], start=(c == 0),
                                                stop=(c == TC - 1))
                        if c == TC - 1:
                            last.then_inc(back, 1)

                with pe.Fori(0, E0 // 2 - 1) as j:
                    turn(j, False)
                turn(E0 // 2 - 1, True)
                pe.wait_ge(y_out, E0 // 2 + 1)
                send_back(TC - 1)


def phase_block(nc, dram, ident, x, spare):
    with ExitStack() as ctx:
        y1 = ctx.enter_context(nc.sbuf_tensor("y1", [P, TC, D], F32))
        ew = ExpertWeights(Scope(nc, ctx, "exp"), dram)
        phase_rows(nc, dram, ident, x, y1, ew)
        phase_dispatch(nc, dram, ident, x, y1, ew, spare)


def rest(nc, dram, ident, x, spare):
    with ExitStack() as ctx:
        ahead = ContextAhead(Scope(nc, ctx, "ahead"), dram)
        phase_scan(nc, dram, ident, x, ahead)
        phase_experts(nc, dram, ident, x)
        phase_context(nc, dram, ident, x, ahead)
    phase_latent(nc, dram, ident, x)
    phase_block(nc, dram, ident, x, spare)


def lay_rest(n, put, rows, cols):
    import numpy as np
    ctx = n["ctx_1024"]
    put["ctxR"] = ctx[:, :P * (NCH - 1)].reshape(B, NCH - 1, P, D).transpose(0, 2, 1, 3)
    put["ctxL"] = ctx[:, P * (NCH - 1):]
    put["rank"] = np.tile(np.arange(E0, 0, -1, dtype=np.float32), (TC, 1))
    put["L0_attn_W_qkva"] = rows(n["L0_attn_W_qkva"].T)
    put["L0_attn_gamma"] = cols(n["L0_attn_gamma"])
    put["L0_ffn_router_w"] = rows(n["L0_ffn_router_w"])
    put["L0_ffn_router_b"] = n["L0_ffn_router_b"]
    put["L0_ffn_expert_b"] = n["L0_ffn_expert_b"]
    put["L0_ffn_expert_w"] = n["L0_ffn_expert_w"].reshape(E0, KC, P, D).transpose(0, 2, 1, 3)
    put["L1_xattn_Wq"] = rows(n["L1_xattn_Wq"].T)
    put["L1_xattn_Wk"] = rows(n["L1_xattn_Wk"])
    put["L1_xattn_Wv"] = rows(n["L1_xattn_Wv"].T)
    put["L1_xattn_Wo"] = rows(n["L1_xattn_Wo"].T)
    put["L1_xattn_bq"] = cols(n["L1_xattn_bq"])
    put["L1_xattn_bv"] = cols(n["L1_xattn_bv"])
    put["L1_xattn_bo"] = n["L1_xattn_bo"]
    put["L1_attn_Wq"] = rows(n["L1_attn_Wq"])
    put["L1_attn_Wl"] = rows(n["L1_attn_Wl"])
    put["L1_attn_Wk"] = n["L1_attn_Wk"]
    put["L1_attn_Wv"] = n["L1_attn_Wv"]
    put["L1_attn_Wo"] = rows(n["L1_attn_Wo"])
    for k in ("bq", "bl", "bk", "bv"):
        put[f"L1_attn_{k}"] = cols(n[f"L1_attn_{k}"])
    put["L1_attn_bo"] = n["L1_attn_bo"]
    put["L1_ffn_in_proj_w"] = rows(n["L1_ffn_in_proj_w"].T)
    put["L1_ffn_in_proj_b"] = cols(n["L1_ffn_in_proj_b"])
    put["L1_ffn_in_proj_bv"] = n["L1_ffn_in_proj_b"][2 * D:]
    put["L1_ffn_out_proj_w"] = rows(n["L1_ffn_out_proj_w"].T)
    for k in ("out_proj_b", "ln1_g", "ln1_b", "ln2_g", "ln2_b"):
        put[f"L1_ffn_{k}"] = n[f"L1_ffn_{k}"]
    put["L1_ffn_wg"] = rows(n["L1_ffn_wg"])
    put["L1_ffn_w1"] = n["L1_ffn_w1"].reshape(E0, KC, P, FF).transpose(0, 2, 1, 3)
    put["L1_ffn_w2"] = n["L1_ffn_w2"].reshape(E0, FC, P, D).transpose(0, 2, 1, 3)
    put["L1_ffn_b1"] = n["L1_ffn_b1"].reshape(E0 // 2, 2, FC, P).transpose(3, 0, 2, 1)
    put["L1_ffn_b2"] = n["L1_ffn_b2"]
    at = np.arange(T)
    put["same_latent"] = (np.arange(LAT)[None, :] == (np.arange(P) % LAT)[:, None]).astype(np.float32)
    put["before"] = (np.arange(P)[:, None] < np.arange(P)[None, :]).astype(np.float32)
    put["slots"] = at.astype(np.float32)
    put["first_slot"] = np.tile(np.arange(0, T, CAP, dtype=np.float32), (TC, 1))


def store_rows(nc, dst, rows):
    with ExitStack() as ctx:
        sc = Scope(nc, ctx, "sto")
        stored = sc.sem("stored")
        block = ctx.enter_context(nc.Block())

        @block.sync
        def _(sp):
            sp.dma_start(dst.rearrange("(t p) d -> p t d", p=P), rows[:]).then_inc(stored, 16)
            sp.wait_ge(stored, 16)


def build(nc, dram, out):
    with ExitStack() as whole:
        keep = Scope(nc, whole, "all")
        ident = keep.sb("ident", [P, P])
        oT = keep.sb("oT", [P, KC, T])
        res = {"ident": ident, "oT": oT}
        with ExitStack() as attn:
            at = Scope(nc, attn, "crossin")
            res["qT"] = at.sb("qT", [P, KC, T])
            res["w_hi"] = at.sb("w_hi", [P, 2, KC, D], F32R)
            res["w_lo"] = at.sb("w_lo", [P, 2, KC, D], F32R)
            res["q_blk_hi"] = at.sb("q_blk_hi", [P, KC, 2, P], F32R)
            res["q_blk_lo"] = at.sb("q_blk_lo", [P, KC, 2, P], F32R)
            res["bk"] = at.sb("bk", [P, KC])
            res["ct_hi"] = at.sb("ct_hi", [P, KC, KPAD], F32R)
            res["ct_lo"] = at.sb("ct_lo", [P, KC, KPAD], F32R)
            phase_queries(nc, dram, res)
            phase_cross(nc, dram, res)
        x = res["x"] = keep.sb("x", [P, TC, D])
        phase_cross_out(nc, dram, res)
        rest(nc, dram, ident, x, oT)
        store_rows(nc, out, x)


def kernel(**inputs):
    import numpy as np
    import concourse.bacc as bacc
    from concourse.bass_utils import run_bass_kernel_spmd

    arrays = {}

    def rows(w):
        k, n = w.shape
        return w.reshape(k // P, P, n).transpose(1, 0, 2)

    def cols(v):
        return v.reshape(-1, P).T

    n = {k: np.asarray(v) for k, v in inputs.items()}
    put = dict(x=n["x"].reshape(T, D))
    ctxT = np.zeros((B, P, KC, KPAD), n["ctx_1024"].dtype)
    ctxT[..., :KEYS] = n["ctx_1024"].transpose(0, 2, 1).reshape(B, KC, P, KEYS).transpose(0, 2, 1, 3)
    put["ctxT"] = ctxT
    for k in ("L0_xattn_Wq", "L0_xattn_Wk", "L0_xattn_Wv", "L0_xattn_Wo"):
        put[k] = rows(n[k].T)
    for k in ("L0_xattn_bq", "L0_xattn_bk", "L0_xattn_bv"):
        put[k] = cols(n[k])
    put["L0_xattn_bo"] = n["L0_xattn_bo"]
    lay_rest(n, put, rows, cols)

    nc = bacc.Bacc("TRN2", target_bir_lowering=False, num_devices=1)
    dram = {}
    for name, a in put.items():
        a = np.ascontiguousarray(a)
        arrays[f"in_{name}"] = a
        dram[name] = nc.dram_tensor(f"in_{name}", a.shape, mybir.dt.from_np(a.dtype), kind="ExternalInput").ap()
    out = nc.dram_tensor("out_0", (T, D), F32, kind="ExternalOutput").ap()
    build(nc, dram, out)
    r = run_bass_kernel_spmd(nc, [arrays], core_ids=[0])
    return r.results[0]["out_0"].reshape(B, LAT, D)
```
